# Optimizing a Trainium2 kernel written in Bass

```python
import numpy as np
import jax
import jax.numpy as jnp

def _softmax(x, axis=-1):
    return jax.nn.softmax(x, axis=axis)

def _gelu(x):
    return jax.nn.gelu(x, approximate=True)

def _silu(x):
    return jax.nn.silu(x)

def _sigmoid(x):
    return jax.nn.sigmoid(x)

def _layernorm(x, axis=-1, eps=1e-05):
    m = jnp.mean(x, axis=axis, keepdims=True)
    v = jnp.var(x, axis=axis, keepdims=True)
    return (x - m) / jnp.sqrt(v + eps)

def _scatter_add(tgt, idx, src, axis=0):
    return tgt.at[idx].add(src)

def _segment_sum(src, seg, n):
    return jax.ops.segment_sum(src, seg, n)
kernel_name = 'mk_hybrid_d4_jaxref_r8_8521d3'

def setup_inputs(seed: int=0):
    np.random.seed(seed)
    _w = jnp.asarray

    def _L0_attn_a_setup():
        import jax, jax.numpy as jnp
        import numpy as np
        EPS = 1e-08

        def rms_norm_multihead(x, weight):
            x32 = x.astype(jnp.float32)
            normed = x32 * jax.lax.rsqrt(jnp.mean(x32 * x32, axis=-1, keepdims=True) + EPS)
            return normed.astype(x.dtype) * weight
        key = jax.random.key(seed)
        k0, k1, k2 = jax.random.split(key, 3)
        B, L, D, H = (2, 128, 128, 16)
        d = D // H
        X = jax.random.normal(k0, (B, L, D), dtype=jnp.float32)
        Wq = jax.random.normal(k1, (D, D), dtype=jnp.float32) * 0.02
        Wv = jax.random.normal(k2, (D, D), dtype=jnp.float32) * 0.02
        q_norm_w = jnp.ones((H, d), dtype=jnp.float32)
        v_norm_w = jnp.ones((H, d), dtype=jnp.float32)
        return {'X': X, 'Wq': Wq, 'Wv': Wv, 'q_norm_w': q_norm_w, 'v_norm_w': v_norm_w}
    _L0_attn_a_in = _L0_attn_a_setup()

    def _L0_attn_b_setup():
        import jax, jax.numpy as jnp
        import numpy as np
        B, S, D = (2, 256, 128)
        H = 16
        DK = 128
        DV = 128
        EPS = 1e-05
        key = jax.random.key(seed)
        k1, k2, k3, k4 = jax.random.split(key, 4)
        x = jax.random.normal(k1, (B, S, D), dtype=jnp.float32)
        Wq = jax.random.normal(k2, (DK, D), dtype=jnp.float32) * 0.02
        Wk = jax.random.normal(k3, (DK, D), dtype=jnp.float32) * 0.02
        Wv = jax.random.normal(k4, (DV, D), dtype=jnp.float32) * 0.02
        return {'x': x, 'Wq': Wq, 'Wk': Wk, 'Wv': Wv}
    _L0_attn_b_in = _L0_attn_b_setup()

    def _L0_ffn_setup():
        import jax, jax.numpy as jnp
        import numpy as np
        B, S, H, E, K, I = (4, 256, 128, 8, 2, 512)
        GATE_EPS = 1e-06
        LN_EPS = 1e-05
        key = jax.random.key(seed)
        k0, k1, k2, k3 = jax.random.split(key, 4)
        x = jax.random.normal(k0, (B, S, H), jnp.float32)
        gate_w = jax.random.normal(k1, (E, H), jnp.float32) * np.float32(np.sqrt(2.0 / (H + E)))
        expert_bias = jnp.zeros((E,), jnp.float32)
        w_up = jax.random.normal(k2, (E, I, H), jnp.float32) * np.float32(np.sqrt(2.0 / (H + I)))
        w_down = jax.random.normal(k3, (E, H, I), jnp.float32) * np.float32(np.sqrt(2.0 / (H + I)))
        return {'x': x, 'gate_w': gate_w, 'expert_bias': expert_bias, 'w_up': w_up, 'w_down': w_down}
    _L0_ffn_in = _L0_ffn_setup()

    def _L1_attn_a_setup():
        import jax, jax.numpy as jnp
        import numpy as np
        D_MODEL = 128
        N_HEADS = 16
        HEAD_DIM = D_MODEL // N_HEADS
        SEQ = 256
        BATCH = 2
        ROPE_BASE = 10000.0

        def _rotary_cache(head_dim, seq_len, base=ROPE_BASE):
            pos = jnp.arange(seq_len, dtype=jnp.float32)
            inv_freq = 1.0 / base ** (jnp.arange(0, head_dim, 2, dtype=jnp.float32) / head_dim)
            freqs = jnp.einsum('i,j->ij', pos, inv_freq)
            cos = jnp.repeat(jnp.cos(freqs), 2, axis=1)
            sin = jnp.repeat(jnp.sin(freqs), 2, axis=1)
            return (cos, sin)

        def _rotate_every_two(x):
            x1 = x[..., ::2]
            x2 = x[..., 1::2]
            return jnp.stack((-x2, x1), axis=-1).reshape(x.shape)

        def _apply_rotary(x, cos, sin):
            return x * cos + _rotate_every_two(x) * sin
        key = jax.random.key(seed)
        k1, k2, k3 = jax.random.split(key, 3)
        s = 1.0 / np.sqrt(D_MODEL)
        x = jax.random.normal(k1, (SEQ, BATCH, D_MODEL), dtype=jnp.float32)
        Wqkv = jax.random.normal(k2, (D_MODEL, 3 * D_MODEL), dtype=jnp.float32) * s
        bqkv = jnp.zeros((3 * D_MODEL,), dtype=jnp.float32)
        Wout = jax.random.normal(k3, (D_MODEL, D_MODEL), dtype=jnp.float32) * s
        bout = jnp.zeros((D_MODEL,), dtype=jnp.float32)
        return {'x': x, 'Wqkv': Wqkv, 'bqkv': bqkv, 'Wout': Wout, 'bout': bout}
    _L1_attn_a_in = _L1_attn_a_setup()

    def _L1_attn_b_setup():
        import math
        import jax, jax.numpy as jnp
        import numpy as np
        B, T, C, H = (4, 256, 128, 128)
        key = jax.random.key(seed)
        kx, kk, kq, kv = jax.random.split(key, 4)
        s = 1.0 / math.sqrt(C)
        return {'x': jax.random.normal(kx, (B, T, C), dtype=jnp.float32), 'Wk': jax.random.uniform(kk, (C, H), dtype=jnp.float32, minval=-s, maxval=s), 'Wq': jax.random.uniform(kq, (C, H), dtype=jnp.float32, minval=-s, maxval=s), 'Wv': jax.random.uniform(kv, (C, H), dtype=jnp.float32, minval=-s, maxval=s)}
    _L1_attn_b_in = _L1_attn_b_setup()

    def _L1_ffn_setup():
        import jax, jax.numpy as jnp
        import numpy as np
        D_MODEL = 128
        D_HIDDEN = 512
        N_EXPERTS = 8
        B, S = (2, 256)
        key = jax.random.key(seed)
        ks = jax.random.split(key, 4)
        sd = 1.0 / np.sqrt(D_MODEL)
        sh = 1.0 / np.sqrt(D_HIDDEN)
        return {'x': jax.random.normal(ks[0], (B, S, D_MODEL), dtype=jnp.float32), 'Wg': jax.random.normal(ks[1], (D_MODEL, N_EXPERTS), dtype=jnp.float32) * sd, 'bg': jnp.zeros((N_EXPERTS,), dtype=jnp.float32), 'W1': jax.random.normal(ks[2], (N_EXPERTS, D_MODEL, D_HIDDEN), dtype=jnp.float32) * sd, 'b1': jnp.zeros((N_EXPERTS, D_HIDDEN), dtype=jnp.float32), 'W2': jax.random.normal(ks[3], (N_EXPERTS, D_HIDDEN, D_MODEL), dtype=jnp.float32) * sh, 'b2': jnp.zeros((N_EXPERTS, D_MODEL), dtype=jnp.float32)}
    _L1_ffn_in = _L1_ffn_setup()

    def _L2_attn_a_setup():
        import jax, jax.numpy as jnp
        import numpy as np
        D_MODEL = 128
        N_HEADS = 16
        D_K = D_MODEL // N_HEADS
        THETA = 10000.0
        EPS = 1e-08

        def _apply_rope(t):
            s = t.shape[-2]
            pos = jnp.arange(s, dtype=jnp.float32)
            kidx = jnp.arange(D_K // 2, dtype=jnp.float32)
            ang = pos[:, None] / THETA ** (2.0 * kidx / D_K)
            cos, sin = (jnp.cos(ang), jnp.sin(ang))
            x1 = t[..., 0::2]
            x2 = t[..., 1::2]
            r1 = cos * x1 - sin * x2
            r2 = sin * x1 + cos * x2
            return jnp.stack([r1, r2], axis=-1).reshape(t.shape)

        def _my_softmax(x, axis):
            m = jnp.max(x, axis=axis, keepdims=True)
            e = jnp.exp(x - m)
            return e / (jnp.sum(e, axis=axis, keepdims=True) + EPS)
        key = jax.random.key(seed)
        ks = jax.random.split(key, 9)
        B, S = (4, 256)
        x = jax.random.normal(ks[0], (B, S, D_MODEL), dtype=jnp.float32)
        scale = 0.02
        Wq = jax.random.normal(ks[1], (D_MODEL, D_MODEL), dtype=jnp.float32) * scale
        Wk = jax.random.normal(ks[2], (D_MODEL, D_MODEL), dtype=jnp.float32) * scale
        Wv = jax.random.normal(ks[3], (D_MODEL, D_MODEL), dtype=jnp.float32) * scale
        Wo = jax.random.normal(ks[4], (D_MODEL, D_MODEL), dtype=jnp.float32) * scale
        bq = jax.random.normal(ks[5], (D_MODEL,), dtype=jnp.float32) * scale
        bk = jax.random.normal(ks[6], (D_MODEL,), dtype=jnp.float32) * scale
        bv = jax.random.normal(ks[7], (D_MODEL,), dtype=jnp.float32) * scale
        bo = jax.random.normal(ks[8], (D_MODEL,), dtype=jnp.float32) * scale
        return {'x': x, 'Wq': Wq, 'bq': bq, 'Wk': Wk, 'bk': bk, 'Wv': Wv, 'bv': bv, 'Wo': Wo, 'bo': bo}
    _L2_attn_a_in = _L2_attn_a_setup()

    def _L2_attn_b_setup():
        import jax, jax.numpy as jnp
        import numpy as np
        B, T, D, H = (4, 256, 128, 16)
        HD = D // H
        EPS = 1e-05
        NEG = 10000000000.0
        key = jax.random.key(seed)
        k1, k2, k3 = jax.random.split(key, 3)
        return {'target': jax.random.normal(k1, (B, T, D), dtype=jnp.float32), 'w_qkv': jax.random.normal(k2, (D, 3 * D), dtype=jnp.float32) * 0.02, 'w_proj': jax.random.normal(k3, (D, D), dtype=jnp.float32) * (0.02 / np.sqrt(24.0)), 'b_proj': jnp.zeros((D,), dtype=jnp.float32), 'ln_gamma': jnp.ones((D,), dtype=jnp.float32), 'ln_beta': jnp.zeros((D,), dtype=jnp.float32)}
    _L2_attn_b_in = _L2_attn_b_setup()

    def _L2_ffn_setup():
        import jax, jax.numpy as jnp
        import numpy as np
        BLOCK = 16
        _GRID = jnp.array([0.0, 0.5, 1.0, 1.5, 2.0, 3.0, 4.0, 6.0], dtype=jnp.float32)
        _MID = jnp.array([0.25, 0.75, 1.25, 1.75, 2.5, 3.5, 5.0], dtype=jnp.float32)

        def fp4_quant_dequant(x):
            shape = x.shape
            xb = x.reshape(shape[:-1] + (shape[-1] // BLOCK, BLOCK))
            scale = jnp.max(jnp.abs(xb), axis=-1, keepdims=True) / 6.0
            scale = jnp.maximum(scale, jnp.float32(1e-12))
            xn = xb / scale
            idx = jnp.searchsorted(_MID, jnp.abs(xn))
            q = _GRID[idx] * jnp.sign(xn) * scale
            return q.reshape(shape)

        def fp4_linear(x, w):
            xq = fp4_quant_dequant(x)
            wq = fp4_quant_dequant(w)
            return jnp.einsum('bsk,nk->bsn', xq, wq)
        key = jax.random.key(seed)
        k1, k2, k3, k4 = jax.random.split(key, 4)
        H, I = (128, 352)
        x = jax.random.normal(k1, (4, 512, H), dtype=jnp.float32)
        w_gate = jax.random.normal(k2, (I, H), dtype=jnp.float32) * 0.02
        w_up = jax.random.normal(k3, (I, H), dtype=jnp.float32) * 0.02
        w_down = jax.random.normal(k4, (H, I), dtype=jnp.float32) * 0.02
        return {'x': x, 'w_gate': w_gate, 'w_up': w_up, 'w_down': w_down}
    _L2_ffn_in = _L2_ffn_setup()

    def _L3_attn_a_setup():
        import jax, jax.numpy as jnp
        import numpy as np
        import math
        NUM_HEADS = 16
        ROPE_THETA = 10000.0

        def _rope(x, pos):
            d_k = x.shape[-1]
            inv_freq = 1.0 / ROPE_THETA ** (jnp.arange(0, d_k, 2, dtype=jnp.float32) / d_k)
            ang = pos[:, None].astype(jnp.float32) * inv_freq[None, :]
            cos, sin = (jnp.cos(ang), jnp.sin(ang))
            x1, x2 = (x[..., 0::2], x[..., 1::2])
            r1 = x1 * cos - x2 * sin
            r2 = x1 * sin + x2 * cos
            return jnp.stack([r1, r2], axis=-1).reshape(x.shape)
        key = jax.random.key(seed)
        ks = jax.random.split(key, 5)
        B, S, D = (4, 256, 128)
        return {'x': jax.random.normal(ks[0], (B, S, D), dtype=jnp.float32), 'qkv_w': jax.random.normal(ks[1], (3 * D, D), dtype=jnp.float32) * (1.0 / math.sqrt(D)), 'qkv_b': jax.random.normal(ks[2], (3 * D,), dtype=jnp.float32) * 0.02, 'proj_w': jax.random.normal(ks[3], (D, D), dtype=jnp.float32) * (1.0 / math.sqrt(D)), 'proj_b': jax.random.normal(ks[4], (D,), dtype=jnp.float32) * 0.02}
    _L3_attn_a_in = _L3_attn_a_setup()

    def _L3_attn_b_setup():
        import jax, jax.numpy as jnp
        import numpy as np
        import math
        B, S, D = (4, 256, 128)
        H, DEG, DH, BUS, SLOTS = (8, 4, 32, 128, 64)
        EPS = 1.1920929e-07

        def _rms(x, w):
            return x * jax.lax.rsqrt(jnp.mean(x * x, axis=-1, keepdims=True) + EPS) * w
        key = jax.random.key(seed)
        ks = jax.random.split(key, 20)
        g = lambda k, shape, s=0.02: jax.random.normal(k, shape, jnp.float32) * s
        return {'x': jax.random.normal(ks[0], (B, S, D), jnp.float32), 'w_norm_in': jnp.ones((D,), jnp.float32), 'w_norm_out': jnp.ones((D,), jnp.float32), 'router_w1': g(ks[1], (D, D // 2)), 'router_w2': g(ks[2], (D // 2, 3)), 'router_b2': jnp.full((3,), 0.5, jnp.float32), 'ttt_w1': g(ks[3], (D, D // 4)), 'ttt_b1': jnp.zeros((D // 4,), jnp.float32), 'ttt_w2': g(ks[4], (D // 4, H * DEG)), 'ttt_b2': jnp.zeros((H * DEG,), jnp.float32), 'lambdas': jnp.array([0.9995, 0.9995, 0.997, 0.997, 0.995, 0.995, 0.97, 0.95], jnp.float32), 'slr_wq1': g(ks[5], (D, DH)), 'slr_wq2': g(ks[6], (D, DH)), 'slr_wk1': g(ks[7], (D, DH)), 'slr_wk2': g(ks[8], (D, DH)), 'slr_wv': g(ks[9], (D, DH)), 'slr_wo': g(ks[10], (DH, D)), 'slr_lam': jnp.array(0.5, jnp.float32), 'landmarks': g(ks[11], (SLOTS, D), 0.5), 'mix_w': g(ks[12], (2 * D, D)), 'bus_compress': g(ks[13], (D, BUS)), 'bus_expand': g(ks[14], (BUS, D)), 'bus_publish': g(ks[15], (BUS, BUS))}
    _L3_attn_b_in = _L3_attn_b_setup()

    def _L3_ffn_setup():
        import jax, jax.numpy as jnp
        import numpy as np
        BLOCK = 16
        _GRID = jnp.array([0.0, 0.5, 1.0, 1.5, 2.0, 3.0, 4.0, 6.0], dtype=jnp.float32)
        _MID = jnp.array([0.25, 0.75, 1.25, 1.75, 2.5, 3.5, 5.0], dtype=jnp.float32)

        def fp4_quant_dequant(x):
            shape = x.shape
            xb = x.reshape(shape[:-1] + (shape[-1] // BLOCK, BLOCK))
            scale = jnp.max(jnp.abs(xb), axis=-1, keepdims=True) / 6.0
            scale = jnp.maximum(scale, jnp.float32(1e-12))
            xn = xb / scale
            idx = jnp.searchsorted(_MID, jnp.abs(xn))
            q = _GRID[idx] * jnp.sign(xn) * scale
            return q.reshape(shape)

        def fp4_linear(x, w):
            xq = fp4_quant_dequant(x)
            wq = fp4_quant_dequant(w)
            return jnp.einsum('bsk,nk->bsn', xq, wq)
        key = jax.random.key(seed)
        k1, k2, k3, k4 = jax.random.split(key, 4)
        H, I = (128, 352)
        x = jax.random.normal(k1, (4, 512, H), dtype=jnp.float32)
        w_gate = jax.random.normal(k2, (I, H), dtype=jnp.float32) * 0.02
        w_up = jax.random.normal(k3, (I, H), dtype=jnp.float32) * 0.02
        w_down = jax.random.normal(k4, (H, I), dtype=jnp.float32) * 0.02
        return {'x': x, 'w_gate': w_gate, 'w_up': w_up, 'w_down': w_down}
    _L3_ffn_in = _L3_ffn_setup()
    _d = {'L0_attn_a_X': _L0_attn_a_in['X'], 'L0_attn_a_Wq': _L0_attn_a_in['Wq'], 'L0_attn_a_Wv': _L0_attn_a_in['Wv'], 'L0_attn_a_q_norm_w': _L0_attn_a_in['q_norm_w'], 'L0_attn_a_v_norm_w': _L0_attn_a_in['v_norm_w'], 'L0_attn_b_Wq': _L0_attn_b_in['Wq'], 'L0_attn_b_Wk': _L0_attn_b_in['Wk'], 'L0_attn_b_Wv': _L0_attn_b_in['Wv'], 'L0_ffn_gate_w': _L0_ffn_in['gate_w'], 'L0_ffn_expert_bias': _L0_ffn_in['expert_bias'], 'L0_ffn_w_up': _L0_ffn_in['w_up'], 'L0_ffn_w_down': _L0_ffn_in['w_down'], 'L1_attn_a_Wqkv': _L1_attn_a_in['Wqkv'], 'L1_attn_a_bqkv': _L1_attn_a_in['bqkv'], 'L1_attn_a_Wout': _L1_attn_a_in['Wout'], 'L1_attn_a_bout': _L1_attn_a_in['bout'], 'L1_attn_b_Wk': _L1_attn_b_in['Wk'], 'L1_attn_b_Wq': _L1_attn_b_in['Wq'], 'L1_attn_b_Wv': _L1_attn_b_in['Wv'], 'L1_ffn_Wg': _L1_ffn_in['Wg'], 'L1_ffn_bg': _L1_ffn_in['bg'], 'L1_ffn_W1': _L1_ffn_in['W1'], 'L1_ffn_b1': _L1_ffn_in['b1'], 'L1_ffn_W2': _L1_ffn_in['W2'], 'L1_ffn_b2': _L1_ffn_in['b2'], 'L2_attn_a_Wq': _L2_attn_a_in['Wq'], 'L2_attn_a_bq': _L2_attn_a_in['bq'], 'L2_attn_a_Wk': _L2_attn_a_in['Wk'], 'L2_attn_a_bk': _L2_attn_a_in['bk'], 'L2_attn_a_Wv': _L2_attn_a_in['Wv'], 'L2_attn_a_bv': _L2_attn_a_in['bv'], 'L2_attn_a_Wo': _L2_attn_a_in['Wo'], 'L2_attn_a_bo': _L2_attn_a_in['bo'], 'L2_attn_b_w_qkv': _L2_attn_b_in['w_qkv'], 'L2_attn_b_w_proj': _L2_attn_b_in['w_proj'], 'L2_attn_b_b_proj': _L2_attn_b_in['b_proj'], 'L2_attn_b_ln_gamma': _L2_attn_b_in['ln_gamma'], 'L2_attn_b_ln_beta': _L2_attn_b_in['ln_beta'], 'L2_ffn_w_gate': _L2_ffn_in['w_gate'], 'L2_ffn_w_up': _L2_ffn_in['w_up'], 'L2_ffn_w_down': _L2_ffn_in['w_down'], 'L3_attn_a_qkv_w': _L3_attn_a_in['qkv_w'], 'L3_attn_a_qkv_b': _L3_attn_a_in['qkv_b'], 'L3_attn_a_proj_w': _L3_attn_a_in['proj_w'], 'L3_attn_a_proj_b': _L3_attn_a_in['proj_b'], 'L3_attn_b_w_norm_in': _L3_attn_b_in['w_norm_in'], 'L3_attn_b_w_norm_out': _L3_attn_b_in['w_norm_out'], 'L3_attn_b_router_w1': _L3_attn_b_in['router_w1'], 'L3_attn_b_router_w2': _L3_attn_b_in['router_w2'], 'L3_attn_b_router_b2': _L3_attn_b_in['router_b2'], 'L3_attn_b_ttt_w1': _L3_attn_b_in['ttt_w1'], 'L3_attn_b_ttt_b1': _L3_attn_b_in['ttt_b1'], 'L3_attn_b_ttt_w2': _L3_attn_b_in['ttt_w2'], 'L3_attn_b_ttt_b2': _L3_attn_b_in['ttt_b2'], 'L3_attn_b_lambdas': _L3_attn_b_in['lambdas'], 'L3_attn_b_slr_wq1': _L3_attn_b_in['slr_wq1'], 'L3_attn_b_slr_wq2': _L3_attn_b_in['slr_wq2'], 'L3_attn_b_slr_wk1': _L3_attn_b_in['slr_wk1'], 'L3_attn_b_slr_wk2': _L3_attn_b_in['slr_wk2'], 'L3_attn_b_slr_wv': _L3_attn_b_in['slr_wv'], 'L3_attn_b_slr_wo': _L3_attn_b_in['slr_wo'], 'L3_attn_b_slr_lam': _L3_attn_b_in['slr_lam'], 'L3_attn_b_landmarks': _L3_attn_b_in['landmarks'], 'L3_attn_b_mix_w': _L3_attn_b_in['mix_w'], 'L3_attn_b_bus_compress': _L3_attn_b_in['bus_compress'], 'L3_attn_b_bus_expand': _L3_attn_b_in['bus_expand'], 'L3_attn_b_bus_publish': _L3_attn_b_in['bus_publish'], 'L3_ffn_w_gate': _L3_ffn_in['w_gate'], 'L3_ffn_w_up': _L3_ffn_in['w_up'], 'L3_ffn_w_down': _L3_ffn_in['w_down']}
    _x0 = _d['L0_attn_a_X']
    _d['L0_attn_a_X'] = jax.random.normal(jax.random.fold_in(jax.random.key(seed), 1), (8, 512, 128), dtype=_x0.dtype)
    del _x0
    return _d

def reference(L0_attn_a_X, L0_attn_a_Wq, L0_attn_a_Wv, L0_attn_a_q_norm_w, L0_attn_a_v_norm_w, L0_attn_b_Wq, L0_attn_b_Wk, L0_attn_b_Wv, L0_ffn_gate_w, L0_ffn_expert_bias, L0_ffn_w_up, L0_ffn_w_down, L1_attn_a_Wqkv, L1_attn_a_bqkv, L1_attn_a_Wout, L1_attn_a_bout, L1_attn_b_Wk, L1_attn_b_Wq, L1_attn_b_Wv, L1_ffn_Wg, L1_ffn_bg, L1_ffn_W1, L1_ffn_b1, L1_ffn_W2, L1_ffn_b2, L2_attn_a_Wq, L2_attn_a_bq, L2_attn_a_Wk, L2_attn_a_bk, L2_attn_a_Wv, L2_attn_a_bv, L2_attn_a_Wo, L2_attn_a_bo, L2_attn_b_w_qkv, L2_attn_b_w_proj, L2_attn_b_b_proj, L2_attn_b_ln_gamma, L2_attn_b_ln_beta, L2_ffn_w_gate, L2_ffn_w_up, L2_ffn_w_down, L3_attn_a_qkv_w, L3_attn_a_qkv_b, L3_attn_a_proj_w, L3_attn_a_proj_b, L3_attn_b_w_norm_in, L3_attn_b_w_norm_out, L3_attn_b_router_w1, L3_attn_b_router_w2, L3_attn_b_router_b2, L3_attn_b_ttt_w1, L3_attn_b_ttt_b1, L3_attn_b_ttt_w2, L3_attn_b_ttt_b2, L3_attn_b_lambdas, L3_attn_b_slr_wq1, L3_attn_b_slr_wq2, L3_attn_b_slr_wk1, L3_attn_b_slr_wk2, L3_attn_b_slr_wv, L3_attn_b_slr_wo, L3_attn_b_slr_lam, L3_attn_b_landmarks, L3_attn_b_mix_w, L3_attn_b_bus_compress, L3_attn_b_bus_expand, L3_attn_b_bus_publish, L3_ffn_w_gate, L3_ffn_w_up, L3_ffn_w_down):

    def _L0_attn_a_ref(X, Wq, Wv, q_norm_w, v_norm_w):
        import jax, jax.numpy as jnp
        import numpy as np
        EPS = 1e-08

        def rms_norm_multihead(x, weight):
            x32 = x.astype(jnp.float32)
            normed = x32 * jax.lax.rsqrt(jnp.mean(x32 * x32, axis=-1, keepdims=True) + EPS)
            return normed.astype(x.dtype) * weight
        B, L, D = X.shape
        H, d = q_norm_w.shape
        K = X.reshape(B, L, H, d)
        Q = rms_norm_multihead((X @ Wq.T).reshape(B, L, H, d), q_norm_w)
        V = rms_norm_multihead((X @ Wv.T).reshape(B, L, H, d), v_norm_w)
        W = jnp.cumsum(jnp.einsum('blhd,blhe->blhde', K, V), axis=1)
        out = jnp.einsum('blhd,blhde->blhe', Q, W).reshape(B, L, D)
        return out

    def _L0_attn_b_ref(x, Wq, Wk, Wv):
        import jax, jax.numpy as jnp
        import numpy as np
        B, S, D = (2, 256, 128)
        H = 16
        DK = 128
        DV = 128
        EPS = 1e-05
        b, s, d = x.shape
        dkh = DK // H
        dvh = DV // H
        Q = (x @ Wq.T).reshape(H, b, s, dkh)
        K = (x @ Wk.T).reshape(H, b, s, dkh)
        V = (x @ Wv.T).reshape(H, b, s, dvh)
        scores = jnp.einsum('hbqd,hbkd->hbqk', Q, K)
        atten = jax.nn.softmax(scores, axis=-1)
        out = jnp.einsum('hbqk,hbkd->hbqd', atten, V).reshape(b, s, -1)
        y = out + x
        mu = jnp.mean(y, axis=(1, 2), keepdims=True)
        var = jnp.var(y, axis=(1, 2), keepdims=True)
        return (y - mu) / jnp.sqrt(var + EPS)

    def _L0_ffn_ref(x, gate_w, expert_bias, w_up, w_down):
        import jax, jax.numpy as jnp
        import numpy as np
        B, S, H, E, K, I = (4, 256, 128, 8, 2, 512)
        GATE_EPS = 1e-06
        LN_EPS = 1e-05
        logits = jnp.einsum('bsh,eh->bse', x, gate_w) + expert_bias
        weights = jax.nn.softmax(logits, axis=-1)
        top_w, top_i = jax.lax.top_k(weights, K)
        top_w = top_w / (jnp.sum(top_w, axis=-1, keepdims=True) + GATE_EPS)
        sparse_w = jnp.sum(jax.nn.one_hot(top_i, E, dtype=weights.dtype) * top_w[..., None], axis=-2)
        out = jnp.zeros_like(x)
        for e in range(E):
            h = jax.nn.gelu(jnp.einsum('bsh,ih->bsi', x, w_up[e]), approximate=False)
            y = jnp.einsum('bsi,hi->bsh', h, w_down[e])
            out = out + sparse_w[..., e:e + 1] * y
        mu = jnp.mean(out, axis=-1, keepdims=True)
        var = jnp.mean(jnp.square(out - mu), axis=-1, keepdims=True)
        out = (out - mu) * jax.lax.rsqrt(var + LN_EPS)
        return out + x

    def _L1_attn_a_ref(x, Wqkv, bqkv, Wout, bout):
        import jax, jax.numpy as jnp
        import numpy as np
        D_MODEL = 128
        N_HEADS = 16
        HEAD_DIM = D_MODEL // N_HEADS
        SEQ = 256
        BATCH = 2
        ROPE_BASE = 10000.0

        def _rotary_cache(head_dim, seq_len, base=ROPE_BASE):
            pos = jnp.arange(seq_len, dtype=jnp.float32)
            inv_freq = 1.0 / base ** (jnp.arange(0, head_dim, 2, dtype=jnp.float32) / head_dim)
            freqs = jnp.einsum('i,j->ij', pos, inv_freq)
            cos = jnp.repeat(jnp.cos(freqs), 2, axis=1)
            sin = jnp.repeat(jnp.sin(freqs), 2, axis=1)
            return (cos, sin)

        def _rotate_every_two(x):
            x1 = x[..., ::2]
            x2 = x[..., 1::2]
            return jnp.stack((-x2, x1), axis=-1).reshape(x.shape)

        def _apply_rotary(x, cos, sin):
            return x * cos + _rotate_every_two(x) * sin
        seq_len, batch, _ = x.shape
        scale = HEAD_DIM ** (-0.5)
        xb = jnp.transpose(x, (1, 0, 2))
        qkv = xb @ Wqkv + bqkv
        q, k, v = jnp.split(qkv, 3, axis=-1)

        def split_heads(t):
            return t.reshape(batch, seq_len, N_HEADS, HEAD_DIM).transpose(0, 2, 1, 3)
        q, k, v = (split_heads(q), split_heads(k), split_heads(v))
        cos, sin = _rotary_cache(HEAD_DIM, seq_len)
        cos = cos[None, None]
        sin = sin[None, None]
        q = _apply_rotary(q, cos, sin)
        k = _apply_rotary(k, cos, sin)
        scores = jnp.einsum('bhqd,bhkd->bhqk', q, k) * scale
        causal = jnp.triu(jnp.ones((seq_len, seq_len), dtype=bool), k=1)
        scores = jnp.where(causal[None, None], -jnp.inf, scores)
        weights = jax.nn.softmax(scores, axis=-1)
        attn = jnp.einsum('bhqk,bhkd->bhqd', weights, v)
        attn = attn.transpose(0, 2, 1, 3).reshape(batch, seq_len, D_MODEL)
        out = attn @ Wout + bout
        return jnp.transpose(out, (1, 0, 2))

    def _L1_attn_b_ref(x, Wk, Wq, Wv):
        import math
        import jax, jax.numpy as jnp
        import numpy as np
        B, T, C, H = (4, 256, 128, 128)
        K = x @ Wk
        Q = x @ Wq
        V = x @ Wv
        scale = 1.0 / math.sqrt(K.shape[-1])
        wei = jnp.einsum('bth,bsh->bts', Q, K) * scale
        t = x.shape[1]
        causal = jnp.tril(jnp.ones((t, t), dtype=bool))
        wei = jnp.where(causal, wei, -jnp.inf)
        wei = jax.nn.softmax(wei, axis=-1)
        wei = jax.nn.relu(wei)
        return jnp.einsum('bts,bsh->bth', wei, V)

    def _L1_ffn_ref(x, Wg, bg, W1, b1, W2, b2):
        import jax, jax.numpy as jnp
        import numpy as np
        D_MODEL = 128
        D_HIDDEN = 512
        N_EXPERTS = 8
        B, S = (2, 256)
        logits = jnp.einsum('bsd,de->bse', x, Wg) + bg
        expert_idx = jnp.argmax(logits, axis=-1)
        h = jax.nn.gelu(jnp.einsum('bsd,edh->bseh', x, W1) + b1, approximate=False)
        y = jnp.einsum('bseh,ehd->bsed', h, W2) + b2
        out = jnp.take_along_axis(y, expert_idx[:, :, None, None], axis=2)[:, :, 0, :]
        return out

    def _L2_attn_a_ref(x, Wq, bq, Wk, bk, Wv, bv, Wo, bo):
        import jax, jax.numpy as jnp
        import numpy as np
        D_MODEL = 128
        N_HEADS = 16
        D_K = D_MODEL // N_HEADS
        THETA = 10000.0
        EPS = 1e-08

        def _apply_rope(t):
            s = t.shape[-2]
            pos = jnp.arange(s, dtype=jnp.float32)
            kidx = jnp.arange(D_K // 2, dtype=jnp.float32)
            ang = pos[:, None] / THETA ** (2.0 * kidx / D_K)
            cos, sin = (jnp.cos(ang), jnp.sin(ang))
            x1 = t[..., 0::2]
            x2 = t[..., 1::2]
            r1 = cos * x1 - sin * x2
            r2 = sin * x1 + cos * x2
            return jnp.stack([r1, r2], axis=-1).reshape(t.shape)

        def _my_softmax(x, axis):
            m = jnp.max(x, axis=axis, keepdims=True)
            e = jnp.exp(x - m)
            return e / (jnp.sum(e, axis=axis, keepdims=True) + EPS)
        B, S, _ = x.shape
        q = x @ Wq.T + bq
        k = x @ Wk.T + bk
        v = x @ Wv.T + bv

        def split_heads(t):
            return t.reshape(B, S, N_HEADS, D_K).transpose(0, 2, 1, 3)
        q, k, v = (split_heads(q), split_heads(k), split_heads(v))
        q = _apply_rope(q)
        k = _apply_rope(k)
        scores = jnp.einsum('bhqd,bhkd->bhqk', q, k) / jnp.sqrt(jnp.float32(D_K))
        causal = jnp.tril(jnp.ones((S, S), dtype=bool))
        scores = jnp.where(causal, scores, -jnp.inf)
        attn = _my_softmax(scores, axis=-1)
        ctx = jnp.einsum('bhqk,bhkd->bhqd', attn, v)
        ctx = ctx.transpose(0, 2, 1, 3).reshape(B, S, D_MODEL)
        return ctx @ Wo.T + bo

    def _L2_attn_b_ref(target, w_qkv, w_proj, b_proj, ln_gamma, ln_beta):
        import jax, jax.numpy as jnp
        import numpy as np
        B, T, D, H = (4, 256, 128, 16)
        HD = D // H
        EPS = 1e-05
        NEG = 10000000000.0
        b, t, d = target.shape
        resid = target
        qkv = target @ w_qkv
        q, k, v = jnp.split(qkv, 3, axis=-1)
        q = q.reshape(b, t, H, HD).transpose(0, 2, 1, 3)
        k = k.reshape(b, t, H, HD).transpose(0, 2, 1, 3)
        v = v.reshape(b, t, H, HD).transpose(0, 2, 1, 3)
        scores = jnp.einsum('bhqd,bhkd->bhqk', q, k) * (1.0 / np.sqrt(HD))
        causal = (jnp.arange(t)[:, None] >= jnp.arange(t)[None, :]).astype(scores.dtype)
        scores = scores * causal - (1.0 - causal) * NEG
        attn = jax.nn.softmax(scores, axis=-1)
        out = jnp.einsum('bhqk,bhkd->bhqd', attn, v)
        out = out.transpose(0, 2, 1, 3).reshape(b, t, d)
        proj = out @ w_proj + b_proj
        x = proj + resid
        mu = jnp.mean(x, axis=-1, keepdims=True)
        var = jnp.var(x, axis=-1, keepdims=True)
        return (x - mu) * jax.lax.rsqrt(var + EPS) * ln_gamma + ln_beta

    def _L2_ffn_ref(x, w_gate, w_up, w_down):
        import jax, jax.numpy as jnp
        import numpy as np
        BLOCK = 16
        _GRID = jnp.array([0.0, 0.5, 1.0, 1.5, 2.0, 3.0, 4.0, 6.0], dtype=jnp.float32)
        _MID = jnp.array([0.25, 0.75, 1.25, 1.75, 2.5, 3.5, 5.0], dtype=jnp.float32)

        def fp4_quant_dequant(x):
            shape = x.shape
            xb = x.reshape(shape[:-1] + (shape[-1] // BLOCK, BLOCK))
            scale = jnp.max(jnp.abs(xb), axis=-1, keepdims=True) / 6.0
            scale = jnp.maximum(scale, jnp.float32(1e-12))
            xn = xb / scale
            idx = jnp.searchsorted(_MID, jnp.abs(xn))
            q = _GRID[idx] * jnp.sign(xn) * scale
            return q.reshape(shape)

        def fp4_linear(x, w):
            xq = fp4_quant_dequant(x)
            wq = fp4_quant_dequant(w)
            return jnp.einsum('bsk,nk->bsn', xq, wq)
        gate = fp4_linear(x, w_gate)
        y = fp4_linear(x, w_up)
        h = jax.nn.silu(gate) * y
        return fp4_linear(h, w_down)

    def _L3_attn_a_ref(x, qkv_w, qkv_b, proj_w, proj_b):
        import jax, jax.numpy as jnp
        import numpy as np
        import math
        NUM_HEADS = 16
        ROPE_THETA = 10000.0

        def _rope(x, pos):
            d_k = x.shape[-1]
            inv_freq = 1.0 / ROPE_THETA ** (jnp.arange(0, d_k, 2, dtype=jnp.float32) / d_k)
            ang = pos[:, None].astype(jnp.float32) * inv_freq[None, :]
            cos, sin = (jnp.cos(ang), jnp.sin(ang))
            x1, x2 = (x[..., 0::2], x[..., 1::2])
            r1 = x1 * cos - x2 * sin
            r2 = x1 * sin + x2 * cos
            return jnp.stack([r1, r2], axis=-1).reshape(x.shape)
        B, S, D = x.shape
        H = NUM_HEADS
        d_k = D // H
        qkv = x @ qkv_w.T + qkv_b
        qkv = qkv.reshape(B, S, 3, H, d_k).transpose(2, 0, 3, 1, 4)
        q, k, v = (qkv[0], qkv[1], qkv[2])
        pos = jnp.arange(S)
        q = _rope(q, pos)
        k = _rope(k, pos)
        scale = 1.0 / math.sqrt(d_k)
        scores = jnp.einsum('bhqd,bhkd->bhqk', q, k) * scale
        causal = jnp.tril(jnp.ones((S, S), dtype=bool))
        scores = jnp.where(causal[None, None], scores, -jnp.inf)
        attn = jax.nn.softmax(scores, axis=-1)
        y = jnp.einsum('bhqk,bhkd->bhqd', attn, v)
        y = y.transpose(0, 2, 1, 3).reshape(B, S, D)
        return y @ proj_w.T + proj_b

    def _L3_attn_b_ref(x, w_norm_in, w_norm_out, router_w1, router_w2, router_b2, ttt_w1, ttt_b1, ttt_w2, ttt_b2, lambdas, slr_wq1, slr_wq2, slr_wk1, slr_wk2, slr_wv, slr_wo, slr_lam, landmarks, mix_w, bus_compress, bus_expand, bus_publish):
        import jax, jax.numpy as jnp
        import numpy as np
        import math
        B, S, D = (4, 256, 128)
        H, DEG, DH, BUS, SLOTS = (8, 4, 32, 128, 64)
        EPS = 1.1920929e-07

        def _rms(x, w):
            return x * jax.lax.rsqrt(jnp.mean(x * x, axis=-1, keepdims=True) + EPS) * w
        b, s, d = x.shape
        hd = d // H
        residual = x
        xn = _rms(x, w_norm_in)
        route_in = xn.mean(axis=1)
        logits = jax.nn.silu(route_in @ router_w1) @ router_w2 + router_b2
        probs = jax.nn.softmax(logits, axis=-1)
        p_medium, p_full = (probs[:, 1], probs[:, 2])
        ttt = (jax.nn.silu(route_in @ ttt_w1 + ttt_b1) @ ttt_w2 + ttt_b2).reshape(b, H, DEG)
        ttt_scale = 0.1 * jnp.tanh(ttt)
        xh = xn.reshape(b, s, H, hd).transpose(1, 0, 2, 3)
        lam = lambdas[None, :, None]

        def ema_step(state, xt):
            state = lam * state + (1.0 - lam) * xt
            return (state, state)
        _, ys = jax.lax.scan(ema_step, jnp.zeros((b, H, hd), x.dtype), xh)
        ssm_out = ys.transpose(1, 0, 2, 3).reshape(b, s, d)
        q1, q2 = (xn @ slr_wq1, xn @ slr_wq2)
        k1, k2 = (xn @ slr_wk1, xn @ slr_wk2)
        v = xn @ slr_wv
        sc = 1.0 / math.sqrt(DH)
        a1 = jax.nn.softmax(jnp.einsum('bqd,bkd->bqk', q1, k1) * sc, axis=-1)
        a2 = jax.nn.softmax(jnp.einsum('bqd,bkd->bqk', q2, k2) * sc, axis=-1)
        ctx = jnp.einsum('bqk,bkd->bqd', a1 - slr_lam * a2, v)
        slr_out = ctx @ slr_wo
        mixed = ssm_out + (p_medium + p_full)[:, None, None] * slr_out
        qy = xn[:, -1:, :]
        kk = jnp.broadcast_to(landmarks[None], (b, SLOTS, d))
        attn = jax.nn.softmax(jnp.einsum('bqd,bkd->bqk', qy, kk) / math.sqrt(d), axis=-1)
        arc_ctx = jnp.einsum('bqk,bkd->bqd', attn, kk)
        mixed = mixed.at[:, -1:, :].add(p_full[:, None, None] * arc_ctx)
        out = jnp.concatenate([mixed, xn], axis=-1) @ mix_w
        out = residual + _rms(out, w_norm_out)
        summary = out.mean(axis=1, keepdims=True) @ bus_compress
        published = summary @ bus_publish
        aw = jax.nn.softmax(jnp.einsum('bqd,bkd->bqk', summary, published) / math.sqrt(BUS), axis=-1)
        context = jnp.einsum('bqk,bkd->bqd', aw, published)
        out = out + 0.1 * (context @ bus_expand)
        return out

    def _L3_ffn_ref(x, w_gate, w_up, w_down):
        import jax, jax.numpy as jnp
        import numpy as np
        BLOCK = 16
        _GRID = jnp.array([0.0, 0.5, 1.0, 1.5, 2.0, 3.0, 4.0, 6.0], dtype=jnp.float32)
        _MID = jnp.array([0.25, 0.75, 1.25, 1.75, 2.5, 3.5, 5.0], dtype=jnp.float32)

        def fp4_quant_dequant(x):
            shape = x.shape
            xb = x.reshape(shape[:-1] + (shape[-1] // BLOCK, BLOCK))
            scale = jnp.max(jnp.abs(xb), axis=-1, keepdims=True) / 6.0
            scale = jnp.maximum(scale, jnp.float32(1e-12))
            xn = xb / scale
            idx = jnp.searchsorted(_MID, jnp.abs(xn))
            q = _GRID[idx] * jnp.sign(xn) * scale
            return q.reshape(shape)

        def fp4_linear(x, w):
            xq = fp4_quant_dequant(x)
            wq = fp4_quant_dequant(w)
            return jnp.einsum('bsk,nk->bsn', xq, wq)
        gate = fp4_linear(x, w_gate)
        y = fp4_linear(x, w_up)
        h = jax.nn.silu(gate) * y
        return fp4_linear(h, w_down)
    x = L0_attn_a_X
    x = x + _L0_attn_a_ref(_layernorm(x, axis=-1), L0_attn_a_Wq, L0_attn_a_Wv, L0_attn_a_q_norm_w, L0_attn_a_v_norm_w)
    x = x + _L0_ffn_ref(_layernorm(x, axis=-1), L0_ffn_gate_w, L0_ffn_expert_bias, L0_ffn_w_up, L0_ffn_w_down)
    x = x + _L0_attn_b_ref(_layernorm(x, axis=-1), L0_attn_b_Wq, L0_attn_b_Wk, L0_attn_b_Wv)
    x = x + _L0_ffn_ref(_layernorm(x, axis=-1), L0_ffn_gate_w, L0_ffn_expert_bias, L0_ffn_w_up, L0_ffn_w_down)
    x = x + _L1_attn_a_ref(_layernorm(x, axis=-1), L1_attn_a_Wqkv, L1_attn_a_bqkv, L1_attn_a_Wout, L1_attn_a_bout)
    x = x + _L1_ffn_ref(_layernorm(x, axis=-1), L1_ffn_Wg, L1_ffn_bg, L1_ffn_W1, L1_ffn_b1, L1_ffn_W2, L1_ffn_b2)
    x = x + _L1_attn_b_ref(_layernorm(x, axis=-1), L1_attn_b_Wk, L1_attn_b_Wq, L1_attn_b_Wv)
    x = x + _L1_ffn_ref(_layernorm(x, axis=-1), L1_ffn_Wg, L1_ffn_bg, L1_ffn_W1, L1_ffn_b1, L1_ffn_W2, L1_ffn_b2)
    x = x + _L2_attn_a_ref(_layernorm(x, axis=-1), L2_attn_a_Wq, L2_attn_a_bq, L2_attn_a_Wk, L2_attn_a_bk, L2_attn_a_Wv, L2_attn_a_bv, L2_attn_a_Wo, L2_attn_a_bo)
    x = x + _L2_ffn_ref(_layernorm(x, axis=-1), L2_ffn_w_gate, L2_ffn_w_up, L2_ffn_w_down)
    x = x + _L2_attn_b_ref(_layernorm(x, axis=-1), L2_attn_b_w_qkv, L2_attn_b_w_proj, L2_attn_b_b_proj, L2_attn_b_ln_gamma, L2_attn_b_ln_beta)
    x = x + _L2_ffn_ref(_layernorm(x, axis=-1), L2_ffn_w_gate, L2_ffn_w_up, L2_ffn_w_down)
    x = x + _L3_attn_a_ref(_layernorm(x, axis=-1), L3_attn_a_qkv_w, L3_attn_a_qkv_b, L3_attn_a_proj_w, L3_attn_a_proj_b)
    x = x + _L3_ffn_ref(_layernorm(x, axis=-1), L3_ffn_w_gate, L3_ffn_w_up, L3_ffn_w_down)
    x = x + _L3_attn_b_ref(_layernorm(x, axis=-1), L3_attn_b_w_norm_in, L3_attn_b_w_norm_out, L3_attn_b_router_w1, L3_attn_b_router_w2, L3_attn_b_router_b2, L3_attn_b_ttt_w1, L3_attn_b_ttt_b1, L3_attn_b_ttt_w2, L3_attn_b_ttt_b2, L3_attn_b_lambdas, L3_attn_b_slr_wq1, L3_attn_b_slr_wq2, L3_attn_b_slr_wk1, L3_attn_b_slr_wk2, L3_attn_b_slr_wv, L3_attn_b_slr_wo, L3_attn_b_slr_lam, L3_attn_b_landmarks, L3_attn_b_mix_w, L3_attn_b_bus_compress, L3_attn_b_bus_expand, L3_attn_b_bus_publish)
    x = x + _L3_ffn_ref(_layernorm(x, axis=-1), L3_ffn_w_gate, L3_ffn_w_up, L3_ffn_w_down)
    return x

_drawn_inputs = setup_inputs


def setup_inputs(seed=0):
    import zlib

    import numpy as np

    out = dict(_drawn_inputs(seed))
    spreads = {'L0_attn_a_q_norm_w': (1.0, 0.2),
     'L0_attn_a_v_norm_w': (1.0, 0.2),
     'L0_ffn_expert_bias': (0.0, 0.1),
     'L1_attn_a_bqkv': (0.0, 0.1),
     'L1_attn_a_bout': (0.0, 0.1),
     'L1_ffn_bg': (0.0, 0.1),
     'L1_ffn_b1': (0.0, 0.1),
     'L1_ffn_b2': (0.0, 0.1),
     'L2_attn_b_b_proj': (0.0, 0.1),
     'L2_attn_b_ln_gamma': (1.0, 0.2),
     'L2_attn_b_ln_beta': (0.0, 0.1),
     'L3_attn_b_w_norm_in': (1.0, 0.2),
     'L3_attn_b_w_norm_out': (1.0, 0.2),
     'L3_attn_b_router_b2': (0.5, 0.2),
     'L3_attn_b_ttt_b1': (0.0, 0.1),
     'L3_attn_b_ttt_b2': (0.0, 0.1)}
    factors = {}
    for name, (base, spread) in spreads.items():
        noise = np.random.default_rng([zlib.crc32(name.encode()), seed]).standard_normal(out[name].shape)
        drawn = base * np.exp(spread * noise) if base else spread * noise
        out[name] = jnp.asarray(drawn.astype(out[name].dtype))
    for name, factor in factors.items():
        out[name] = (out[name] * factor).astype(out[name].dtype)
    return out
```

```python
import math
from contextlib import ExitStack

import numpy as np

import concourse.bass as bass
from concourse import mybir

FP32 = mybir.dt.float32
BF16 = mybir.dt.bfloat16
I32 = mybir.dt.int32
U32 = mybir.dt.uint32
ALU = mybir.AluOpType
ACT = mybir.ActivationFunctionType
AX = mybir.AxisListType

B, S, D = 8, 512, 128
P = 128
NT = B * S // P
TB = S // P
H, HD = 16, 8
PAIRS = H // 2
SLOT = 64
NEG = -1.0e30
LN_EPS = 1e-5
PRIME = 8


class Signal:

    def __init__(self, sem):
        self.sem, self.base, self.per = sem, PRIME, 0

    def begin(self, per):
        self.per = per

    def at(self, i, k):
        return i * self.per + (self.base + k)

    def end(self, rounds):
        self.base += rounds * self.per


class Chain:

    def __init__(self, signal, eng, i, passed=None):
        self.s, self.eng, self.i, self.k, self.passed = signal, eng, i, 0, passed

    def link(self, ins):
        self.k += 1
        ins.then_inc(self.s.sem, 1)
        self.eng.wait_ge(self.s.sem, self.s.at(self.i, self.k))
        if self.passed is not None:
            self.eng.sem_inc(self.passed, 1)

    def close(self):
        assert self.k <= self.s.per, (self.k, self.s.per)
        if self.s.per > self.k:
            self.eng.sem_inc(self.s.sem, self.s.per - self.k)


class Core:

    def __init__(self, nc, ctx):
        self.nc, self.ctx = nc, ctx
        self.signals = {}
        self.banks = [ctx.enter_context(nc.psum_tensor(f"bank{n}", [P, 512], FP32)) for n in range(0)]

    def sb(self, name, shape, dt=FP32):
        return self.ctx.enter_context(self.nc.sbuf_tensor(name, shape, dt))

    def begin(self, **per):
        out = []
        for name, n in per.items():
            s = self.signals[name]
            s.begin(n)
            out.append(s)
        return out

    def end(self, rounds, signals):
        for s in signals:
            s.end(rounds)


SIGNALS = [
    "dve_step", "act_step", "pool_step", "stats_ready", "rstd_ready", "norm_ready", "normT_in_psum",
    "normT_ready", "xT_ready", "proj_in_psum", "proj_read", "rotated", "k_ready", "qv_ready",
    "qkT_in_psum", "qkT_ready", "scores_ready", "scores_read", "max_ready", "q2T_in_psum", "q2T_ready",
    "scoresT_ready", "probs_ready", "pv_ready", "pv_read", "pvT_ready", "pvT_read", "attn_ready", "attnT_in_psum",
    "attnT_ready", "out_ready", "out_read", "up_ready", "act_ready", "down_ready", "down_read",
    "gate_ready", "exp_ready", "quant_ready", "quantT_in_psum", "quantT_ready", "state_ready",
    "state_used", "sum_ready", "pool_ready", "xq_ready", "xqT_in_psum", "mul_done",
    "decayed", "repeated", "silu_ready", "route_in_psum", "route_max", "route_exp", "route_ready",
    "land_max", "land_exp", "mixed_ready", "output_ready", "mean_in_psum",
]


def token_view(ap):
    return ap.rearrange("b (t p) d -> p (b t) d", p=P)


LATER = {"l1f_up": "l0f_up", "l1f_down": "l0f_down"}


def load_stage(core, dram):
    nc = core.nc
    core.pool_passed = core.ctx.enter_context(nc.semaphore("pool_passed"))
    core.w = {}
    core.X = core.sb("X", [P, NT, D])
    core.XN = core.sb("XN", [P, NT, D])
    core.XNT = core.sb("XNT", [P, NT * P])
    core.identf = core.sb("identf", [P, P])
    core.identb = core.sb("identb", [P, P], BF16)
    core.mask_qk = core.sb("mask_qk", [P, P], BF16)
    core.mask_kq = core.sb("mask_kq", [P, P], BF16)
    core.keep_kq = core.sb("keep_kq", [P, P])
    core.ones = core.sb("ones", [P, P])
    core.iota8 = core.sb("iota8", [P, 8])
    core.minus_half = core.sb("minus_half", [P, 8])
    core.w_inT = core.sb("w_inT", [P, 2 * HID])
    core.w_outT = core.sb("w_outT", [P, 3, D])
    core.G = core.sb("G", [P, NT, 8])
    core.loads2 = core.ctx.enter_context(nc.semaphore("weights2_loaded"))
    core.work_base = None
    made = core.ctx.enter_context(nc.semaphore("constants_made"))
    done = core.ctx.enter_context(nc.semaphore("x_loaded"))
    core.loads = core.ctx.enter_context(nc.semaphore("weights_loaded"))

    core.dram = dram
    dram_now = {name: src for name, src in dram.items() if name not in LATER}
    for name, src in dram_now.items():
        if name != "X":
            core.w[name] = core.sb(name, [P if n == 0 else x for n, x in enumerate(src.shape)])

    with nc.Block() as block:
        @block.sync
        def _(sp):
            sp.dma_start(core.X[:, :, :], token_view(dram["X"])).then_inc(done, 16)
            n = 0
            for name, src in dram_now.items():
                if name != "X":
                    dst = core.w[name][tuple(slice(0, x) for x in src.shape)]
                    sp.dma_start(dst, src).then_inc(core.loads, 16)
                    n += 16
            sp.wait_ge(done, 16)
            sp.wait_ge(core.loads, n)

        @block.vector
        def _(dve):
            for s in core.signals.values():
                dve.sem_inc(s.sem, PRIME)

        @block.gpsimd
        def _(pool):
            pool.memset(core.identf[:, :], 0.0).then_inc(made, 1)
            pool.memset(core.identb[:, :], 0.0).then_inc(made, 1)
            pool.memset(core.mask_qk[:, :], 0.0).then_inc(made, 1)
            pool.memset(core.mask_kq[:, :], 0.0).then_inc(made, 1)
            pool.memset(core.keep_kq[:, :], 1.0).then_inc(made, 1)
            pool.memset(core.ones[:, :], 1.0).then_inc(made, 1)
            pool.memset(core.minus_half[:, :], -0.5).then_inc(made, 1)
            pool.iota(core.iota8[:, :], [[1, 8]], base=0, channel_multiplier=0,
                      allow_small_or_imprecise_dtypes=True).then_inc(made, 1)
            pool.wait_ge(made, 8)
            for m in (core.identf, core.identb):
                pool.affine_select(out=m[:, :], in_=m[:, :], compare_op=ALU.not_equal, fill=1.0,
                                   base=0, pattern=[[-1, P]], channel_multiplier=1).then_inc(made, 1)
            pool.affine_select(out=core.mask_qk[:, :], in_=core.mask_qk[:, :], compare_op=ALU.is_ge,
                               fill=NEG, base=0, pattern=[[-1, P]], channel_multiplier=1).then_inc(made, 1)
            for m, fill in ((core.mask_kq, NEG), (core.keep_kq, 0.0)):
                pool.affine_select(out=m[:, :], in_=m[:, :], compare_op=ALU.is_ge,
                                   fill=fill, base=0, pattern=[[1, P]], channel_multiplier=-1).then_inc(made, 1)
            pool.wait_ge(made, 13)


def store_stage(core, out):
    nc = core.nc
    stored = core.ctx.enter_context(nc.semaphore("stored"))
    with nc.Block() as block:
        @block.sync
        def _(sp):
            sp.dma_start(token_view(out), core.X[:, :, :]).then_inc(stored, 16)
            sp.wait_ge(stored, 16)


def norm_stage(core, name):
    nc = core.nc
    with ExitStack() as ctx:
        stats = ctx.enter_context(nc.sbuf_tensor(f"{name}_stats", [P, TB, 6], FP32))
        mv = ctx.enter_context(nc.sbuf_tensor(f"{name}_mv", [P, 2, TB, 2], FP32))
        var = ctx.enter_context(nc.sbuf_tensor(f"{name}_var", [P, TB], FP32))
        rstd = ctx.enter_context(nc.sbuf_tensor(f"{name}_rstd", [P, TB], FP32))
        xs = ctx.enter_context(nc.sbuf_tensor(f"{name}_xs", [P, 2, TB, D], FP32))
        ps = ctx.enter_context(nc.psum_tensor(f"{name}_ps", [P, 2, S], FP32))
        R = B // 2
        sig = core.begin(dve_step=16, stats_ready=2, rstd_ready=2, norm_ready=2, normT_in_psum=2,
                         normT_ready=2)
        dve_step, stats_ready, rstd_ready, norm_ready, normT_in_psum, normT_ready = sig
        block = ctx.enter_context(nc.Block())

        @block.vector
        def _(dve):
            with dve.Fori(0, R) as i:
                ch = Chain(dve_step, dve, i)
                for u in range(2):
                    for t in range(TB):
                        st = dve.bn_stats(stats[:, t, :], core.X[:, bass.ds(i * (2 * TB) + u * TB + t, 1), :])
                    ch.link(st)
                    dve.memset(var[:, 0:1], 0.0)
                    for t in range(TB):
                        ag = dve.bn_aggr(mv[:, u, t, :], stats[:, t, :])
                    ch.link(ag)
                    dve.tensor_scalar(var[:, :], mv[:, u, :, 1], LN_EPS, None, ALU.add).then_inc(stats_ready.sem, 1)
                    dve.wait_ge(rstd_ready.sem, rstd_ready.at(i, u + 1))
                    dve.wait_ge(normT_in_psum.sem, normT_in_psum.at(i, u - 1))
                    for t in range(TB):
                        a = dve.tensor_scalar(xs[:, u, t, :], core.X[:, bass.ds(i * (2 * TB) + u * TB + t, 1), :],
                                              mv[:, u, t, 0:1], rstd[:, t:t + 1], ALU.subtract, ALU.mult)
                    a.then_inc(norm_ready.sem, 1)
                    dve.wait_ge(norm_ready.sem, norm_ready.at(i, u + 1))
                    dve.tensor_copy(core.XN[:, bass.ds(i * (2 * TB) + u * TB, TB), :], xs[:, u, :, :])
                ch.close()

        @block.gpsimd
        def _(pool):
            with pool.Fori(0, R) as i:
                for u in range(2):
                    pool.wait_ge(stats_ready.sem, stats_ready.at(i, u + 1))
                    pool.tensor_tensor(rstd[:, :], var[:, :], core.minus_half[:, 0:TB], ALU.pow).then_inc(rstd_ready.sem, 1)

        @block.tensor
        def _(pe):
            with pe.Fori(0, R) as i:
                for u in range(2):
                    pe.wait_ge(norm_ready.sem, norm_ready.at(i, u + 1))
                    pe.wait_ge(normT_ready.sem, normT_ready.at(i, u - 1))
                    for t in range(TB):
                        tr = pe.transpose(ps[:, u, t * P:(t + 1) * P], xs[:, u, t, :], core.identf[:, :])
                    tr.then_inc(normT_in_psum.sem, 1)

        @block.scalar
        def _(act):
            with act.Fori(0, R) as i:
                for u in range(2):
                    act.wait_ge(normT_in_psum.sem, normT_in_psum.at(i, u + 1))
                    act.activation(core.XNT[:, bass.ds(i * (2 * S) + u * S, S)], ps[:, u, :], ACT.Copy).then_inc(normT_ready.sem, 1)

    core.end(R, sig)


def split3(ch, eng, out_parts, x, hi, rest, tmp):
    src = x
    for n, places in enumerate(out_parts):
        ch.link(eng.tensor_copy(places[0], src))
        for place in places[1:]:
            eng.tensor_copy(place, places[0])
        if n < 2:
            dst = rest if n == 0 else tmp
            ch.link(eng.tensor_tensor(dst, src, places[0], ALU.subtract))
            src = dst


Q_ROWS = ((0, 8, 24), (16, 48), (40,))
K_ROWS = ((0, 16, 40), (8, 48), (24,))
M_ROW = 32


def heads_attention_stage(core, name, w, wo=None, bo=None, bias=None, rope=True, eps=0.0, out_norm=None,
                          grouped=False):
    nc = core.nc
    scale = 1.0 if grouped else 1.0 / math.sqrt(HD)
    causal = not grouped
    first_q = [P * k if causal else 0 for k in range(TB)]
    keys = [P * (q + 1) if causal else S for q in range(TB)]
    OFF = [sum(S - n for n in first_q[:k]) for k in range(TB)]
    NE = sum(S - n for n in first_q)
    G = H // 4
    with ExitStack() as ctx:
        def sb(n, shape, dt=FP32):
            return ctx.enter_context(nc.sbuf_tensor(f"{name}_{n}", shape, dt))

        def psum(n, shape, dt=FP32):
            return ctx.enter_context(nc.psum_tensor(f"{name}_{n}", shape, dt))

        xT = sb("xT", [P, S])
        qkv = sb("qkv", [P, TB, 3 * D])
        if rope:
            rot = sb("rot", [P, TB, 2 * H, HD])
            swapped = sb("swapped", [P, TB, 2 * H, HD])
        q_rest = sb("q_rest", [P, TB * H, HD])
        q_tmp = sb("q_tmp", [P, TB * H, HD])
        k_rest = sb("k_rest", [P, TB * H, HD])
        k_tmp = sb("k_tmp", [P, TB * H, HD])
        qs = sb("qs", [P, TB, H * SLOT], BF16)
        ks = sb("ks", [P, TB, H * SLOT], BF16)
        v1 = sb("v1", [P, TB, H, 32])
        qkT = sb("qkT", [P, 2, 2, S], BF16)
        q2T = sb("q2T", [P, 2, S], BF16)
        E = sb("E", [P, 2, 2, NE])
        negm = sb("negm", [P, TB, H])
        m_rest = sb("m_rest", [P, TB, 2])
        m_tmp = sb("m_tmp", [P, TB, 2])
        oT = q_rest[:, :, :].rearrange("p n d -> p (n d)")
        ao = q_tmp[:, :, :].rearrange("p (t h) d -> p t (h d)", t=TB)
        y = qkv[:, :, 0:D]
        den = sb("den", [P, TB, 4])
        rec = sb("rec", [P, TB, 4])
        if wo is not None:
            aoT = sb("aoT", [P, S])
        if out_norm is not None:
            stats = sb("stats", [P, TB, 6])
            mv = sb("mv", [P, TB, 2])
            var = sb("var", [P, TB])
            rstd = sb("rstd", [P, TB])
        ps_s = [psum(f"ps_s{n}", [P, S]) for n in range(2)]
        ps_t = [psum(f"ps_t{n}", [P, 2, S]) for n in range(2)]
        ps_tr = psum("ps_tr", [P, S])
        ps_m = psum("ps_m", [P, S])
        tr_b = ps_tr[:, :].bitcast(BF16)
        q4 = qs[:, :, :].rearrange("p t (h s) -> p (t h) s", s=SLOT)
        k4 = ks[:, :, :].rearrange("p t (h s) -> p (t h) s", s=SLOT)

        projected, normed = int(wo is not None), int(out_norm is not None)
        sig = core.begin(dve_step=96, pool_step=16, xT_ready=1, proj_in_psum=1, rotated=1, k_ready=1, qv_ready=1,
                         qkT_in_psum=PAIRS, qkT_ready=PAIRS, q2T_in_psum=PAIRS, q2T_ready=PAIRS,
                         scores_ready=8 * PAIRS, scores_read=8 * PAIRS, max_ready=PAIRS,
                         scoresT_ready=TB * PAIRS, probs_ready=TB * PAIRS, pv_ready=PAIRS, pv_read=G, pvT_ready=G, pvT_read=G,
                         attnT_in_psum=projected, attnT_ready=projected, out_ready=projected, out_read=projected,
                         stats_ready=normed, rstd_ready=normed)
        (dve_step, pool_step, xT_ready, proj_in_psum, rotated, k_ready, qv_ready, qkT_in_psum, qkT_ready,
         q2T_in_psum, q2T_ready, scores_ready, scores_read, max_ready, scoresT_ready, probs_ready,
         pv_ready, pv_read, pvT_ready, pvT_read, attnT_in_psum, attnT_ready, out_ready, out_read, stats_ready, rstd_ready) = sig
        started = ctx.enter_context(nc.semaphore(f"{name}_started"))
        q_cleared = ctx.enter_context(nc.semaphore(f"{name}_q_cleared"))
        block = ctx.enter_context(nc.Block())

        @block.tensor
        def _(pe):
            with pe.Fori(0, B) as i:
                pe.wait_ge(xT_ready.sem, xT_ready.at(i, 1))
                pe.wait_ge(probs_ready.sem, probs_ready.at(i, 0))
                for t in range(TB):
                    mm = pe.matmul(ps_t[t // 2][:, t % 2, 0:3 * D], xT[:, t * P:(t + 1) * P], w[:, :],
                                   start=True, stop=True)
                mm.then_inc(proj_in_psum.sem, 1)
                pe.wait_ge(qv_ready.sem, qv_ready.at(i, 1))
                pe.wait_ge(k_ready.sem, k_ready.at(i, 1))

                def transposes(j):
                    pe.wait_ge(qkT_ready.sem, qkT_ready.at(i, j))
                    pe.wait_ge(q2T_ready.sem, q2T_ready.at(i, max(j - 1, 0)))
                    if j == 0 and wo is not None:
                        pe.wait_ge(attnT_ready.sem, attnT_ready.at(i, 0))
                    pe.wait_ge(pvT_read.sem, pvT_read.at(i, max(0, (j - 2) // 2)))
                    for n, src in enumerate((qs, ks)):
                        for t in range(TB):
                            tr = pe.transpose(tr_b[:, n * S + t * P:n * S + (t + 1) * P],
                                              src[:, t, j * P:(j + 1) * P], core.identb[:, :])
                    tr.then_inc(qkT_in_psum.sem, 1)

                def scores(j, qt):
                    for hh in range(2):
                        n = 8 * j + 2 * qt + hh
                        pe.wait_ge(scores_read.sem, scores_read.at(i, n - 1))
                        r = slice(64 * hh, 64 * hh + 64)
                        mm = pe.matmul(ps_s[hh][:, 0:keys[qt]], qkT[r, j % 2, 0, qt * P:(qt + 1) * P],
                                       qkT[r, j % 2, 1, 0:keys[qt]], start=True, stop=not causal, skip_group_check=True)
                        if causal:
                            mm = pe.matmul(ps_s[hh][:, P * qt:P * (qt + 1)], core.identb[:, :], core.mask_qk[:, :],
                                           start=False, stop=True, skip_group_check=True)
                        mm.then_inc(scores_ready.sem, 1)

                def transposes2(j):
                    pe.wait_ge(max_ready.sem, max_ready.at(i, j + 1))
                    pe.wait_ge(qkT_ready.sem, qkT_ready.at(i, min(j + 2, PAIRS)))
                    pe.wait_ge(pvT_read.sem, pvT_read.at(i, max(0, (j - 1) // 2)))
                    for t in range(TB):
                        tr = pe.transpose(tr_b[:, t * P:(t + 1) * P], qs[:, t, j * P:(j + 1) * P], core.identb[:, :])
                    tr.then_inc(q2T_in_psum.sem, 1)

                def scoresT(j, kt):
                    n = TB * j + kt
                    pe.wait_ge(probs_ready.sem, probs_ready.at(i, n - 1))
                    for hh in range(2):
                        r = slice(64 * hh, 64 * hh + 64)
                        mm = pe.matmul(ps_t[n % 2][:, hh, 0:S - first_q[kt]], qkT[r, j % 2, 1, kt * P:(kt + 1) * P],
                                       q2T[r, j % 2, first_q[kt]:S], start=True, stop=not causal, skip_group_check=True)
                        if causal:
                            mm = pe.matmul(ps_t[n % 2][:, hh, 0:P], core.identb[:, :], core.mask_kq[:, :],
                                           start=False, stop=True, skip_group_check=True)
                    mm.then_inc(scoresT_ready.sem, 1)

                def values(j):
                    pe.wait_ge(probs_ready.sem, probs_ready.at(i, TB * (j + 1)))
                    pe.wait_ge(pv_read.sem, pv_read.at(i, j // 2))
                    if j == 0 and wo is not None:
                        pe.wait_ge(out_read.sem, out_read.at(i, 0))
                    for hh in range(2):
                        r = 32 * ((2 * j + hh) % 4)
                        for kt in range(TB):
                            mm = pe.matmul(ps_m[r:r + 32, first_q[kt]:S], v1[:, kt, 2 * j + hh, :],
                                           E[:, j % 2, hh, OFF[kt]:OFF[kt] + S - first_q[kt]], start=(kt == 0),
                                           stop=(kt == TB - 1), skip_group_check=True)
                    mm.then_inc(pv_ready.sem, 1)

                def back(g):
                    pe.wait_ge(pv_read.sem, pv_read.at(i, g + 1))
                    pe.wait_ge(q2T_ready.sem, q2T_ready.at(i, min(2 * g + 3, PAIRS)))
                    for t in range(TB):
                        tr = pe.transpose(ps_tr[:, t * P:(t + 1) * P], oT[:, t * P:(t + 1) * P], core.identf[:, :])
                    tr.then_inc(pvT_ready.sem, 1)

                transposes(0)
                pe.wait_ge(qkT_ready.sem, qkT_ready.at(i, 1))
                for qt in range(TB):
                    scores(0, qt)
                for j in range(PAIRS):
                    if j + 1 < PAIRS:
                        transposes(j + 1)
                    transposes2(j)
                    pe.wait_ge(q2T_ready.sem, q2T_ready.at(i, j + 1))
                    for x in range(TB):
                        if j + 1 < PAIRS:
                            scores(j + 1, x)
                        scoresT(j, x)
                    if j > 0 and j % 2 == 0:
                        back(j // 2 - 1)
                    values(j)
                pe.wait_ge(pvT_read.sem, pvT_read.at(i, G - 1))
                back(G - 1)
                if wo is not None:
                    pe.wait_ge(pvT_read.sem, pvT_read.at(i, G))
                    for t in range(TB):
                        tr = pe.transpose(ps_tr[:, t * P:(t + 1) * P], ao[:, t, :], core.identf[:, :])
                    tr.then_inc(attnT_in_psum.sem, 1)
                    pe.wait_ge(attnT_ready.sem, attnT_ready.at(i, 1))
                    for t in range(TB):
                        mm = pe.matmul(ps_m[:, t * P:(t + 1) * P], aoT[:, t * P:(t + 1) * P], wo[:, :], start=True, stop=True)
                    mm.then_inc(out_ready.sem, 1)

        @block.scalar
        def _(act):
            with act.Fori(0, B) as i:
                act.wait_ge(proj_in_psum.sem, proj_in_psum.at(i, 0))
                act.activation(xT[:, :], core.XNT[:, bass.ds(i * S, S)], ACT.Copy).then_inc(xT_ready.sem, 1)

                def copy_qk(j):
                    act.wait_ge(qkT_in_psum.sem, qkT_in_psum.at(i, j + 1))
                    act.wait_ge(scoresT_ready.sem, scoresT_ready.at(i, TB * (j - 1) if j >= 1 else 0))
                    act.activation(qkT[:, j % 2, :, :], tr_b.rearrange("p (a s) -> p a s", a=2), ACT.Copy).then_inc(qkT_ready.sem, 1)

                def copy_o(g):
                    act.wait_ge(pv_ready.sem, pv_ready.at(i, 2 * g + 2))
                    act.wait_ge(pvT_ready.sem, pvT_ready.at(i, g))
                    act.activation(oT, ps_m[:, :], ACT.Copy).then_inc(pv_read.sem, 1)

                copy_qk(0)
                for j in range(PAIRS):
                    if j > 0 and j % 2 == 0:
                        copy_o(j // 2 - 1)
                    if j + 1 < PAIRS:
                        copy_qk(j + 1)
                    act.wait_ge(q2T_in_psum.sem, q2T_in_psum.at(i, j + 1))
                    act.activation(q2T[:, j % 2, :], tr_b[:, 0:S], ACT.Copy).then_inc(q2T_ready.sem, 1)
                    act.wait_ge(pv_ready.sem, pv_ready.at(i, j - 1))
                    for kt in range(TB):
                        n = TB * j + kt
                        act.wait_ge(scoresT_ready.sem, scoresT_ready.at(i, n + 1))
                        act.activation(E[:, j % 2, :, OFF[kt]:OFF[kt] + S - first_q[kt]], ps_t[n % 2][:, :, 0:S - first_q[kt]],
                                       ACT.Exp, scale=scale).then_inc(probs_ready.sem, 1)
                copy_o(G - 1)
                if wo is not None:
                    act.wait_ge(attnT_in_psum.sem, attnT_in_psum.at(i, 1))
                    act.activation(aoT[:, :], ps_tr[:, :], ACT.Copy).then_inc(attnT_ready.sem, 1)

        @block.gpsimd
        def _(pool):
            pool.memset(ks[:, :, :], 0.0).then_inc(started, 1)
            pool.wait_ge(started, 1)
            pool.memset(k4[:, :, M_ROW:M_ROW + 3], 1.0).then_inc(started, 1)
            pool.memset(v1[:, :, :, HD:HD + 1], 1.0).then_inc(started, 1)
            pool.memset(v1[:, :, :, HD + 1:32], 0.0).then_inc(started, 1)
            pool.wait_ge(started, 4)
            with pool.Fori(0, B) as i:
                ch = Chain(pool_step, pool, i, core.pool_passed)
                pool.wait_ge(rotated.sem, rotated.at(i, 1))
                pool.sem_inc(core.pool_passed, 1)
                src = (rot[:, :, H:2 * H, :] if rope else qkv[:, :, D:2 * D].rearrange("p t (h d) -> p t h d", d=HD))
                ksrc = k_tmp[:, :, :].rearrange("p (t h) d -> p t h d", t=TB)
                ch.link(pool.tensor_copy(ksrc, src))
                split3(ch, pool, [[k4[:, :, r:r + HD] for r in rows] for rows in K_ROWS],
                       k_tmp[:, :, :], None, k_rest[:, :, :], k_tmp[:, :, :])
                ch.close()
                pool.memset(k_rest[:, 0, 0:1], 0.0).then_inc(k_ready.sem, 1)
                if out_norm is not None:
                    pool.wait_ge(stats_ready.sem, stats_ready.at(i, 1))
                    pool.tensor_tensor(rstd[:, :], var[:, :], core.minus_half[:, 0:TB], ALU.pow).then_inc(rstd_ready.sem, 1)

        @block.vector
        def _(dve):
            dve.memset(qs[:, :, :], 0.0).then_inc(q_cleared, 1)
            dve.wait_ge(q_cleared, 1)
            dve.wait_ge(started, 4)
            def batch(i):
                ch = Chain(dve_step, dve, i)
                dve.memset(q4[:, :, M_ROW:M_ROW + 3], 0.0)
                dve.wait_ge(proj_in_psum.sem, proj_in_psum.at(i, 1))
                dve.wait_ge(k_ready.sem, k_ready.at(i, 0))
                for t in range(TB):
                    src = ps_t[t // 2][:, t % 2, 0:3 * D]
                    if grouped:
                        for g in range(4):
                            for r in range(4):
                                dst = qkv[:, :, :].rearrange("p n (a h d) -> p a n h d", a=3, d=HD)
                                e = dve.tensor_copy(dst[32 * g:32 * g + 32, :, :, 4 * t + r, :],
                                                    src[32 * r:32 * r + 32, :].rearrange("p (a n g d) -> p a n g d", a=3, n=4, g=4)[:, :, :, g, :])
                    elif bias is not None:
                        e = dve.tensor_tensor(qkv[:, t, :], src, bias[:, :], ALU.add)
                    else:
                        e = dve.tensor_copy(qkv[:, t, :], src)
                ch.link(e)
                qk = qkv[:, :, 0:2 * D].rearrange("p t (h d) -> p t h d", d=HD)
                if rope:
                    cos = core.w["rope"][:, :, 0:1, :].broadcast_to([P, TB, 2 * H, HD])
                    sin = core.w["rope"][:, :, 1:2, :].broadcast_to([P, TB, 2 * H, HD])
                    dve.tensor_tensor(rot[:, :, :, :], qk, cos, ALU.mult)
                    dve.tensor_tensor(swapped[:, :, :, 0::2], qk[:, :, :, 1::2], sin[:, :, :, 0::2], ALU.mult)
                    ch.link(dve.tensor_tensor(swapped[:, :, :, 1::2], qk[:, :, :, 0::2], sin[:, :, :, 1::2], ALU.mult))
                    dve.tensor_tensor(rot[:, :, :, :], rot[:, :, :, :], swapped[:, :, :, :], ALU.add).then_inc(rotated.sem, 1)
                    q0 = rot[:, :, 0:H, :]
                else:
                    dve.memset(den[:, 0, :], 0.0).then_inc(rotated.sem, 1)
                    q0 = qk[:, :, 0:H, :]
                dve.wait_ge(rotated.sem, rotated.at(i, 1))
                qsrc = q_tmp[:, :, :].rearrange("p (t h) d -> p t h d", t=TB)
                ch.link(dve.tensor_copy(qsrc, q0))
                split3(ch, dve, [[q4[:, :, r:r + HD] for r in rows] for rows in Q_ROWS],
                       q_tmp[:, :, :], None, q_rest[:, :, :], q_tmp[:, :, :])
                dve.tensor_copy(v1[:, :, :, 0:HD], qkv[:, :, 2 * D:3 * D].rearrange("p t (h d) -> p t h d", d=HD)).then_inc(qv_ready.sem, 1)

                def maxima(j):
                    for qt in range(TB):
                        for hh in range(2):
                            n = 8 * j + 2 * qt + hh
                            dve.wait_ge(scores_ready.sem, scores_ready.at(i, n + 1))
                            r = dve.tensor_reduce(negm[:, qt, 2 * j + hh:2 * j + hh + 1], ps_s[hh][:, 0:keys[qt]],
                                                  AX.X, ALU.max, negate=True).then_inc(scores_read.sem, 1)
                    dve.wait_ge(scores_read.sem, scores_read.at(i, 8 * (j + 1)))
                    q5 = qs[:, :, :].rearrange("p t (h s) -> p t h s", s=SLOT)[:, :, 2 * j:2 * j + 2, :]
                    src = negm[:, :, 2 * j:2 * j + 2]
                    for n in range(3):
                        place = q5[:, :, :, M_ROW + n]
                        c = dve.tensor_copy(place, src)
                        if n == 2:
                            c.then_inc(max_ready.sem, 1)
                            break
                        ch.link(c)
                        dst = (m_rest, m_tmp)[n][:, :, :]
                        ch.link(dve.tensor_tensor(dst, src, place, ALU.subtract))
                        src = dst

                def weighted(g):
                    dve.wait_ge(pvT_ready.sem, pvT_ready.at(i, g + 1))
                    pv = ps_tr[:, :].rearrange("p (t h c) -> p t h c", t=TB, c=32)
                    ch.link(dve.tensor_scalar(den[:, :, :], pv[:, :, :, HD], eps, None, ALU.add))
                    ch.link(dve.reciprocal(rec[:, :, :], den[:, :, :]))
                    r = rec[:, :, :].rearrange("p t (h a) -> p t h a", a=1).broadcast_to([P, TB, 4, HD])
                    dve.tensor_tensor(ao[:, :, g * 32:(g + 1) * 32].rearrange("p t (h d) -> p t h d", d=HD),
                                      pv[:, :, :, 0:HD], r, ALU.mult).then_inc(pvT_read.sem, 1)

                maxima(0)
                for j in range(PAIRS):
                    if j + 1 < PAIRS:
                        maxima(j + 1)
                    if j > 0 and j % 2 == 0:
                        weighted(j // 2 - 1)
                weighted(G - 1)
                if grouped:
                    dve.wait_ge(pvT_read.sem, pvT_read.at(i, G))
                    for g in range(4):
                        for r in range(4):
                            src = ao.rearrange("p n (t r d) -> p t n r d", t=4, r=4)[32 * g:32 * g + 32, :, :, r, :]
                            dst = y.rearrange("p t (n g d) -> p t n g d", n=4, g=4)[32 * r:32 * r + 32, :, :, g, :]
                            e = dve.tensor_copy(dst, src)
                    ch.link(e)
                    xi = core.XN[:, bass.ds(i * TB, TB), :]
                    ch.link(dve.tensor_tensor(xi, xi, y, ALU.add))
                    ch.close()
                    return
                dve.wait_ge(out_ready.sem, out_ready.at(i, 1))
                y2 = y
                po = ps_m[:, :].rearrange("p (t d) -> p t d", t=TB)
                if bo is not None:
                    e = dve.tensor_tensor(y2, po, bo[:, :].rearrange("p (a d) -> p a d", a=1).broadcast_to([P, TB, D]), ALU.add)
                else:
                    e = dve.tensor_copy(y2, po)
                e.then_inc(out_read.sem, 1)
                dve.wait_ge(out_read.sem, out_read.at(i, 1))
                if out_norm is not None:
                    ch.link(dve.tensor_tensor(y2, y2, core.XN[:, bass.ds(i * TB, TB), :], ALU.add))
                    for t in range(TB):
                        e = dve.bn_stats(stats[:, t, :], y[:, t, :])
                    ch.link(e)
                    dve.memset(den[:, 0, :], 0.0)
                    for t in range(TB):
                        e = dve.bn_aggr(mv[:, t, :], stats[:, t, :])
                    ch.link(e)
                    dve.tensor_scalar(var[:, :], mv[:, :, 1], LN_EPS, None, ALU.add).then_inc(stats_ready.sem, 1)
                    dve.wait_ge(rstd_ready.sem, rstd_ready.at(i, 1))
                    for t in range(TB):
                        e = dve.tensor_scalar(y[:, t, :], y[:, t, :], mv[:, t, 0:1], rstd[:, t:t + 1], ALU.subtract, ALU.mult)
                    ch.link(e)
                    for n, op in enumerate((ALU.mult, ALU.add)):
                        ch.link(dve.tensor_tensor(y2, y2, out_norm[:, n * D:(n + 1) * D].rearrange("p (a d) -> p a d", a=1).broadcast_to([P, TB, D]), op))
                xi = core.X[:, bass.ds(i * TB, TB), :]
                ch.link(dve.tensor_tensor(xi, xi, y2, ALU.add))
                ch.close()

            with dve.Fori(0, B) as i:
                batch(i)

    core.end(B, sig)


def batch_norm_stage(core, name):
    nc = core.nc
    with ExitStack() as ctx:
        def sb(n, shape, dt=FP32):
            return ctx.enter_context(nc.sbuf_tensor(f"{name}_{n}", shape, dt))

        stats = sb("stats", [P, TB, 6])
        mv = sb("mv", [P, 2])
        both = sb("both", [P, 2])
        sq = sb("sq", [P, 1])
        mean = sb("mean", [P, 2])
        msq = sb("msq", [P, 1])
        var = sb("var", [P, 1])
        rstd = sb("rstd", [P, 1])
        average = sb("average", [P, P])
        xs = sb("xs", [P, TB, D])
        xn = sb("xn", [P, TB, D])
        ps = ctx.enter_context(nc.psum_tensor(f"{name}_ps", [P, 2], FP32))
        sig = core.begin(dve_step=12, stats_ready=1, out_ready=1, sum_ready=1, rstd_ready=1)
        dve_step, stats_ready, out_ready, sum_ready, rstd_ready = sig
        made = ctx.enter_context(nc.semaphore(f"{name}_made"))
        block = ctx.enter_context(nc.Block())

        @block.vector
        def _(dve):
            dve.memset(average[:, :], 1.0 / P).then_inc(made, 1)
            with dve.Fori(0, B) as i:
                ch = Chain(dve_step, dve, i)
                ch.link(dve.tensor_copy(xn[:, :, :], core.XN[:, bass.ds(i * TB, TB), :]))
                for t in range(TB):
                    e = dve.bn_stats(stats[:, t, :], xn[:, t, :])
                ch.link(e)
                dve.memset(sq[:, :], 0.0)
                ch.link(dve.bn_aggr(mv[:, :], stats[:, :, :].rearrange("p t s -> p (t s)")))
                dve.tensor_copy(both[:, 0:1], mv[:, 0:1])
                ch.link(dve.tensor_tensor(sq[:, :], mv[:, 0:1], mv[:, 0:1], ALU.mult))
                dve.tensor_tensor(both[:, 1:2], sq[:, :], mv[:, 1:2], ALU.add).then_inc(stats_ready.sem, 1)
                dve.wait_ge(out_ready.sem, out_ready.at(i, 1))
                ch.link(dve.tensor_copy(mean[:, :], ps[:, :]))
                ch.link(dve.tensor_tensor(msq[:, :], mean[:, 0:1], mean[:, 0:1], ALU.mult))
                ch.link(dve.tensor_tensor(var[:, :], mean[:, 1:2], msq[:, :], ALU.subtract))
                dve.tensor_scalar(var[:, :], var[:, :], LN_EPS, None, ALU.add).then_inc(sum_ready.sem, 1)
                dve.wait_ge(rstd_ready.sem, rstd_ready.at(i, 1))
                ch.link(dve.tensor_scalar(xs[:, :, :], xn[:, :, :], mean[:, 0:1], rstd[:, 0:1], ALU.subtract, ALU.mult))
                xi = core.X[:, bass.ds(i * TB, TB), :]
                ch.link(dve.tensor_tensor(xi, xi, xs[:, :, :], ALU.add))
                ch.close()

        @block.gpsimd
        def _(pool):
            with pool.Fori(0, B) as i:
                pool.wait_ge(sum_ready.sem, sum_ready.at(i, 1))
                pool.tensor_tensor(rstd[:, :], var[:, :], core.minus_half[:, 0:1], ALU.pow).then_inc(rstd_ready.sem, 1)

        @block.tensor
        def _(pe):
            pe.wait_ge(made, 1)
            with pe.Fori(0, B) as i:
                pe.wait_ge(stats_ready.sem, stats_ready.at(i, 1))
                pe.matmul(ps[:, :], average[:, :], both[:, :], start=True, stop=True).then_inc(out_ready.sem, 1)

    core.end(B, sig)


def single_head_attention_stage(core, name, w):
    nc = core.nc
    scale = 1.0 / math.sqrt(D)
    with ExitStack() as ctx:
        def sb(n, shape, dt=FP32):
            return ctx.enter_context(nc.sbuf_tensor(f"{name}_{n}", shape, dt))

        def psum(n, shape, dt=FP32):
            return ctx.enter_context(nc.psum_tensor(f"{name}_{n}", shape, dt))

        xT = sb("xT", [P, S])
        qT = sb("qT", [P, S])
        kT = sb("kT", [P, S])
        v = sb("v", [P, TB, D])
        m = sb("m", [P, TB])
        negm = sb("negm", [P, TB])
        E = sb("E", [P, TB, S])
        total = sb("total", [P, TB])
        rec = sb("rec", [P, TB])
        ET = sb("ET", [P, TB, S])
        y = sb("y", [P, TB, D])
        ps_q, ps_k, ps_v, ps_o = [psum(n, [P, S]) for n in ("ps_q", "ps_k", "ps_v", "ps_o")]
        ps_s = [psum(f"ps_s{n}", [P, S]) for n in range(2)]
        ps_e = [psum(f"ps_e{n}", [P, S]) for n in range(2)]
        sig = core.begin(dve_step=32, xT_ready=1, proj_in_psum=1, proj_read=2, qv_ready=1, scores_ready=TB, max_ready=TB,
                         probs_ready=TB, pvT_ready=TB, pvT_read=TB, out_ready=1, out_read=1)
        (dve_step, xT_ready, proj_in_psum, qk_ready, v_ready, scores_ready, max_ready, probs_ready,
         probsT_in_psum, probsT_ready, out_ready, out_read) = sig
        block = ctx.enter_context(nc.Block())

        def probabilities_back(pe, i, qt):
            pe.wait_ge(probs_ready.sem, probs_ready.at(i, qt + 1))
            pe.wait_ge(probsT_ready.sem, probsT_ready.at(i, qt - 1))
            for kt in range(qt + 1):
                tr = pe.transpose(ps_e[qt % 2][:, kt * P:(kt + 1) * P], E[:, qt, kt * P:(kt + 1) * P], core.identf[:, :])
            tr.then_inc(probsT_in_psum.sem, 1)

        @block.tensor
        def _(pe):
            with pe.Fori(0, B) as i:
                pe.wait_ge(xT_ready.sem, xT_ready.at(i, 1))
                pe.matmul(ps_q[:, :], w[:, 0:D], xT[:, :], start=True, stop=True)
                pe.matmul(ps_k[:, :], w[:, D:2 * D], xT[:, :], start=True, stop=True)
                for t in range(TB):
                    mm = pe.matmul(ps_v[:, t * D:(t + 1) * D], xT[:, t * P:(t + 1) * P], w[:, 2 * D:3 * D], start=True, stop=True)
                mm.then_inc(proj_in_psum.sem, 1)
                pe.wait_ge(qk_ready.sem, qk_ready.at(i, 2))
                for qt in range(TB):
                    pe.wait_ge(probs_ready.sem, probs_ready.at(i, qt - 1))
                    n = P * (qt + 1)
                    pe.matmul(ps_s[qt % 2][:, 0:n], qT[:, qt * P:n], kT[:, 0:n], start=True, stop=False, skip_group_check=True)
                    pe.matmul(ps_s[qt % 2][:, qt * P:n], core.identb[:, :], core.mask_qk[:, :],
                              start=False, stop=True, skip_group_check=True).then_inc(scores_ready.sem, 1)
                    if qt > 0:
                        probabilities_back(pe, i, qt - 1)
                probabilities_back(pe, i, TB - 1)
                pe.wait_ge(v_ready.sem, v_ready.at(i, 1))
                pe.wait_ge(out_read.sem, out_read.at(i, 0))
                for qt in range(TB):
                    pe.wait_ge(probsT_ready.sem, probsT_ready.at(i, qt + 1))
                    for kt in range(qt + 1):
                        mm = pe.matmul(ps_o[:, qt * D:(qt + 1) * D], ET[:, qt, kt * P:(kt + 1) * P], v[:, kt, :],
                                       start=(kt == 0), stop=(kt == qt), skip_group_check=True)
                mm.then_inc(out_ready.sem, 1)

        @block.scalar
        def _(act):
            with act.Fori(0, B) as i:
                act.wait_ge(proj_in_psum.sem, proj_in_psum.at(i, 0))
                act.activation(xT[:, :], core.XNT[:, bass.ds(i * S, S)], ACT.Copy).then_inc(xT_ready.sem, 1)
                act.wait_ge(scores_ready.sem, scores_ready.at(i, 0))
                act.wait_ge(proj_in_psum.sem, proj_in_psum.at(i, 1))
                act.activation(qT[:, :], ps_q[:, :], ACT.Copy).then_inc(qk_ready.sem, 1)
                act.activation(kT[:, :], ps_k[:, :], ACT.Copy).then_inc(qk_ready.sem, 1)
                for qt in range(TB):
                    n = P * (qt + 1)
                    act.wait_ge(max_ready.sem, max_ready.at(i, qt + 1))
                    act.wait_ge(probsT_in_psum.sem, probsT_in_psum.at(i, 0))
                    act.activation(E[:, qt, 0:n], ps_s[qt % 2][:, 0:n], ACT.Exp, bias=negm[:, qt:qt + 1], scale=scale,
                                   accum_out=total[:, qt:qt + 1]).then_inc(probs_ready.sem, 1)

        @block.vector
        def _(dve):
            with dve.Fori(0, B) as i:
                ch = Chain(dve_step, dve, i)
                dve.wait_ge(proj_in_psum.sem, proj_in_psum.at(i, 1))
                dve.tensor_copy(v[:, :, :], ps_v[:, :].rearrange("p (t d) -> p t d", t=TB)).then_inc(v_ready.sem, 1)

                def back(qt):
                    dve.wait_ge(probsT_in_psum.sem, probsT_in_psum.at(i, qt + 1))
                    n = P * (qt + 1)
                    dve.tensor_copy(ET[:, qt, 0:n], ps_e[qt % 2][:, 0:n]).then_inc(probsT_ready.sem, 1)

                for qt in range(TB):
                    dve.wait_ge(scores_ready.sem, scores_ready.at(i, qt + 1))
                    ch.link(dve.tensor_reduce(m[:, qt:qt + 1], ps_s[qt % 2][:, 0:P * (qt + 1)], AX.X, ALU.max, negate=True))
                    dve.tensor_scalar(negm[:, qt:qt + 1], m[:, qt:qt + 1], scale, None, ALU.mult).then_inc(max_ready.sem, 1)
                    if qt > 0:
                        back(qt - 1)
                back(TB - 1)
                dve.wait_ge(probs_ready.sem, probs_ready.at(i, TB))
                ch.link(dve.reciprocal(rec[:, :], total[:, :]))
                dve.wait_ge(out_ready.sem, out_ready.at(i, 1))
                r = rec[:, :].rearrange("p (t a) -> p t a", a=1).broadcast_to([P, TB, D])
                dve.tensor_tensor(y[:, :, :], ps_o[:, :].rearrange("p (t d) -> p t d", t=TB), r, ALU.mult).then_inc(out_read.sem, 1)
                dve.wait_ge(out_read.sem, out_read.at(i, 1))
                xi = core.X[:, bass.ds(i * TB, TB), :]
                ch.link(dve.tensor_tensor(xi, xi, y[:, :, :], ALU.add))
                ch.close()

    core.end(B, sig)


def linear_attention_stage(core, name, w, norm_w, head_mask, block_mask):
    nc = core.nc
    with ExitStack() as ctx:
        def sb(n, shape, dt=FP32):
            return ctx.enter_context(nc.sbuf_tensor(f"{name}_{n}", shape, dt))

        def psum(n, shape, dt=FP32):
            return ctx.enter_context(nc.psum_tensor(f"{name}_{n}", shape, dt))

        NA = 3
        xT = sb("xT", [P, S])
        k = sb("k", [P, TB, D])
        qv = sb("qv", [P, TB, 2 * D])
        sq = sb("sq", [P, TB, 2 * D])
        ms = sb("ms", [P, TB, 2 * H])
        rstd = sb("rstd", [P, TB, 2 * H])
        qT = sb("qT", [P, S])
        qTm = sb("qTm", [P, 4, S])
        state = sb("state", [P, TB - 1, D])
        A = sb("A", [P, NA, TB, P])
        y = sb("y", [P, TB, D])
        ps_p = psum("ps_p", [P, TB, 2 * D])
        ps_q = psum("ps_q", [P, S])
        ps_w = psum("ps_w", [P, TB, D])
        ps_o = psum("ps_o", [P, TB, D])
        ps_s = [psum(f"ps_s{n}", [P, TB, P]) for n in range(NA)]
        sig = core.begin(dve_step=16, xT_ready=1, proj_in_psum=1, stats_ready=1, rstd_ready=1, qv_ready=1,
                         qkT_in_psum=1, qkT_ready=5, state_ready=1, state_used=1, scores_ready=H, scores_read=H,
                         pv_ready=H, out_read=1)
        (dve_step, xT_ready, proj_in_psum, stats_ready, rstd_ready, qv_ready, qT_in_psum, qT_ready, state_in_psum,
         state_ready, scores_ready, scores_read, pv_ready, out_read) = sig
        block = ctx.enter_context(nc.Block())

        @block.tensor
        def _(pe):
            with pe.Fori(0, B) as i:
                pe.wait_ge(xT_ready.sem, xT_ready.at(i, 1))
                for t in range(TB):
                    mm = pe.matmul(ps_p[:, t, :], xT[:, t * P:(t + 1) * P], w[:, :], start=True, stop=True)
                mm.then_inc(proj_in_psum.sem, 1)
                pe.wait_ge(qv_ready.sem, qv_ready.at(i, 1))
                for t in range(TB):
                    tr = pe.transpose(ps_q[:, t * P:(t + 1) * P], qv[:, t, 0:D], core.identf[:, :])
                tr.then_inc(qT_in_psum.sem, 1)
                for t in range(1, TB):
                    for b in range(t):
                        mm = pe.matmul(ps_w[:, t - 1, :], k[:, b, :], qv[:, b, D:2 * D], start=(b == 0), stop=(b == t - 1))
                mm.then_inc(state_in_psum.sem, 1)

                def scores(h):
                    r = slice(32 * (h // 4), 32 * (h // 4) + 32)
                    pe.wait_ge(scores_read.sem, scores_read.at(i, h - NA + 1))
                    for t in range(TB):
                        mm = pe.matmul(ps_s[h % NA][:, t, :], xT[r, t * P:(t + 1) * P], qTm[r, h % 4, t * P:(t + 1) * P],
                                       start=True, stop=True)
                    mm.then_inc(scores_ready.sem, 1)

                pe.wait_ge(qT_ready.sem, qT_ready.at(i, 5))
                for h in range(NA - 1):
                    scores(h)
                pe.wait_ge(state_ready.sem, state_ready.at(i, 1))
                pe.wait_ge(out_read.sem, out_read.at(i, 0))
                for t in range(1, TB):
                    pe.matmul(ps_o[:, t, :], qT[:, t * P:(t + 1) * P], state[:, t - 1, :], start=(t == 1), stop=False, skip_group_check=True)
                for h in range(H):
                    if h + NA - 1 < H:
                        scores(h + NA - 1)
                    pe.wait_ge(scores_read.sem, scores_read.at(i, h + 1))
                    for t in range(TB):
                        mm = pe.matmul(ps_o[:, t, h * HD:(h + 1) * HD], A[:, h % NA, t, :], qv[:, t, D + h * HD:D + (h + 1) * HD],
                                       start=False, stop=(h == H - 1), skip_group_check=True)
                    mm.then_inc(pv_ready.sem, 1)

        @block.scalar
        def _(act):
            with act.Fori(0, B) as i:
                act.wait_ge(pv_ready.sem, pv_ready.at(i, 0))
                act.activation(xT[:, :], core.XNT[:, bass.ds(i * S, S)], ACT.Copy).then_inc(xT_ready.sem, 1)
                act.wait_ge(qT_in_psum.sem, qT_in_psum.at(i, 1))
                for n in range(4):
                    act.activation(qTm[:, n, :], ps_q[:, :], ACT.Copy, scale=head_mask[:, n:n + 1]).then_inc(qT_ready.sem, 1)
                act.activation(qT[:, :], ps_q[:, :], ACT.Copy).then_inc(qT_ready.sem, 1)

        @block.gpsimd
        def _(pool):
            with pool.Fori(0, B) as i:
                pool.wait_ge(stats_ready.sem, stats_ready.at(i, 1))
                pool.tensor_tensor(rstd[:, :, :], ms[:, :, :],
                                   core.minus_half[:, 0:1].rearrange("p (a b) -> p a b", a=1).broadcast_to([P, TB, 2 * H]),
                                   ALU.pow).then_inc(rstd_ready.sem, 1)

        @block.vector
        def _(dve):
            with dve.Fori(0, B) as i:
                ch = Chain(dve_step, dve, i)
                dve.tensor_copy(k[:, :, :], core.XN[:, bass.ds(i * TB, TB), :])
                dve.wait_ge(proj_in_psum.sem, proj_in_psum.at(i, 1))
                ch.link(dve.tensor_copy(qv[:, :, :], ps_p[:, :, :]))
                ch.link(dve.tensor_tensor(sq[:, :, :], qv[:, :, :], qv[:, :, :], ALU.mult))
                ch.link(dve.tensor_reduce(ms[:, :, :], sq[:, :, :].rearrange("p t (h d) -> p t h d", d=HD), AX.X, ALU.add))
                dve.tensor_scalar(ms[:, :, :], ms[:, :, :], 1.0 / HD, 1e-8, ALU.mult, ALU.add).then_inc(stats_ready.sem, 1)
                dve.wait_ge(rstd_ready.sem, rstd_ready.at(i, 1))
                qv4 = qv[:, :, :].rearrange("p t (h d) -> p t h d", d=HD)
                r4 = rstd[:, :, :].rearrange("p t (h a) -> p t h a", a=1).broadcast_to([P, TB, 2 * H, HD])
                ch.link(dve.tensor_tensor(qv4, qv4, r4, ALU.mult))
                nw = norm_w[:, :].rearrange("p (a d) -> p a d", a=1).broadcast_to([P, TB, 2 * D])
                dve.tensor_tensor(qv[:, :, :], qv[:, :, :], nw, ALU.mult).then_inc(qv_ready.sem, 1)
                dve.wait_ge(state_in_psum.sem, state_in_psum.at(i, 1))
                dve.tensor_tensor(state[:, :, :], ps_w[:, 0:TB - 1, :],
                                  block_mask.rearrange("p (a d) -> p a d", a=1).broadcast_to([P, TB - 1, D]),
                                  ALU.mult).then_inc(state_ready.sem, 1)
                keep = core.keep_kq[:, :].rearrange("p (a d) -> p a d", a=1).broadcast_to([P, TB, P])
                for h in range(H):
                    dve.wait_ge(scores_ready.sem, scores_ready.at(i, h + 1))
                    dve.wait_ge(pv_ready.sem, pv_ready.at(i, h - NA + 1))
                    dve.tensor_tensor(A[:, h % NA, :, :], ps_s[h % NA][:, :, :], keep, ALU.mult).then_inc(scores_read.sem, 1)
                dve.wait_ge(pv_ready.sem, pv_ready.at(i, H))
                dve.tensor_copy(y[:, :, :], ps_o[:, :, :]).then_inc(out_read.sem, 1)
                dve.wait_ge(out_read.sem, out_read.at(i, 1))
                xi = core.X[:, bass.ds(i * TB, TB), :]
                ch.link(dve.tensor_tensor(xi, xi, y[:, :, :], ALU.add))
                ch.close()

    core.end(B, sig)


def batch_attention_stage(core, name, w, bias, wo, bo):
    nc = core.nc
    scale = HD ** -0.5
    tri = [b * (b + 1) // 2 for b in range(B + 1)]
    with ExitStack() as ctx:
        def sb(n, shape, dt=FP32):
            return ctx.enter_context(nc.sbuf_tensor(f"{name}_{n}", shape, dt))

        def psum(n, shape, dt=FP32):
            return ctx.enter_context(nc.psum_tensor(f"{name}_{n}", shape, dt))

        xT = sb("xT", [P, B, P])
        qkv = sb("qkv", [P, B, 3 * D])
        rot = sb("rot", [P, B, 2 * H, HD])
        swapped = sb("swapped", [P, B, 2 * H, HD])
        prod = sb("prod", [P, tri[B], H, HD])
        sc = sb("sc", [P, B, H, B])
        e = sb("e", [P, B, H, B])
        top = sb("top", [P, B, H])
        total = sb("total", [P, B, H])
        att = sb("att", [P, B, D])
        attT = sb("attT", [P, B, P])
        y = sb("y", [P, B, D])
        ps_p = [psum(f"ps_p{n}", [P, 3 * D]) for n in range(4)]
        ps_t = [psum(f"ps_t{n}", [P, 4, P]) for n in range(2)]
        ps_o = [psum(f"ps_o{n}", [P, 4, D]) for n in range(2)]
        sig = core.begin(dve_step=32, xT_ready=1, proj_in_psum=B, proj_read=B, gate_ready=1, exp_ready=1,
                         attn_ready=1, attnT_in_psum=2, attnT_ready=2, out_ready=2, out_read=2)
        (dve_step, xT_ready, proj_in_psum, proj_read, scores_ready, probs_ready, attn_ready, attnT_in_psum,
         attnT_ready, out_ready, out_read) = sig
        block = ctx.enter_context(nc.Block())

        @block.tensor
        def _(pe):
            with pe.Fori(0, TB) as i:
                pe.wait_ge(xT_ready.sem, xT_ready.at(i, 1))
                for b in range(B):
                    pe.wait_ge(proj_read.sem, proj_read.at(i, b - 3))
                    pe.matmul(ps_p[b % 4][:, :], xT[:, b, :], w[:, :], start=True, stop=True).then_inc(proj_in_psum.sem, 1)
                pe.wait_ge(attn_ready.sem, attn_ready.at(i, 1))
                for n in range(2):
                    for b in range(4):
                        tr = pe.transpose(ps_t[n][:, b, :], att[:, 4 * n + b, :], core.identf[:, :])
                    tr.then_inc(attnT_in_psum.sem, 1)
                for n in range(2):
                    pe.wait_ge(attnT_ready.sem, attnT_ready.at(i, n + 1))
                    pe.wait_ge(out_read.sem, out_read.at(i, n - 1))
                    for b in range(4):
                        mm = pe.matmul(ps_o[n][:, b, :], attT[:, 4 * n + b, :], wo[:, :], start=True, stop=True)
                    mm.then_inc(out_ready.sem, 1)

        @block.scalar
        def _(act):
            with act.Fori(0, TB) as i:
                act.wait_ge(proj_in_psum.sem, proj_in_psum.at(i, 0))
                act.activation(xT[:, :, :], core.XNT[:, :].rearrange("p (b t n) -> p b t n", b=B, t=TB)[:, :, bass.ds(i, 1), :]
                               .rearrange("p b a n -> p b (a n)"), ACT.Copy).then_inc(xT_ready.sem, 1)
                act.wait_ge(scores_ready.sem, scores_ready.at(i, 1))
                act.activation(e[:, :, :, :], sc[:, :, :, :], ACT.Exp, scale=scale).then_inc(probs_ready.sem, 1)
                for n in range(2):
                    act.wait_ge(attnT_in_psum.sem, attnT_in_psum.at(i, n + 1))
                    act.wait_ge(out_ready.sem, out_ready.at(i, 0))
                    act.activation(attT[:, 4 * n:4 * n + 4, :], ps_t[n][:, :, :], ACT.Copy).then_inc(attnT_ready.sem, 1)

        @block.vector
        def _(dve):
            with dve.Fori(0, TB) as i:
                ch = Chain(dve_step, dve, i)
                dve.memset(sc[:, :, :, :], NEG)
                for b in range(B):
                    dve.wait_ge(proj_in_psum.sem, proj_in_psum.at(i, b + 1))
                    dve.tensor_tensor(qkv[:, b, :], ps_p[b % 4][:, :], bias[:, :], ALU.add).then_inc(proj_read.sem, 1)
                dve.wait_ge(proj_read.sem, proj_read.at(i, B))
                qk = qkv[:, :, 0:2 * D].rearrange("p b (h d) -> p b h d", d=HD)
                cos = core.w["rope_batch"][:, :, 0:1, :].broadcast_to([P, B, 2 * H, HD])
                sin = core.w["rope_batch"][:, :, 1:2, :].broadcast_to([P, B, 2 * H, HD])
                dve.tensor_tensor(rot[:, :, :, :], qk, cos, ALU.mult)
                dve.tensor_tensor(swapped[:, :, :, 0::2], qk[:, :, :, 1::2], sin[:, :, :, 0::2], ALU.mult)
                ch.link(dve.tensor_tensor(swapped[:, :, :, 1::2], qk[:, :, :, 0::2], sin[:, :, :, 1::2], ALU.mult))
                ch.link(dve.tensor_tensor(rot[:, :, :, :], rot[:, :, :, :], swapped[:, :, :, :], ALU.add))
                for b in range(B):
                    q = rot[:, b:b + 1, 0:H, :].broadcast_to([P, b + 1, H, HD])
                    m = dve.tensor_tensor(prod[:, tri[b]:tri[b + 1], :, :], q, rot[:, 0:b + 1, H:2 * H, :], ALU.mult)
                ch.link(m)
                for b in range(B):
                    m = dve.tensor_reduce(sc[:, b, :, :].rearrange("p h c -> p c h")[:, 0:b + 1, :],
                                          prod[:, tri[b]:tri[b + 1], :, :], AX.X, ALU.add)
                ch.link(m)
                ch.link(dve.tensor_reduce(top[:, :, :], sc[:, :, :, :], AX.X, ALU.max))
                dve.tensor_tensor(sc[:, :, :, :], sc[:, :, :, :],
                                  top[:, :, :].rearrange("p b (h a) -> p b h a", a=1).broadcast_to([P, B, H, B]),
                                  ALU.subtract).then_inc(scores_ready.sem, 1)
                dve.wait_ge(probs_ready.sem, probs_ready.at(i, 1))
                dve.tensor_reduce(total[:, :, :], e[:, :, :, :], AX.X, ALU.add)
                v4 = qkv[:, :, 2 * D:3 * D].rearrange("p b (h d) -> p b h d", d=HD)
                for b in range(B):
                    p4 = e[:, b, :, 0:b + 1].rearrange("p h (c a) -> p c h a", a=1).broadcast_to([P, b + 1, H, HD])
                    m = dve.tensor_tensor(prod[:, tri[b]:tri[b + 1], :, :], p4, v4[:, 0:b + 1, :, :], ALU.mult)
                ch.link(m)
                for b in range(B):
                    m = dve.tensor_reduce(att[:, b, :], prod[:, tri[b]:tri[b + 1], :, :].rearrange("p c h d -> p (h d) c"), AX.X, ALU.add)
                dve.reciprocal(total[:, :, :], total[:, :, :])
                ch.link(dve.memset(top[:, 0, :], 0.0))
                a4 = att[:, :, :].rearrange("p b (h d) -> p b h d", d=HD)
                dve.tensor_tensor(a4, a4, total[:, :, :].rearrange("p b (h a) -> p b h a", a=1).broadcast_to([P, B, H, HD]),
                                  ALU.mult).then_inc(attn_ready.sem, 1)
                b4 = bo[:, :].rearrange("p (a d) -> p a d", a=1).broadcast_to([P, 4, D])
                for n in range(2):
                    dve.wait_ge(out_ready.sem, out_ready.at(i, n + 1))
                    dve.tensor_tensor(y[:, 4 * n:4 * n + 4, :], ps_o[n][:, :, :], b4, ALU.add).then_inc(out_read.sem, 1)
                dve.wait_ge(out_read.sem, out_read.at(i, 2))
                xi = core.X[:, :, :].rearrange("p (b t) d -> p b t d", b=B)[:, :, bass.ds(i, 1), :].rearrange("p b a d -> p b (a d)")
                ch.link(dve.tensor_tensor(xi, xi, y[:, :, :], ALU.add))
                ch.close()

    core.end(TB, sig)


def mixer_stage(core, name, w, meanT):
    nc = core.nc
    DH, SLOTS, NR = 32, 64, 3
    RMS_EPS = 1.1920929e-07
    scale, land_scale = 1.0 / math.sqrt(DH), 1.0 / math.sqrt(D)
    with ExitStack() as ctx:
        def sb(n, shape, dt=FP32):
            return ctx.enter_context(nc.sbuf_tensor(f"{name}_{n}", shape, dt))

        def psum(n, shape, dt=FP32):
            return ctx.enter_context(nc.psum_tensor(f"{name}_{n}", shape, dt))

        xr = sb("xr", [P, TB, D])
        sq = sb("sq", [P, TB, D])
        ms = sb("ms", [P, TB])
        rstd = sb("rstd", [P, 2, TB])
        xn = sb("xn", [P, TB, D])
        xnT = sb("xnT", [P, S])
        xsum = sb("xsum", [P, 1])
        fresh = sb("fresh", [P, S])
        lam = sb("lam", [P, S])
        one_less = sb("one_less", [P, 1])
        minus_slam = sb("minus_slam", [P, 1])
        ssm = sb("ssm", [P, S])
        sum_rep = sb("sum_rep", [P, P])
        last_rep = sb("last_rep", [P, P])
        hidden = sb("hidden", [SLOTS, P])
        route = sb("route", [P, NR])
        route_e = sb("route_e", [P, NR])
        route_s = sb("route_s", [P, 4])
        land_s = sb("land_s", [P, 4])
        land_e = sb("land_e", [P, SLOTS])
        land_p = sb("land_p", [P, SLOTS])
        qT = sb("qT", [2 * DH, S])
        kT = sb("kT", [2 * DH, S])
        v = sb("v", [P, TB, DH])
        m = sb("m", [P, 2 * TB])
        negm = sb("negm", [P, 2 * TB])
        total = sb("total", [P, 2 * TB])
        rec = sb("rec", [P, 2 * TB])
        E = sb("E", [P, 4, S])
        first = sb("first", [P, 2, S])
        wt = sb("wt", [P, 2, S])
        wtT = sb("wtT", [P, TB, S])
        ctxT = sb("ctxT", [DH, S])
        mixT = sb("mixT", [P, S])
        o = sb("o", [P, TB, D])
        average = sb("average", [P, 1])
        ps_x = psum("ps_x", [P, S])
        ps_qk = psum("ps_qk", [P, S])
        ps_r = psum("ps_r", [P, S])
        ps_m = psum("ps_m", [P, S])
        ps_s = [psum(f"ps_s{n}", [P, S]) for n in range(2)]
        ps_e = [psum(f"ps_e{n}", [P, TB, P]) for n in range(2)]
        V0, R0, L0 = 0, TB * DH, TB * DH + P
        sig = core.begin(dve_step=48, stats_ready=2, rstd_ready=2, norm_ready=1, normT_in_psum=1, normT_ready=1,
                         decayed=1, repeated=1, proj_in_psum=1, proj_read=2, qv_ready=1, silu_ready=1,
                         route_in_psum=1, route_max=1, route_exp=1, route_ready=1, land_max=1, land_exp=1,
                         scores_ready=8, max_ready=8, probs_ready=8, attn_ready=TB, attnT_in_psum=TB, attnT_ready=TB,
                         pv_ready=1, pv_read=1, out_ready=1, mixed_ready=1, down_ready=1, output_ready=1, mean_in_psum=1)
        (dve_step, stats_ready, rstd_ready, norm_ready, normT_in_psum, normT_ready, decayed, repeated, proj_in_psum,
         qk_ready, v_ready, silu_ready, route_in_psum, route_max, route_exp, route_ready, land_max,
         land_exp, scores_ready, max_ready, probs_ready, attn_ready, attnT_in_psum, attnT_ready, context_in_psum,
         context_ready, slr_in_psum, mixed_ready, output_in_psum, output_ready, mean_in_psum) = sig
        started = ctx.enter_context(nc.semaphore(f"{name}_started"))
        block = ctx.enter_context(nc.Block())

        @block.tensor
        def _(pe):
            with pe.Fori(0, B) as i:
                pe.wait_ge(norm_ready.sem, norm_ready.at(i, 1))
                for t in range(TB):
                    tr = pe.transpose(ps_x[:, t * P:(t + 1) * P], xn[:, t, :], core.identf[:, :])
                tr.then_inc(normT_in_psum.sem, 1)
                pe.wait_ge(normT_ready.sem, normT_ready.at(i, 1))
                pe.matmul(ps_qk[:, :], w["l3b_qk"][:, 0:4 * DH], xnT[:, :], start=True, stop=True)
                for t in range(TB):
                    mm = pe.matmul(ps_r[:, V0 + t * DH:V0 + (t + 1) * DH], xnT[:, t * P:(t + 1) * P], w["l3b_qk"][:, 4 * DH:5 * DH],
                                   start=True, stop=True)
                pe.wait_ge(repeated.sem, repeated.at(i, 1))
                pe.matmul(ps_r[0:SLOTS, R0:R0 + P], w["l3b_r1"][:, :], sum_rep[:, :], start=True, stop=True)
                pe.matmul(ps_r[:, L0:L0 + SLOTS], last_rep[:, :], w["l3b_landT"][:, :], start=True, stop=True).then_inc(proj_in_psum.sem, 1)
                pe.wait_ge(silu_ready.sem, silu_ready.at(i, 1))
                pe.matmul(ps_m[:, 0:NR], hidden[:, :], w["l3b_r2"][0:SLOTS, :], start=True, stop=True).then_inc(route_in_psum.sem, 1)
                pe.wait_ge(qk_ready.sem, qk_ready.at(i, 2))
                pe.wait_ge(v_ready.sem, v_ready.at(i, 1))

                def back(qt):
                    pe.wait_ge(attn_ready.sem, attn_ready.at(i, qt + 1))
                    pe.wait_ge(attnT_ready.sem, attnT_ready.at(i, qt - 1))
                    for kt in range(TB):
                        tr = pe.transpose(ps_e[qt % 2][:, kt, :], wt[:, qt % 2, kt * P:(kt + 1) * P], core.identf[:, :])
                    tr.then_inc(attnT_in_psum.sem, 1)

                for qt in range(TB):
                    for a in range(2):
                        n = 2 * qt + a
                        pe.wait_ge(probs_ready.sem, probs_ready.at(i, n - 1))
                        pe.matmul(ps_s[a][:, :], qT[DH * a:DH * a + DH, qt * P:(qt + 1) * P], kT[DH * a:DH * a + DH, :],
                                  start=True, stop=True).then_inc(scores_ready.sem, 1)
                    if qt > 0:
                        back(qt - 1)
                back(TB - 1)
                pe.wait_ge(attnT_ready.sem, attnT_ready.at(i, TB))
                for kt in range(TB):
                    mm = pe.matmul(ps_qk[0:DH, :], v[:, kt, :], wtT[:, kt, :], start=(kt == 0), stop=(kt == TB - 1))
                mm.then_inc(context_in_psum.sem, 1)
                pe.wait_ge(context_ready.sem, context_ready.at(i, 1))
                pe.matmul(ps_x[:, :], w["l3b_wo"][0:DH, :], ctxT[:, :], start=True, stop=True).then_inc(slr_in_psum.sem, 1)
                pe.wait_ge(mixed_ready.sem, mixed_ready.at(i, 1))
                for t in range(TB):
                    pe.matmul(ps_e[0][:, t, :], mixT[:, t * P:(t + 1) * P], w["l3b_mix"][:, 0, :], start=True, stop=False)
                    mm = pe.matmul(ps_e[0][:, t, :], xnT[:, t * P:(t + 1) * P], w["l3b_mix"][:, 1, :], start=False, stop=True)
                mm.then_inc(output_in_psum.sem, 1)
                pe.wait_ge(output_ready.sem, output_ready.at(i, 1))
                for t in range(TB):
                    mm = pe.matmul(ps_m[:, 8:9], o[:, t, :], average[:, :], start=(t == 0), stop=(t == TB - 1))
                mm.then_inc(mean_in_psum.sem, 1)

        @block.scalar
        def _(act):
            act.wait_ge(started, 1)
            with act.Fori(0, B) as i:
                act.wait_ge(normT_in_psum.sem, normT_in_psum.at(i, 1))
                act.activation(xnT[:, :], ps_x[:, :], ACT.Copy, accum_out=xsum[:, :]).then_inc(normT_ready.sem, 1)
                act.activation(fresh[:, :], ps_x[:, :], ACT.Copy, scale=one_less[:, :]).then_inc(decayed.sem, 1)
                act.wait_ge(proj_in_psum.sem, proj_in_psum.at(i, 1))
                act.activation(qT[:, :], ps_qk[0:2 * DH, :], ACT.Copy).then_inc(qk_ready.sem, 1)
                act.activation(kT[:, :], ps_qk[2 * DH:4 * DH, :], ACT.Copy).then_inc(qk_ready.sem, 1)
                act.wait_ge(v_ready.sem, v_ready.at(i, 1))
                act.activation(hidden[:, :], ps_r[0:SLOTS, R0:R0 + P], ACT.Silu, scale=1.0 / S).then_inc(silu_ready.sem, 1)
                act.wait_ge(land_max.sem, land_max.at(i, 1))
                act.activation(land_e[:, :], land_p[:, :], ACT.Exp, bias=land_s[:, 0:1], scale=land_scale,
                               accum_out=land_s[:, 1:2]).then_inc(land_exp.sem, 1)
                act.wait_ge(route_max.sem, route_max.at(i, 1))
                act.activation(route_e[:, :], route[:, :], ACT.Exp, bias=route_s[:, 0:1],
                               accum_out=route_s[:, 1:2]).then_inc(route_exp.sem, 1)

                def copy_back(qt):
                    act.wait_ge(attnT_in_psum.sem, attnT_in_psum.at(i, qt + 1))
                    act.activation(wtT[:, :, qt * P:(qt + 1) * P], ps_e[qt % 2][:, :, :], ACT.Copy).then_inc(attnT_ready.sem, 1)

                for qt in range(TB):
                    for a in range(2):
                        n = 2 * qt + a
                        act.wait_ge(max_ready.sem, max_ready.at(i, n + 1))
                        act.wait_ge(attn_ready.sem, attn_ready.at(i, qt - 1))
                        act.activation(E[:, n % 4, :], ps_s[a][:, :], ACT.Exp, bias=negm[:, n:n + 1], scale=scale,
                                       accum_out=total[:, n:n + 1]).then_inc(probs_ready.sem, 1)
                    if qt > 0:
                        copy_back(qt - 1)
                copy_back(TB - 1)
                act.wait_ge(context_in_psum.sem, context_in_psum.at(i, 1))
                act.wait_ge(route_ready.sem, route_ready.at(i, 1))
                act.activation(ctxT[:, :], ps_qk[0:DH, :], ACT.Copy, scale=route_s[0:DH, 2:3]).then_inc(context_ready.sem, 1)

        @block.gpsimd
        def _(pool):
            with pool.Fori(0, B) as i:
                for n in range(2):
                    pool.wait_ge(stats_ready.sem, stats_ready.at(i, n + 1))
                    pool.tensor_tensor(rstd[:, n, :], ms[:, :], core.minus_half[:, 0:TB], ALU.pow).then_inc(rstd_ready.sem, 1)

        @block.vector
        def _(dve):
            dve.tensor_copy(lam[:, :], w["l3b_lam"][:, :].broadcast_to([P, S]))
            dve.tensor_scalar(one_less[:, :], w["l3b_lam"][:, :], -1.0, 1.0, ALU.mult, ALU.add)
            dve.tensor_scalar(minus_slam[:, :], w["l3b_slam"][:, :], -1.0, None, ALU.mult)
            dve.memset(average[:, :], 1.0 / S).then_inc(started, 1)
            dve.wait_ge(started, 1)

            def rms(ch, i, n, x, weight):
                ch.link(dve.tensor_tensor(sq[:, :, :], x, x, ALU.mult))
                ch.link(dve.tensor_reduce(ms[:, :], sq[:, :, :], AX.X, ALU.add))
                dve.tensor_scalar(ms[:, :], ms[:, :], 1.0 / D, RMS_EPS, ALU.mult, ALU.add).then_inc(stats_ready.sem, 1)
                dve.wait_ge(rstd_ready.sem, rstd_ready.at(i, n + 1))
                r = rstd[:, n, :].rearrange("p (t a) -> p t a", a=1).broadcast_to([P, TB, D])
                ch.link(dve.tensor_tensor(x, x, r, ALU.mult))
                return dve.tensor_tensor(x, x, weight.rearrange("p (a d) -> p a d", a=1).broadcast_to([P, TB, D]), ALU.mult)

            with dve.Fori(0, B) as i:
                ch = Chain(dve_step, dve, i)
                dve.tensor_copy(xr[:, :, :], core.XN[:, bass.ds(i * TB, TB), :])
                ch.link(dve.tensor_copy(xn[:, :, :], core.XN[:, bass.ds(i * TB, TB), :]))
                rms(ch, i, 0, xn[:, :, :], w["l3b_norm_w"][:, 0:D]).then_inc(norm_ready.sem, 1)
                dve.wait_ge(normT_ready.sem, normT_ready.at(i, 1))
                dve.tensor_copy(sum_rep[:, :], xsum[:, :].broadcast_to([P, P]))
                dve.tensor_copy(last_rep[:, :], xnT[:, S - 1:S].broadcast_to([P, P])).then_inc(repeated.sem, 1)
                dve.wait_ge(decayed.sem, decayed.at(i, 1))
                ch.link(dve.tensor_tensor_scan(ssm[:, :], lam[:, :], fresh[:, :], 0.0, ALU.mult, ALU.add))
                dve.wait_ge(proj_in_psum.sem, proj_in_psum.at(i, 1))
                ch.link(dve.tensor_copy(land_p[:, :], ps_r[:, L0:L0 + SLOTS]))
                dve.tensor_copy(v[:, :, :], ps_r[:, V0:V0 + TB * DH].rearrange("p (t d) -> p t d", t=TB)).then_inc(v_ready.sem, 1)
                ch.link(dve.tensor_reduce(land_s[:, 2:3], land_p[:, :], AX.X, ALU.max, negate=True))
                dve.tensor_scalar(land_s[:, 0:1], land_s[:, 2:3], land_scale, None, ALU.mult).then_inc(land_max.sem, 1)
                dve.wait_ge(route_in_psum.sem, route_in_psum.at(i, 1))
                ch.link(dve.tensor_tensor(route[:, :], ps_m[:, 0:NR], w["l3b_rb"][:, :], ALU.add))
                dve.tensor_reduce(route_s[:, 0:1], route[:, :], AX.X, ALU.max, negate=True).then_inc(route_max.sem, 1)
                dve.wait_ge(land_exp.sem, land_exp.at(i, 1))
                ch.link(dve.tensor_tensor(land_p[:, :], land_e[:, :], w["l3b_landT"][:, :], ALU.mult))
                dve.tensor_reduce(land_s[:, 2:3], land_p[:, :], AX.X, ALU.add)
                ch.link(dve.reciprocal(land_s[:, 3:4], land_s[:, 1:2]))
                ch.link(dve.tensor_tensor(land_s[:, 2:3], land_s[:, 2:3], land_s[:, 3:4], ALU.mult))
                dve.wait_ge(route_exp.sem, route_exp.at(i, 1))
                dve.tensor_tensor(route_s[:, 2:3], route_e[:, 1:2], route_e[:, 2:3], ALU.add)
                ch.link(dve.reciprocal(route_s[:, 3:4], route_s[:, 1:2]))
                ch.link(dve.tensor_tensor(route_s[:, 2:3], route_s[:, 2:3], route_s[:, 3:4], ALU.mult))
                dve.tensor_tensor(route_s[:, 3:4], route_e[:, 2:3], route_s[:, 3:4], ALU.mult).then_inc(route_ready.sem, 1)
                dve.wait_ge(route_ready.sem, route_ready.at(i, 1))
                ch.link(dve.tensor_tensor(land_s[:, 2:3], land_s[:, 2:3], route_s[:, 3:4], ALU.mult))

                def combined(qt):
                    dve.wait_ge(probs_ready.sem, probs_ready.at(i, 2 * qt + 2))
                    ch.link(dve.reciprocal(rec[:, 2 * qt:2 * qt + 2], total[:, 2 * qt:2 * qt + 2]))
                    dve.tensor_scalar(first[:, qt % 2, :], E[:, 2 * qt % 4, :], rec[:, 2 * qt:2 * qt + 1], None, ALU.mult)
                    ch.link(dve.tensor_tensor(rec[:, 2 * qt + 1:2 * qt + 2], rec[:, 2 * qt + 1:2 * qt + 2], minus_slam[:, :], ALU.mult))
                    dve.wait_ge(attnT_in_psum.sem, attnT_in_psum.at(i, qt - 1))
                    dve.scalar_tensor_tensor(wt[:, qt % 2, :], E[:, (2 * qt + 1) % 4, :], rec[:, 2 * qt + 1:2 * qt + 2],
                                             first[:, qt % 2, :], ALU.mult, ALU.add).then_inc(attn_ready.sem, 1)

                for qt in range(TB):
                    for a in range(2):
                        n = 2 * qt + a
                        dve.wait_ge(scores_ready.sem, scores_ready.at(i, n + 1))
                        ch.link(dve.tensor_reduce(m[:, n:n + 1], ps_s[a][:, :], AX.X, ALU.max, negate=True))
                        dve.tensor_scalar(negm[:, n:n + 1], m[:, n:n + 1], scale, None, ALU.mult).then_inc(max_ready.sem, 1)
                    if qt > 0:
                        combined(qt - 1)
                combined(TB - 1)
                dve.wait_ge(slr_in_psum.sem, slr_in_psum.at(i, 1))
                ch.link(dve.tensor_tensor(mixT[:, :], ssm[:, :], ps_x[:, :], ALU.add))
                dve.tensor_tensor(mixT[:, S - 1:S], mixT[:, S - 1:S], land_s[:, 2:3], ALU.add).then_inc(mixed_ready.sem, 1)
                dve.wait_ge(output_in_psum.sem, output_in_psum.at(i, 1))
                dve.wait_ge(mean_in_psum.sem, mean_in_psum.at(i, 0))
                ch.link(dve.tensor_copy(o[:, :, :], ps_e[0][:, :, :]))
                ch.link(rms(ch, i, 1, o[:, :, :], w["l3b_norm_w"][:, D:2 * D]))
                dve.tensor_tensor(o[:, :, :], o[:, :, :], xr[:, :, :], ALU.add).then_inc(output_ready.sem, 1)
                dve.wait_ge(output_ready.sem, output_ready.at(i, 1))
                xi = core.X[:, bass.ds(i * TB, TB), :]
                ch.link(dve.tensor_tensor(xi, xi, o[:, :, :], ALU.add))
                dve.wait_ge(mean_in_psum.sem, mean_in_psum.at(i, 1))
                ch.link(dve.tensor_copy(meanT[:, bass.ds(i, 1)], ps_m[:, 8:9]))
                ch.close()

    core.end(B, sig)


def bus_stage(core, name, w, meanT):
    nc = core.nc
    with ExitStack() as ctx:
        def sb(n, shape, dt=FP32):
            return ctx.enter_context(nc.sbuf_tensor(f"{name}_{n}", shape, dt))

        summary = sb("summary", [P, B])
        published = sb("published", [P, B, P])
        y = sb("y", [P, B, D])
        ps_c = ctx.enter_context(nc.psum_tensor(f"{name}_ps_c", [P, B], FP32))
        ps_p = ctx.enter_context(nc.psum_tensor(f"{name}_ps_p", [P, B], FP32))
        ps_y = ctx.enter_context(nc.psum_tensor(f"{name}_ps_y", [P, B, D], FP32))
        in_psum = ctx.enter_context(nc.semaphore(f"{name}_in_psum"))
        copied = ctx.enter_context(nc.semaphore(f"{name}_copied"))
        block = ctx.enter_context(nc.Block())

        @block.tensor
        def _(pe):
            pe.matmul(ps_c[:, :], w["l3b_bus"][:, 0:D], meanT[:, :], start=True, stop=True).then_inc(in_psum, 1)
            pe.wait_ge(copied, 1)
            pe.matmul(ps_p[:, :], w["l3b_bus"][:, D:2 * D], summary[:, :], start=True, stop=True).then_inc(in_psum, 1)
            pe.wait_ge(copied, 2)
            for b in range(B):
                mm = pe.matmul(ps_y[:, b, :], published[:, b, :], w["l3b_bus"][:, 2 * D:3 * D], start=True, stop=True)
            mm.then_inc(in_psum, 1)

        @block.vector
        def _(dve):
            dve.wait_ge(in_psum, 1)
            dve.tensor_copy(summary[:, :], ps_c[:, :]).then_inc(copied, 1)
            dve.wait_ge(in_psum, 2)
            dve.tensor_copy(published[:, :, :], ps_p[:, :].rearrange("p (b a) -> p b a", a=1).broadcast_to([P, B, P])).then_inc(copied, 1)
            dve.wait_ge(in_psum, 3)
            dve.tensor_scalar(y[:, :, :], ps_y[:, :, :], 0.1, None, ALU.mult).then_inc(copied, 1)
            dve.wait_ge(copied, 3)
            x = core.X[:, :, :].rearrange("p (b t) d -> p b t d", b=B)
            dve.tensor_tensor(x, x, y[:, :, :].rearrange("p b (a d) -> p b a d", a=1).broadcast_to([P, B, TB, D]),
                              ALU.add).then_inc(copied, 1)


def gates_stage(core, name, w, bias, top2, b2=None):
    nc = core.nc
    NE = 8
    with ExitStack() as ctx:
        def sb(n, shape, dt=FP32):
            return ctx.enter_context(nc.sbuf_tensor(f"{name}_{n}", shape, dt))

        xT = sb("xT", [P, S])
        logits = sb("logits", [P, TB, NE])
        top = sb("top", [P, TB, 8])
        top_u = sb("top_u", [P, TB, 8], U32)
        top_i = sb("top_i", [P, TB, 8])
        negm = sb("negm", [P, TB])
        shifted = sb("shifted", [P, TB, NE])
        e = sb("e", [P, TB, NE])
        total = sb("total", [P, TB])
        first = sb("first", [P, TB, NE])
        second = sb("second", [P, TB, NE])
        g_s = sb("g_s", [P, TB, NE])
        gT = sb("gT", [NE, S])
        ps_g = ctx.enter_context(nc.psum_tensor(f"{name}_ps_g", [P, TB, NE], FP32))
        ps_gT = ctx.enter_context(nc.psum_tensor(f"{name}_ps_gT", [NE, S], FP32))
        ps_b = ctx.enter_context(nc.psum_tensor(f"{name}_ps_b", [P, TB, D], FP32))
        biased = int(b2 is not None)
        sig = core.begin(dve_step=32, xT_ready=1, proj_in_psum=1, proj_read=1, gate_ready=1, exp_ready=int(top2),
                         attnT_in_psum=biased, attnT_ready=biased, out_ready=biased)
        dve_step, xT_ready, proj_in_psum, proj_read, gate_ready, exp_ready, gT_in_psum, gT_ready, out_ready = sig
        block = ctx.enter_context(nc.Block())

        @block.scalar
        def _(act):
            with act.Fori(0, B) as i:
                act.wait_ge(proj_in_psum.sem, proj_in_psum.at(i, 0))
                act.activation(xT[:, :], core.XNT[:, bass.ds(i * S, S)], ACT.Copy).then_inc(xT_ready.sem, 1)
                if top2:
                    act.wait_ge(gate_ready.sem, gate_ready.at(i, 1))
                    act.activation(e[:, :, :], shifted[:, :, :], ACT.Exp).then_inc(exp_ready.sem, 1)
                if b2 is not None:
                    act.wait_ge(gT_in_psum.sem, gT_in_psum.at(i, 1))
                    act.activation(gT[:, :], ps_gT[:, :], ACT.Copy).then_inc(gT_ready.sem, 1)

        @block.tensor
        def _(pe):
            with pe.Fori(0, B) as i:
                pe.wait_ge(xT_ready.sem, xT_ready.at(i, 1))
                pe.wait_ge(proj_read.sem, proj_read.at(i, 0))
                for t in range(TB):
                    mm = pe.matmul(ps_g[:, t, :], xT[:, t * P:(t + 1) * P], w[:, :], start=True, stop=True)
                mm.then_inc(proj_in_psum.sem, 1)
                if b2 is not None:
                    pe.wait_ge(gate_ready.sem, gate_ready.at(i, 1))
                    for t in range(TB):
                        tr = pe.transpose(ps_gT[:, t * P:(t + 1) * P], g_s[:, t, :], core.identf[:, :])
                    tr.then_inc(gT_in_psum.sem, 1)
                    pe.wait_ge(gT_ready.sem, gT_ready.at(i, 1))
                    for t in range(TB):
                        mm = pe.matmul(ps_b[:, t, :], gT[:, t * P:(t + 1) * P], b2[0:NE, :], start=True, stop=True)
                    mm.then_inc(out_ready.sem, 1)

        @block.vector
        def _(dve):
            with dve.Fori(0, B) as i:
                ch = Chain(dve_step, dve, i)
                dve.wait_ge(proj_in_psum.sem, proj_in_psum.at(i, 1))
                dve.tensor_tensor(logits[:, :, :], ps_g[:, :, :],
                                  bias[:, :].rearrange("p (a e) -> p a e", a=1).broadcast_to([P, TB, NE]),
                                  ALU.add).then_inc(proj_read.sem, 1)
                dve.wait_ge(proj_read.sem, proj_read.at(i, 1))
                ranked = logits
                if top2:
                    ch.link(dve.tensor_reduce(negm[:, :], logits[:, :, :], AX.X, ALU.max, negate=True))
                    dve.tensor_tensor(shifted[:, :, :], logits[:, :, :],
                                      negm[:, :].rearrange("p (t a) -> p t a", a=1).broadcast_to([P, TB, NE]),
                                      ALU.add).then_inc(gate_ready.sem, 1)
                    dve.wait_ge(exp_ready.sem, exp_ready.at(i, 1))
                    ch.link(dve.tensor_reduce(total[:, :], e[:, :, :], AX.X, ALU.add))
                    ch.link(dve.reciprocal(total[:, :], total[:, :]))
                    ch.link(dve.tensor_tensor(shifted[:, :, :], e[:, :, :],
                                              total[:, :].rearrange("p (t a) -> p t a", a=1).broadcast_to([P, TB, NE]),
                                              ALU.mult))
                    ranked = shifted
                dve.memset(negm[:, 0:1], 0.0)
                for t in range(TB):
                    m = dve.max(top[:, t, :], ranked[:, t, :])
                ch.link(m)
                dve.memset(negm[:, 0:1], 0.0)
                for t in range(TB):
                    m = dve.max_index(top_u[:, t, :], top[:, t, :], ranked[:, t, :])
                ch.link(m)
                ch.link(dve.tensor_copy(top_i[:, :, :], top_u[:, :, :]))
                if top2:
                    ch.link(dve.tensor_tensor(total[:, :], top[:, :, 0], top[:, :, 1], ALU.add))
                    ch.link(dve.tensor_scalar(total[:, :], total[:, :], 1e-6, None, ALU.add))
                    ch.link(dve.reciprocal(total[:, :], total[:, :]))
                    ch.link(dve.tensor_tensor(top[:, :, 0:2], top[:, :, 0:2],
                                              total[:, :].rearrange("p (t a) -> p t a", a=1).broadcast_to([P, TB, 2]),
                                              ALU.mult))
                    for t in range(TB):
                        dve.tensor_scalar(first[:, t, :], core.iota8[:, :], top_i[:, t, 0:1], top[:, t, 0:1], ALU.is_equal, ALU.mult)
                        m = dve.tensor_scalar(second[:, t, :], core.iota8[:, :], top_i[:, t, 1:2], top[:, t, 1:2], ALU.is_equal, ALU.mult)
                    ch.link(m)
                    ch.link(dve.tensor_tensor(core.G[:, bass.ds(i * TB, TB), :], first[:, :, :], second[:, :, :], ALU.add))
                else:
                    for t in range(TB):
                        m = dve.tensor_scalar(g_s[:, t, :], core.iota8[:, :], top_i[:, t, 0:1], None, ALU.is_equal)
                    m.then_inc(gate_ready.sem, 1)
                    dve.wait_ge(gate_ready.sem, gate_ready.at(i, 1))
                    ch.link(dve.tensor_copy(core.G[:, bass.ds(i * TB, TB), :], g_s[:, :, :]))
                    dve.wait_ge(out_ready.sem, out_ready.at(i, 1))
                    xi = core.X[:, bass.ds(i * TB, TB), :]
                    ch.link(dve.tensor_tensor(xi, xi, ps_b[:, :, :], ALU.add))
                ch.close()

    core.end(B, sig)


def experts_stage(core, name, up, down, b1=None, out_norm=False):
    nc = core.nc
    NE, NC = 8, 4
    with ExitStack() as ctx:
        def sb(n, shape, dt=FP32):
            return ctx.enter_context(nc.sbuf_tensor(f"{name}_{n}", shape, dt))

        hT = sb("hT", [P, 2, NC, S])
        acc = sb("acc", [P, TB, D])
        g = sb("g", [P, TB, NE])
        stats = sb("stats", [P, TB, 6])
        mv = sb("mv", [P, TB, 2])
        var = sb("var", [P, TB])
        rstd = sb("rstd", [P, TB])
        ps_up = [ctx.enter_context(nc.psum_tensor(f"{name}_up{n}", [P, S], FP32)) for n in range(4)]
        ps_down = [ctx.enter_context(nc.psum_tensor(f"{name}_down{n}", [P, TB, D], FP32)) for n in range(2)]
        sig = core.begin(dve_step=64, up_ready=NE * NC, act_ready=NE * NC, down_ready=NE, down_read=NE,
                         stats_ready=int(out_norm), rstd_ready=int(out_norm))
        dve_step, up_ready, act_ready, down_ready, down_read, stats_ready, rstd_ready = sig
        block = ctx.enter_context(nc.Block())

        @block.tensor
        def _(pe):
            with pe.Fori(0, B) as i:
                def up_product(e, c):
                    n = NC * e + c
                    pe.wait_ge(act_ready.sem, act_ready.at(i, n - 3))
                    pe.matmul(ps_up[n % 4][:, :], up[:, e, c * P:(c + 1) * P], core.XNT[:, bass.ds(i * S, S)],
                              start=True, stop=True).then_inc(up_ready.sem, 1)

                def down_product(e):
                    pe.wait_ge(act_ready.sem, act_ready.at(i, NC * (e + 1)))
                    pe.wait_ge(down_read.sem, down_read.at(i, e - 1))
                    for t in range(TB):
                        for c in range(NC):
                            mm = pe.matmul(ps_down[e % 2][:, t, :], hT[:, e % 2, c, t * P:(t + 1) * P], down[:, e, c, :],
                                           start=(c == 0), stop=(c == NC - 1))
                    mm.then_inc(down_ready.sem, 1)

                for c in range(NC):
                    up_product(0, c)
                for e in range(NE):
                    if e + 1 < NE:
                        for c in range(NC):
                            up_product(e + 1, c)
                    down_product(e)

        @block.scalar
        def _(act):
            with act.Fori(0, B) as i:
                for e in range(NE):
                    act.wait_ge(down_ready.sem, down_ready.at(i, e - 1))
                    for c in range(NC):
                        n = NC * e + c
                        act.wait_ge(up_ready.sem, up_ready.at(i, n + 1))
                        if b1 is not None:
                            a = act.activation(hT[:, e % 2, c, :], ps_up[n % 4][:, :], ACT.Gelu, bias=b1[:, e, c:c + 1])
                        else:
                            a = act.activation(hT[:, e % 2, c, :], ps_up[n % 4][:, :], ACT.Gelu)
                        a.then_inc(act_ready.sem, 1)

        @block.gpsimd
        def _(pool):
            if out_norm:
                with pool.Fori(0, B) as i:
                    pool.wait_ge(stats_ready.sem, stats_ready.at(i, 1))
                    pool.tensor_tensor(rstd[:, :], var[:, :], core.minus_half[:, 0:TB], ALU.pow).then_inc(rstd_ready.sem, 1)

        @block.vector
        def _(dve):
            with dve.Fori(0, B) as i:
                ch = Chain(dve_step, dve, i)
                ch.link(dve.tensor_copy(g[:, :, :], core.G[:, bass.ds(i * TB, TB), :]))
                for e in range(NE):
                    dve.wait_ge(down_ready.sem, down_ready.at(i, e + 1))
                    for t in range(TB):
                        if e == 0:
                            a = dve.tensor_scalar(acc[:, t, :], ps_down[e % 2][:, t, :], g[:, t, e:e + 1], None, ALU.mult)
                        else:
                            a = dve.scalar_tensor_tensor(acc[:, t, :], ps_down[e % 2][:, t, :], g[:, t, e:e + 1],
                                                         acc[:, t, :], ALU.mult, ALU.add)
                    a.then_inc(down_read.sem, 1)
                    dve.wait_ge(down_read.sem, down_read.at(i, e + 1))
                if out_norm:
                    for t in range(TB):
                        a = dve.bn_stats(stats[:, t, :], acc[:, t, :])
                    ch.link(a)
                    dve.memset(var[:, :], 0.0)
                    for t in range(TB):
                        a = dve.bn_aggr(mv[:, t, :], stats[:, t, :])
                    ch.link(a)
                    dve.tensor_scalar(var[:, :], mv[:, :, 1], LN_EPS, None, ALU.add).then_inc(stats_ready.sem, 1)
                    dve.wait_ge(rstd_ready.sem, rstd_ready.at(i, 1))
                    for t in range(TB):
                        a = dve.tensor_scalar(acc[:, t, :], acc[:, t, :], mv[:, t, 0:1], rstd[:, t:t + 1], ALU.subtract, ALU.mult)
                    ch.link(a)
                    ch.link(dve.tensor_tensor(acc[:, :, :], acc[:, :, :], core.XN[:, bass.ds(i * TB, TB), :], ALU.add))
                xi = core.X[:, bass.ds(i * TB, TB), :]
                ch.link(dve.tensor_tensor(xi, xi, acc[:, :, :], ALU.add))
                ch.close()

    core.end(B, sig)


def layer1_weights_stage(core):
    nc = core.nc
    n = 0
    with nc.Block() as block:
        @block.sync
        def _(sp):
            for name, over in LATER.items():
                core.w[name] = core.w[over]
                src = core.dram[name]
                sp.dma_start(core.w[name][tuple(slice(0, x) for x in src.shape)], src).then_inc(core.loads2, 16)
            sp.wait_ge(core.loads2, 16 * len(LATER))


def layer0_experts(core, name):
    norm_stage(core, name + "_norm")
    w = core.w
    gates_stage(core, name + "_gates", w["l0f_gate"], w["l0f_bias"], True)
    experts_stage(core, name, w["l0f_up"], w["l0f_down"], out_norm=True)


def layer1_experts(core, name, first):
    if first:
        layer1_weights_stage(core)
    norm_stage(core, name + "_norm")
    w = core.w
    gates_stage(core, name + "_gates", w["l1f_gate"], w["l1f_bias"], False, b2=w["l1f_b2"])
    experts_stage(core, name, w["l1f_up"], w["l1f_down"], b1=w["l1f_b1"])


BLOCK = 16
HID = 352
CHUNKS = ((0, 128), (128, 256), (256, 352))


def quantize(ch, dve, out, x, v, power, scale, inv):
    rows, blocks = scale.shape

    def wide(s):
        return s.rearrange("p (n a) -> p n a", a=1).broadcast_to([rows, blocks, BLOCK])

    ch.link(dve.tensor_reduce(scale, x, AX.X, ALU.max, apply_absolute_value=True))
    ch.link(dve.tensor_scalar(scale, scale, 1.0 / 6.0, 1e-12, ALU.mult, ALU.max))
    ch.link(dve.reciprocal(inv, scale))
    ch.link(dve.tensor_scalar(inv, inv, 1.0 - 2.0 ** -23, None, ALU.mult))
    ch.link(dve.tensor_tensor(v, x, wide(inv), ALU.mult))
    ch.link(dve.tensor_scalar(power.bitcast(U32), v.bitcast(U32), 0x7F800000, None, ALU.bitwise_and))
    ch.link(dve.tensor_scalar(power, power, 1.0, 0.75 * 2.0 ** 23, ALU.max, ALU.mult))
    ch.link(dve.tensor_tensor(v, v, power, ALU.add))
    ch.link(dve.tensor_tensor(v, v, power, ALU.subtract))
    return dve.tensor_tensor(out, v, wide(scale), ALU.mult)


def quantized_weights_stage(core, name, w_in, w_out):
    nc = core.nc
    R = 88
    w_inT, w_outT = core.w_inT, core.w_outT
    with ExitStack() as ctx:
        def sb(n, shape, dt=FP32):
            return ctx.enter_context(nc.sbuf_tensor(f"{name}_{n}", shape, dt))

        a = sb("a", [P, 64, BLOCK])
        b = sb("b", [P, 22, BLOCK])
        v = sb("v", [P, 64, BLOCK])
        power = sb("power", [P, 64, BLOCK])
        scale = sb("scale", [P, 64])
        inv = sb("inv", [P, 64])
        ps_in = [ctx.enter_context(nc.psum_tensor(f"{name}_in{n}", [P, HID], FP32)) for n in range(2)]
        ps_out = [ctx.enter_context(nc.psum_tensor(f"{name}_out{n}", [P, D], FP32)) for n in range(3)]
        sig = core.begin(dve_step=32, quant_ready=2, quantT_in_psum=1)
        dve_step, quant_ready, quantT_in_psum = sig
        block = ctx.enter_context(nc.Block())

        @block.vector
        def _(dve):
            ch = Chain(dve_step, dve, 0)
            quantize(ch, dve, a[0:R, :, :], w_in[0:R, :, :].rearrange("p t (n c) -> p (t n) c", c=BLOCK),
                     v[0:R, :, :], power[0:R, :, :], scale[0:R, :], inv[0:R, :]).then_inc(quant_ready.sem, 1)
            dve.wait_ge(quant_ready.sem, quant_ready.at(0, 1))
            quantize(ch, dve, b[:, :, :], w_out[:, :].rearrange("p (n c) -> p n c", c=BLOCK),
                     v[:, 0:22, :], power[:, 0:22, :], scale[:, 0:22], inv[:, 0:22]).then_inc(quant_ready.sem, 1)
            dve.wait_ge(quantT_in_psum.sem, quantT_in_psum.at(0, 1))
            for n in range(2):
                dve.tensor_copy(w_inT[:, n * HID:(n + 1) * HID], ps_in[n][:, :])
            for c, (lo, hi) in enumerate(CHUNKS):
                dve.tensor_copy(w_outT[0:hi - lo, c, :], ps_out[c][0:hi - lo, :])
            ch.close()

        @block.tensor
        def _(pe):
            pe.wait_ge(quant_ready.sem, quant_ready.at(0, 2))
            aw = a[:, :, :].rearrange("p (t n) c -> p t (n c)", t=8)
            for t in range(8):
                pe.transpose(ps_in[t // 4][:, (t % 4) * R:(t % 4 + 1) * R], aw[0:R, t, :], core.identf[0:R, 0:R])
            bw = b[:, :, :].rearrange("p n c -> p (n c)")
            for c, (lo, hi) in enumerate(CHUNKS):
                tr = pe.transpose(ps_out[c][0:hi - lo, :], bw[:, lo:hi], core.identf[:, :])
            tr.then_inc(quantT_in_psum.sem, 1)

    core.end(1, sig)


def quantized_ffn_stage(core, name):
    nc = core.nc
    w_inT, w_outT = core.w_inT, core.w_outT
    NX, NHB = TB * D // BLOCK, TB * HID // BLOCK
    with ExitStack() as ctx:
        def sb(n, shape, dt=FP32):
            return ctx.enter_context(nc.sbuf_tensor(f"{name}_{n}", shape, dt))

        xs = sb("xs", [P, TB, D])
        xq = sb("xq", [P, TB, D])
        xT = sb("xT", [P, S])
        v = sb("v", [P, NHB, BLOCK])
        power = sb("power", [P, NHB, BLOCK])
        scale = sb("scale", [P, NHB])
        inv = sb("inv", [P, NHB])
        sg = sb("sg", [P, TB, HID])
        h = sb("h", [P, TB, HID])
        hq = sb("hq", [P, TB, HID])
        hT = sb("hT", [P, 3, S])
        ps_x = ctx.enter_context(nc.psum_tensor(f"{name}_ps_x", [P, S], FP32))
        ps_g = [ctx.enter_context(nc.psum_tensor(f"{name}_g{n}", [P, 2, S], FP32)) for n in range(2)]
        ps_h = [ctx.enter_context(nc.psum_tensor(f"{name}_h{n}", [P, S], FP32)) for n in range(2)]
        ps_o = ctx.enter_context(nc.psum_tensor(f"{name}_o", [P, TB, D], FP32))
        sig = core.begin(dve_step=32, xq_ready=1, xqT_in_psum=1, xT_ready=1, up_ready=TB, act_ready=TB, mul_done=TB,
                         quant_ready=1, quantT_in_psum=3, quantT_ready=3, out_ready=1, out_read=1)
        (dve_step, xq_ready, xqT_in_psum, xT_ready, up_ready, act_ready, mul_done, quant_ready, quantT_in_psum,
         quantT_ready, out_ready, out_read) = sig
        block = ctx.enter_context(nc.Block())

        @block.vector
        def _(dve):
            def quantize_x(i, n, ch):
                ch.link(dve.tensor_copy(xs[:, :, :], core.XN[:, bass.ds((i + n) * TB, TB), :]))
                q = quantize(ch, dve, xq[:, :, :].rearrange("p t (n c) -> p (t n) c", c=BLOCK),
                             xs[:, :, :].rearrange("p t (n c) -> p (t n) c", c=BLOCK),
                             v[:, 0:NX, :], power[:, 0:NX, :], scale[:, 0:NX], inv[:, 0:NX])
                q.then_inc(xq_ready.sem, 1)
                dve.wait_ge(xq_ready.sem, xq_ready.at(i, n + 1))

            ch = Chain(dve_step, dve, 0)
            quantize_x(0, 0, ch)
            ch.close()

            def batch(i, ahead):
                ch = Chain(dve_step, dve, i + 1)
                for t in range(TB):
                    dve.wait_ge(act_ready.sem, act_ready.at(i, t + 1))
                    m = dve.tensor_tensor(h[:, t, :], sg[:, t, :], ps_g[t % 2][:, 1, 0:HID], ALU.mult).then_inc(mul_done.sem, 1)
                dve.wait_ge(mul_done.sem, mul_done.at(i, TB))
                quantize(ch, dve, hq[:, :, :].rearrange("p t (n c) -> p (t n) c", c=BLOCK),
                         h[:, :, :].rearrange("p t (n c) -> p (t n) c", c=BLOCK),
                         v[:, :, :], power[:, :, :], scale[:, :], inv[:, :]).then_inc(quant_ready.sem, 1)
                dve.wait_ge(quant_ready.sem, quant_ready.at(i, 1))
                if ahead:
                    quantize_x(i, 1, ch)
                dve.wait_ge(out_ready.sem, out_ready.at(i, 1))
                xi = core.X[:, bass.ds(i * TB, TB), :]
                dve.tensor_tensor(xi, xi, ps_o[:, :, :], ALU.add).then_inc(out_read.sem, 1)
                ch.close()

            with dve.Fori(0, B - 1) as i:
                batch(i, True)
            batch(B - 1, False)

        @block.tensor
        def _(pe):
            def input_products(i, n):
                pe.wait_ge(xq_ready.sem, xq_ready.at(i, n + 1))
                for t in range(TB):
                    tr = pe.transpose(ps_x[:, t * P:(t + 1) * P], xq[:, t, :], core.identf[:, :])
                tr.then_inc(xqT_in_psum.sem, 1)
                pe.wait_ge(xT_ready.sem, xT_ready.at(i, n + 1))
                for t in range(TB):
                    pe.wait_ge(mul_done.sem, mul_done.at(i, n * TB + t - 1))
                    for k in range(2):
                        mm = pe.matmul(ps_g[t % 2][:, k, 0:HID], xT[:, t * P:(t + 1) * P], w_inT[:, k * HID:(k + 1) * HID],
                                       start=True, stop=True)
                    mm.then_inc(up_ready.sem, 1)

            def batch(i, ahead):
                pe.wait_ge(quant_ready.sem, quant_ready.at(i, 1))
                for c, (lo, hi) in enumerate(CHUNKS):
                    pe.wait_ge(quantT_ready.sem, quantT_ready.at(i, c - 1))
                    for t in range(TB):
                        tr = pe.transpose(ps_h[c % 2][0:hi - lo, t * P:(t + 1) * P], hq[:, t, lo:hi], core.identf[:, :])
                    tr.then_inc(quantT_in_psum.sem, 1)
                pe.wait_ge(quantT_ready.sem, quantT_ready.at(i, 3))
                pe.wait_ge(out_read.sem, out_read.at(i, 0))
                for t in range(TB):
                    for c, (lo, hi) in enumerate(CHUNKS):
                        mm = pe.matmul(ps_o[:, t, :], hT[0:hi - lo, c, t * P:(t + 1) * P], w_outT[0:hi - lo, c, :],
                                       start=(c == 0), stop=(c == 2))
                mm.then_inc(out_ready.sem, 1)
                if ahead:
                    input_products(i, 1)

            input_products(0, 0)
            with pe.Fori(0, B - 1) as i:
                batch(i, True)
            batch(B - 1, False)

        @block.scalar
        def _(act):
            def input_activations(i, n):
                act.wait_ge(xqT_in_psum.sem, xqT_in_psum.at(i, n + 1))
                act.wait_ge(up_ready.sem, up_ready.at(i, n * TB))
                act.activation(xT[:, :], ps_x[:, :], ACT.Copy).then_inc(xT_ready.sem, 1)
                for t in range(TB):
                    act.wait_ge(up_ready.sem, up_ready.at(i, n * TB + t + 1))
                    act.wait_ge(mul_done.sem, mul_done.at(i, n * TB))
                    act.activation(sg[:, t, :], ps_g[t % 2][:, 0, 0:HID], ACT.Silu).then_inc(act_ready.sem, 1)

            def batch(i, ahead):
                for c, (lo, hi) in enumerate(CHUNKS):
                    act.wait_ge(quantT_in_psum.sem, quantT_in_psum.at(i, c + 1))
                    act.wait_ge(out_ready.sem, out_ready.at(i, 0))
                    act.activation(hT[0:hi - lo, c, :], ps_h[c % 2][0:hi - lo, :], ACT.Copy).then_inc(quantT_ready.sem, 1)
                if ahead:
                    input_activations(i, 1)

            input_activations(0, 0)
            with act.Fori(0, B - 1) as i:
                batch(i, True)
            batch(B - 1, False)

    core.end(B + 1, [dve_step])
    core.end(B, [xq_ready, xqT_in_psum, xT_ready, up_ready, act_ready, mul_done, quant_ready, quantT_in_psum, quantT_ready, out_ready, out_read])


def layer2_ffn(core, name, first):
    norm_stage(core, name + "_norm")
    if first:
        quantized_weights_stage(core, name + "_w", core.w["l2f_in"], core.w["l2f_out"])
    quantized_ffn_stage(core, name)


def layer3_ffn(core, name, first):
    norm_stage(core, name + "_norm")
    if first:
        quantized_weights_stage(core, name + "_w", core.w["l3f_in"], core.w["l3f_out"])
    quantized_ffn_stage(core, name)


def attention_program(nc, dram, out, stages):
    with ExitStack() as ctx:
        core = Core(nc, ctx)
        for name in SIGNALS:
            core.signals[name] = Signal(ctx.enter_context(nc.semaphore(name)))
        load_stage(core, dram)
        for stage in stages:
            stage(core)
        store_stage(core, out)




def layer0_attention_a(core):
    norm_stage(core, "l0a_norm")
    w = core.w
    linear_attention_stage(core, "l0a", w["l0a_w"], w["l0a_norm_w"], w["l0a_masks"][:, 0:4], w["l0a_masks"][:, 4:4 + D])


def layer0_attention_b(core):
    norm_stage(core, "l0b_norm")
    heads_attention_stage(core, "l0b", core.w["l0b_w"], rope=False, grouped=True)
    batch_norm_stage(core, "l0b_out")


def layer1_attention_a(core):
    norm_stage(core, "l1a_norm")
    w = core.w
    batch_attention_stage(core, "l1a", w["l1a_w"], w["l1a_bias"], w["l1a_wo"], w["l1a_bo"])


def layer1_attention_b(core):
    norm_stage(core, "l1b_norm")
    single_head_attention_stage(core, "l1b", core.w["l1b_w"])


def layer2_attention_a(core):
    norm_stage(core, "l2a_norm")
    w = core.w
    heads_attention_stage(core, "l2a", w["l2a_w"], w["l2a_wo"], bo=w["l2a_bo"], bias=w["l2a_bias"], eps=1e-8)


def layer2_attention_b(core):
    norm_stage(core, "l2b_norm")
    w = core.w
    heads_attention_stage(core, "l2b", w["l2b_w"], w["l2b_wo"], bo=w["l2b_bo"], rope=False, out_norm=w["l2b_gb"])


def layer3_attention_a(core):
    norm_stage(core, "l3a_norm")
    w = core.w
    heads_attention_stage(core, "l3a", w["l3a_w"], w["l3a_wo"], bo=w["l3a_bo"], bias=w["l3a_bias"])


def layer3_attention_b(core):
    norm_stage(core, "l3b_norm")
    with core.nc.sbuf_tensor("l3b_meanT", [P, B], FP32) as meanT:
        mixer_stage(core, "l3b_mixer", core.w, meanT)
        bus_stage(core, "l3b_bus", core.w, meanT)


def whole(stage, *args):
    return lambda core: stage(core, *args)


STAGES = [
    layer0_attention_a,
    whole(layer0_experts, "l0fa"),
    layer0_attention_b,
    whole(layer0_experts, "l0fb"),
    layer1_attention_a,
    whole(layer1_experts, "l1fa", True),
    layer1_attention_b,
    whole(layer1_experts, "l1fb", False),
    layer2_attention_a,
    whole(layer2_ffn, "l2fa", True),
    layer2_attention_b,
    whole(layer2_ffn, "l2fb", False),
    layer3_attention_a,
    whole(layer3_ffn, "l3fa", True),
    layer3_attention_b,
    whole(layer3_ffn, "l3fb", False),
]


def rope_table():
    pos = np.arange(S, dtype=np.float32)
    inv = (1.0 / np.float32(10000.0) ** (np.arange(0, HD, 2, dtype=np.float32) / np.float32(HD))).astype(np.float32)
    ang = (pos[:, None] * inv[None, :]).astype(np.float32)
    cos, sin = np.cos(ang), np.sin(ang)
    table = np.stack([np.repeat(cos, 2, axis=1), np.stack([-sin, sin], -1).reshape(S, HD)], 1)
    return table.astype(np.float32)


def lay_out(a):
    c = np.ascontiguousarray
    w = {}

    def put(name, x):
        w[name] = c(x)

    def row(x):
        return np.broadcast_to(c(x).reshape(1, -1), (P, x.size))

    put("X", a["L0_attn_a_X"])
    table = rope_table().reshape(TB, P, 2, HD).transpose(1, 0, 2, 3)
    put("rope", table)
    put("rope_batch", np.broadcast_to(rope_table()[None, :B], (P, B, 2, HD)))
    put("l0a_w", np.concatenate([a["L0_attn_a_Wq"].T, a["L0_attn_a_Wv"].T], 1))
    put("l0a_norm_w", row(np.stack([a["L0_attn_a_q_norm_w"], a["L0_attn_a_v_norm_w"]])))
    ch = np.arange(D)
    put("l0a_masks", np.concatenate([(ch[:, None] // HD) % 4 == np.arange(4)[None, :],
                                     ch[:, None] // HD == ch[None, :] // HD], 1).astype(np.float32))
    put("l0b_w", np.concatenate([a[f"L0_attn_b_W{n}"].T for n in "qkv"], 1))
    put("l0f_gate", a["L0_ffn_gate_w"].T)
    put("l0f_bias", row(a["L0_ffn_expert_bias"]))
    put("l0f_up", a["L0_ffn_w_up"].transpose(2, 0, 1))
    put("l0f_down", a["L0_ffn_w_down"].reshape(8, D, 4, P).transpose(3, 0, 2, 1))
    put("l1a_w", a["L1_attn_a_Wqkv"])
    put("l1a_bias", row(a["L1_attn_a_bqkv"]))
    put("l1a_wo", a["L1_attn_a_Wout"])
    put("l1a_bo", row(a["L1_attn_a_bout"]))
    put("l1b_w", np.concatenate([a[f"L1_attn_b_W{n}"] for n in "qkv"], 1))
    put("l1f_gate", a["L1_ffn_Wg"])
    put("l1f_bias", row(a["L1_ffn_bg"]))
    put("l1f_up", a["L1_ffn_W1"].transpose(1, 0, 2))
    put("l1f_b1", a["L1_ffn_b1"].reshape(8, 4, P).transpose(2, 0, 1))
    put("l1f_down", a["L1_ffn_W2"].reshape(8, 4, P, D).transpose(2, 0, 1, 3))
    put("l1f_b2", a["L1_ffn_b2"])
    put("l2a_w", np.concatenate([a[f"L2_attn_a_W{n}"].T for n in "qkv"], 1))
    put("l2a_bias", row(np.concatenate([a[f"L2_attn_a_b{n}"] for n in "qkv"])))
    put("l2a_wo", a["L2_attn_a_Wo"].T)
    put("l2a_bo", row(a["L2_attn_a_bo"]))
    put("l2b_w", a["L2_attn_b_w_qkv"])
    put("l2b_wo", a["L2_attn_b_w_proj"])
    put("l2b_bo", row(a["L2_attn_b_b_proj"]))
    put("l2b_gb", row(np.stack([a["L2_attn_b_ln_gamma"], a["L2_attn_b_ln_beta"]])))
    for n in "23":
        put(f"l{n}f_in", np.concatenate([a[f"L{n}_ffn_w_gate"], a[f"L{n}_ffn_w_up"]], 0)
            .reshape(8, 88, D).transpose(1, 0, 2))
        put(f"l{n}f_out", a[f"L{n}_ffn_w_down"])
    put("l3a_w", a["L3_attn_a_qkv_w"].T)
    put("l3a_bias", row(a["L3_attn_a_qkv_b"]))
    put("l3a_wo", a["L3_attn_a_proj_w"].T)
    put("l3a_bo", row(a["L3_attn_a_proj_b"]))
    put("l3b_norm_w", row(np.stack([a["L3_attn_b_w_norm_in"], a["L3_attn_b_w_norm_out"]])))
    put("l3b_r1", a["L3_attn_b_router_w1"])
    put("l3b_r2", a["L3_attn_b_router_w2"])
    put("l3b_rb", row(a["L3_attn_b_router_b2"]))
    put("l3b_lam", np.repeat(a["L3_attn_b_lambdas"], D // 8).reshape(D, 1))
    put("l3b_qk", np.concatenate([a[f"L3_attn_b_slr_w{n}"] for n in ("q1", "q2", "k1", "k2", "v")], 1))
    put("l3b_wo", a["L3_attn_b_slr_wo"])
    put("l3b_slam", row(a["L3_attn_b_slr_lam"].reshape(1)))
    put("l3b_landT", a["L3_attn_b_landmarks"].T)
    put("l3b_mix", a["L3_attn_b_mix_w"].reshape(2, D, D).transpose(1, 0, 2))
    put("l3b_bus", np.concatenate([a[f"L3_attn_b_bus_{n}"] for n in ("compress", "publish", "expand")], 1))
    return w


def kernel(**inputs):
    import concourse.bacc as bacc
    from concourse.bass_utils import run_bass_kernel_spmd

    nc = bacc.Bacc("TRN2", target_bir_lowering=False, num_devices=1)
    arrays, dram = {}, {}
    for name, x in lay_out({k: np.asarray(v) for k, v in inputs.items()}).items():
        arrays[f"in_{name}"] = x
        dram[name] = nc.dram_tensor(f"in_{name}", x.shape, FP32, kind="ExternalInput").ap()
    out = nc.dram_tensor("out_0", (B, S, D), FP32, kind="ExternalOutput").ap()
    attention_program(nc, dram, out, STAGES)
    got = run_bass_kernel_spmd(nc, [arrays], core_ids=[0])
    return got.results[0]["out_0"]
```

```python
import math
from contextlib import ExitStack

import numpy as np

import concourse.bass as bass
from concourse import mybir

FP32 = mybir.dt.float32
BF16 = mybir.dt.bfloat16
I32 = mybir.dt.int32
U32 = mybir.dt.uint32
ALU = mybir.AluOpType
ACT = mybir.ActivationFunctionType
AX = mybir.AxisListType

B, S, D = 8, 512, 128
P = 128
NT = B * S // P
TB = S // P
H, HD = 16, 8
PAIRS = H // 2
SLOT = 64
NEG = -1.0e30
LN_EPS = 1e-5
PRIME = 8


class Batch:

    def __init__(self, r, step, plus):
        self.r, self.step, self.plus = r, step, plus

    def times(self, n, more=0):
        if self.r is None:
            return self.plus * n + more
        return self.r * (self.step * n) + (self.plus * n + more)


class Signal:

    def __init__(self, sem):
        self.sem, self.base, self.per = sem, PRIME, 0

    def begin(self, per):
        self.per = per

    def at(self, i, k):
        if isinstance(i, Batch):
            return i.times(self.per, self.base + k)
        return i * self.per + (self.base + k)

    def end(self, rounds):
        self.base += rounds * self.per


class Chain:

    def __init__(self, signal, eng, i, passed=None):
        self.s, self.eng, self.i, self.k, self.passed = signal, eng, i, 0, passed

    def link(self, ins):
        self.k += 1
        ins.then_inc(self.s.sem, 1)
        self.eng.wait_ge(self.s.sem, self.s.at(self.i, self.k))
        if self.passed is not None:
            self.eng.sem_inc(self.passed, 1)

    def close(self):
        assert self.k <= self.s.per, (self.k, self.s.per)
        if self.s.per > self.k:
            self.eng.sem_inc(self.s.sem, self.s.per - self.k)


class Core:

    def __init__(self, nc, ctx):
        self.nc, self.ctx = nc, ctx
        self.signals = {}
        self.banks = [ctx.enter_context(nc.psum_tensor(f"bank{n}", [P, 512], FP32)) for n in range(0)]

    def sb(self, name, shape, dt=FP32):
        return self.ctx.enter_context(self.nc.sbuf_tensor(name, shape, dt))

    def begin(self, **per):
        out = []
        for name, n in per.items():
            s = self.signals[name]
            s.begin(n)
            out.append(s)
        return out

    def end(self, rounds, signals):
        for s in signals:
            s.end(rounds)


SIGNALS = [
    "dve_step", "act_step", "pool_step", "stats_ready", "rstd_ready", "norm_ready", "normT_in_psum",
    "normT_ready", "xT_ready", "proj_in_psum", "proj_read", "rotated", "k_ready", "qv_ready",
    "qkT_in_psum", "qkT_ready", "scores_ready", "scores_read", "max_ready", "q2T_in_psum", "q2T_ready",
    "scoresT_ready", "probs_ready", "pv_ready", "pv_read", "pvT_ready", "pvT_read", "attn_ready", "attnT_in_psum",
    "attnT_ready", "out_ready", "out_read", "up_ready", "act_ready", "down_ready", "down_read",
    "gate_ready", "exp_ready", "quant_ready", "quantT_in_psum", "quantT_ready", "state_ready",
    "state_used", "sum_ready", "pool_ready", "xq_ready", "xqT_in_psum", "mul_done",
    "decayed", "repeated", "silu_ready", "route_in_psum", "route_max", "route_exp", "route_ready",
    "land_max", "land_exp", "mixed_ready", "output_ready", "mean_in_psum",
]


def token_view(ap):
    return ap.rearrange("b (t p) d -> p (b t) d", p=P)


LATER = {"l0f_up": "room_up", "l0f_down": "room_down", "l1f_up": "room_up", "l1f_down": "room_down"}


def load_stage(core, dram):
    nc = core.nc
    core.pool_passed = core.ctx.enter_context(nc.semaphore("pool_passed"))
    core.w = {}
    core.X = core.sb("X", [P, NT, D])
    core.XN = core.sb("XN", [P, NT, D])
    core.XNT = core.sb("XNT", [P, NT * P])
    core.identf = core.sb("identf", [P, P])
    core.identb = core.sb("identb", [P, P], BF16)
    core.mask_qk = core.sb("mask_qk", [P, P], BF16)
    core.mask_kq = core.sb("mask_kq", [P, P], BF16)
    core.keep_kq = core.sb("keep_kq", [P, P])
    core.ones = core.sb("ones", [P, P])
    core.iota8 = core.sb("iota8", [P, 8])
    core.minus_half = core.sb("minus_half", [P, 8])
    core.w_inT = core.sb("w_inT", [P, 2 * HID])
    core.w_outT = core.sb("w_outT", [P, 3, D])
    core.G = core.sb("G", [P, NT, 8])
    core.room_up = core.sb("room_up", [P, 8, S])
    core.room_down = core.sb("room_down", [P, 8, TB, D])
    core.loads2 = core.ctx.enter_context(nc.semaphore("weights2_loaded"))
    core.work_base = None
    made = core.ctx.enter_context(nc.semaphore("constants_made"))
    done = core.ctx.enter_context(nc.semaphore("x_loaded"))
    core.loads = core.ctx.enter_context(nc.semaphore("weights_loaded"))

    core.dram, core.loads2_count = dram, 0
    dram_now = {name: src for name, src in dram.items() if name not in LATER}
    core.loads_pending = 16 * (len(dram_now) - 1)
    for name, src in dram_now.items():
        if name != "X":
            core.w[name] = core.sb(name, [P if n == 0 else x for n, x in enumerate(src.shape)])

    with nc.Block() as block:
        @block.sync
        def _(sp):
            sp.dma_start(core.X[:, :, :], token_view(dram["X"])).then_inc(done, 16)
            for name, src in dram_now.items():
                if name != "X":
                    dst = core.w[name][tuple(slice(0, x) for x in src.shape)]
                    sp.dma_start(dst, src).then_inc(core.loads, 16)
            sp.wait_ge(done, 16)

        @block.vector
        def _(dve):
            for s in core.signals.values():
                dve.sem_inc(s.sem, PRIME)

        @block.gpsimd
        def _(pool):
            pool.memset(core.identf[:, :], 0.0).then_inc(made, 1)
            pool.memset(core.identb[:, :], 0.0).then_inc(made, 1)
            pool.memset(core.mask_qk[:, :], 0.0).then_inc(made, 1)
            pool.memset(core.mask_kq[:, :], 0.0).then_inc(made, 1)
            pool.memset(core.keep_kq[:, :], 1.0).then_inc(made, 1)
            pool.memset(core.ones[:, :], 1.0).then_inc(made, 1)
            pool.memset(core.minus_half[:, :], -0.5).then_inc(made, 1)
            pool.iota(core.iota8[:, :], [[1, 8]], base=0, channel_multiplier=0,
                      allow_small_or_imprecise_dtypes=True).then_inc(made, 1)
            pool.wait_ge(made, 8)
            for m in (core.identf, core.identb):
                pool.affine_select(out=m[:, :], in_=m[:, :], compare_op=ALU.not_equal, fill=1.0,
                                   base=0, pattern=[[-1, P]], channel_multiplier=1).then_inc(made, 1)
            pool.affine_select(out=core.mask_qk[:, :], in_=core.mask_qk[:, :], compare_op=ALU.is_ge,
                               fill=NEG, base=0, pattern=[[-1, P]], channel_multiplier=1).then_inc(made, 1)
            for m, fill in ((core.mask_kq, NEG), (core.keep_kq, 0.0)):
                pool.affine_select(out=m[:, :], in_=m[:, :], compare_op=ALU.is_ge,
                                   fill=fill, base=0, pattern=[[1, P]], channel_multiplier=-1).then_inc(made, 1)
            pool.wait_ge(made, 13)


def store_stage(core, out):
    nc = core.nc
    stored = core.ctx.enter_context(nc.semaphore("stored"))
    with nc.Block() as block:
        @block.sync
        def _(sp):
            sp.dma_start(token_view(out), core.X[:, :, :]).then_inc(stored, 16)
            sp.wait_ge(stored, 16)


def norm_stage(core, name):
    nc = core.nc
    with ExitStack() as ctx:
        stats = ctx.enter_context(nc.sbuf_tensor(f"{name}_stats", [P, TB, 6], FP32))
        mv = ctx.enter_context(nc.sbuf_tensor(f"{name}_mv", [P, 2, TB, 2], FP32))
        var = ctx.enter_context(nc.sbuf_tensor(f"{name}_var", [P, TB], FP32))
        rstd = ctx.enter_context(nc.sbuf_tensor(f"{name}_rstd", [P, TB], FP32))
        xs = ctx.enter_context(nc.sbuf_tensor(f"{name}_xs", [P, 2, TB, D], FP32))
        ps = ctx.enter_context(nc.psum_tensor(f"{name}_ps", [P, 2, S], FP32))
        R = B // 2
        sig = core.begin(dve_step=16, stats_ready=2, rstd_ready=2, norm_ready=2, normT_in_psum=2,
                         normT_ready=2)
        dve_step, stats_ready, rstd_ready, norm_ready, normT_in_psum, normT_ready = sig
        block = ctx.enter_context(nc.Block())

        if core.loads_pending:
            pending, core.loads_pending = core.loads_pending, 0

            @block.sync
            def _(sp):
                sp.wait_ge(core.loads, pending)

        @block.vector
        def _(dve):
            with dve.Fori(0, R) as i:
                ch = Chain(dve_step, dve, i)
                for u in range(2):
                    for t in range(TB):
                        st = dve.bn_stats(stats[:, t, :], core.X[:, bass.ds(i * (2 * TB) + u * TB + t, 1), :])
                    ch.link(st)
                    dve.memset(var[:, 0:1], 0.0)
                    for t in range(TB):
                        ag = dve.bn_aggr(mv[:, u, t, :], stats[:, t, :])
                    ch.link(ag)
                    dve.tensor_scalar(var[:, :], mv[:, u, :, 1], LN_EPS, None, ALU.add).then_inc(stats_ready.sem, 1)
                    dve.wait_ge(rstd_ready.sem, rstd_ready.at(i, u + 1))
                    dve.wait_ge(normT_in_psum.sem, normT_in_psum.at(i, u - 1))
                    for t in range(TB):
                        a = dve.tensor_scalar(xs[:, u, t, :], core.X[:, bass.ds(i * (2 * TB) + u * TB + t, 1), :],
                                              mv[:, u, t, 0:1], rstd[:, t:t + 1], ALU.subtract, ALU.mult)
                    a.then_inc(norm_ready.sem, 1)
                    dve.wait_ge(norm_ready.sem, norm_ready.at(i, u + 1))
                    dve.tensor_copy(core.XN[:, bass.ds(i * (2 * TB) + u * TB, TB), :], xs[:, u, :, :])
                ch.close()

        @block.gpsimd
        def _(pool):
            with pool.Fori(0, R) as i:
                for u in range(2):
                    pool.wait_ge(stats_ready.sem, stats_ready.at(i, u + 1))
                    pool.tensor_tensor(rstd[:, :], var[:, :], core.minus_half[:, 0:TB], ALU.pow).then_inc(rstd_ready.sem, 1)

        @block.tensor
        def _(pe):
            with pe.Fori(0, R) as i:
                for u in range(2):
                    pe.wait_ge(norm_ready.sem, norm_ready.at(i, u + 1))
                    pe.wait_ge(normT_ready.sem, normT_ready.at(i, u - 1))
                    for t in range(TB):
                        tr = pe.transpose(ps[:, u, t * P:(t + 1) * P], xs[:, u, t, :], core.identf[:, :])
                    tr.then_inc(normT_in_psum.sem, 1)

        @block.scalar
        def _(act):
            with act.Fori(0, R) as i:
                for u in range(2):
                    act.wait_ge(normT_in_psum.sem, normT_in_psum.at(i, u + 1))
                    act.activation(core.XNT[:, bass.ds(i * (2 * S) + u * S, S)], ps[:, u, :], ACT.Copy).then_inc(normT_ready.sem, 1)

    core.end(R, sig)


def split3(ch, eng, out_parts, x, rest, tmp):
    src = x
    for n, places in enumerate(out_parts):
        ch.link(eng.tensor_copy(places[0], src))
        for place in places[1:]:
            eng.tensor_copy(place, places[0])
        if n < 2:
            dst = rest if n == 0 else tmp
            ch.link(eng.tensor_tensor(dst, src, places[0], ALU.subtract))
            src = dst


Q_ROWS = ((0, 8, 24), (16, 48), (40,))
K_ROWS = ((0, 16, 40), (8, 48), (24,))
M_ROW = 32


def heads_attention_stage(core, name, w, wo=None, bo=None, bias=None, rope=True, eps=0.0, out_norm=None,
                          grouped=False):
    nc = core.nc
    scale = 1.0 if grouped else 1.0 / math.sqrt(HD)
    causal = not grouped
    first_q = [P * k if causal else 0 for k in range(TB)]
    keys = [P * (q + 1) if causal else S for q in range(TB)]
    OFF = [sum(S - n for n in first_q[:k]) for k in range(TB)]
    NE = sum(S - n for n in first_q)
    VW = HD + 1
    VROW = H * VW + 32 - VW
    G = H // 4
    projected, normed = int(wo is not None), int(out_norm is not None)
    with ExitStack() as ctx:
        def sb(n, shape, dt=FP32):
            return ctx.enter_context(nc.sbuf_tensor(f"{name}_{n}", shape, dt))

        def psum(n, shape, dt=FP32):
            return ctx.enter_context(nc.psum_tensor(f"{name}_{n}", shape, dt))

        xT = sb("xT", [P, S])
        qkv = sb("qkv", [P, TB, 3 * D])
        if rope:
            rot = sb("rot", [P, TB, 2 * H, HD])
            swapped = sb("swapped", [P, TB, 2 * H, HD])
        q_rest = sb("q_rest", [P, TB * H, HD])
        q_tmp = sb("q_tmp", [P, TB * H, HD])
        k_rest = sb("k_rest", [P, TB * H, HD])
        k_tmp = sb("k_tmp", [P, TB * H, HD])
        room = [core.room_up[:, :, :].rearrange("p a b -> p (a b)").bitcast(BF16),
                core.room_down[:, :, :, :].rearrange("p a b c -> p (a b c)").bitcast(BF16)]
        qs, ks = [[part[:, u * TB * H * SLOT:(u + 1) * TB * H * SLOT].rearrange("p (t n) -> p t n", t=TB) for u in range(2)]
                  for part in room]
        v_row = [sb(f"v1_{u}", [P, TB, VROW]) for u in range(2)]
        v1 = [x[:, :, 0:H * VW].rearrange("p t (h c) -> p t h c", c=VW) for x in v_row]
        qkT = sb("qkT", [P, 2, 2, S], BF16)
        q2T = sb("q2T", [P, 2, S], BF16)
        E = sb("E", [P, 2, 2, NE])
        negm = sb("negm", [P, TB, H])
        m_rest = sb("m_rest", [P, TB, 2])
        m_tmp = sb("m_tmp", [P, TB, 2])
        oT = sb("oT", [P, S])
        den = sb("den", [P, TB, 4])
        rec = sb("rec", [P, TB, 4])
        ao = sb("ao", [P, TB, D])
        y = sb("y", [P, TB, D])
        if projected:
            aoT = sb("aoT", [P, S])
        if normed:
            stats = sb("stats", [P, TB, 6])
            mv = sb("mv", [P, TB, 2])
            var = sb("var", [P, TB])
            rstd = sb("rstd", [P, TB])
        ps_s = [psum(f"ps_s{n}", [P, S]) for n in range(2)]
        ps_t = [psum(f"ps_t{n}", [P, 2, S]) for n in range(2)]
        ps_tr = psum("ps_tr", [P, S])
        ps_m = psum("ps_m", [P, S])
        tr_b = ps_tr[:, :].bitcast(BF16)
        q4 = [x.rearrange("p t (h s) -> p (t h) s", s=SLOT) for x in qs]
        k4 = [x.rearrange("p t (h s) -> p (t h) s", s=SLOT) for x in ks]

        sig = core.begin(xT_ready=1, proj_in_psum=TB, proj_read=TB, rotated=1, k_ready=1, qv_ready=1,
                         qkT_in_psum=PAIRS, qkT_ready=PAIRS, q2T_in_psum=PAIRS, q2T_ready=PAIRS,
                         scores_ready=8 * PAIRS, scores_read=8 * PAIRS, max_ready=PAIRS,
                         scoresT_ready=TB * PAIRS, probs_ready=TB * PAIRS, pv_ready=PAIRS, pv_read=G, pvT_ready=G, pvT_read=G,
                         attnT_in_psum=projected, attnT_ready=projected, out_ready=projected, out_read=projected,
                         stats_ready=normed, rstd_ready=normed)
        (xT_ready, proj_in_psum, proj_read, rotated, k_ready, qv_ready, qkT_in_psum, qkT_ready,
         q2T_in_psum, q2T_ready, scores_ready, scores_read, max_ready, scoresT_ready, probs_ready,
         pv_ready, pv_read, pvT_ready, pvT_read, attnT_in_psum, attnT_ready, out_ready, out_read, stats_ready, rstd_ready) = sig
        (dve_step, pool_step) = own = core.begin(dve_step=128, pool_step=16)
        started = ctx.enter_context(nc.semaphore(f"{name}_started"))
        q_cleared = ctx.enter_context(nc.semaphore(f"{name}_q_cleared"))
        block = ctx.enter_context(nc.Block())

        def all_batches(eng, start, batch, finish):
            start()
            batch(Batch(None, 0, 0), 0, False, True)
            with eng.Fori(0, (B - 2) // 2) as r:
                for k in (1, 2):
                    batch(Batch(r, 2, k), k % 2, True, True)
            batch(Batch(None, 0, B - 1), (B - 1) % 2, True, False)
            finish()

        @block.tensor
        def _(pe):
            def projection(i, t):
                pe.wait_ge(xT_ready.sem, xT_ready.at(i, 2))
                pe.matmul(ps_tr[:, 0:3 * D], xT[:, t * P:(t + 1) * P], w[:, :],
                          start=True, stop=True).then_inc(proj_in_psum.sem, 1)

            def transposes(i, j, u):
                if j % PAIRS == 0:
                    pe.wait_ge(qv_ready.sem, qv_ready.at(i, j // PAIRS + 1))
                    pe.wait_ge(k_ready.sem, k_ready.at(i, j // PAIRS + 1))
                c = j % PAIRS
                for n, src in enumerate((qs[u], ks[u])):
                    for t in range(TB):
                        tr = pe.transpose(tr_b[:, n * S + t * P:n * S + (t + 1) * P],
                                          src[:, t, c * P:(c + 1) * P], core.identb[:, :])
                tr.then_inc(qkT_in_psum.sem, 1)

            def transposes2(i, j, u):
                pe.wait_ge(max_ready.sem, max_ready.at(i, j + 1))
                for t in range(TB):
                    tr = pe.transpose(tr_b[:, t * P:(t + 1) * P], qs[u][:, t, j * P:(j + 1) * P], core.identb[:, :])
                tr.then_inc(q2T_in_psum.sem, 1)

            def scores(i, j, x):
                qt = TB - 1 - x
                for hh in range(2):
                    n = 8 * j + 2 * x + hh
                    pe.wait_ge(scores_read.sem, scores_read.at(i, n - 1))
                    r = slice(64 * hh, 64 * hh + 64)
                    mm = pe.matmul(ps_s[hh][:, 0:keys[qt]], qkT[r, j % 2, 0, qt * P:(qt + 1) * P],
                                   qkT[r, j % 2, 1, 0:keys[qt]], start=True, stop=not causal, skip_group_check=True)
                    if causal:
                        mm = pe.matmul(ps_s[hh][:, P * qt:P * (qt + 1)], core.identb[:, :], core.mask_qk[:, :],
                                       start=False, stop=True, skip_group_check=True)
                    mm.then_inc(scores_ready.sem, 1)

            def scoresT(i, j, kt):
                n = TB * j + kt
                pe.wait_ge(probs_ready.sem, probs_ready.at(i, n - 1))
                for hh in range(2):
                    r = slice(64 * hh, 64 * hh + 64)
                    mm = pe.matmul(ps_t[n % 2][:, hh, 0:S - first_q[kt]], qkT[r, j % 2, 1, kt * P:(kt + 1) * P],
                                   q2T[r, j % 2, first_q[kt]:S], start=True, stop=not causal, skip_group_check=True)
                    if causal:
                        mm = pe.matmul(ps_t[n % 2][:, hh, 0:P], core.identb[:, :], core.mask_kq[:, :],
                                       start=False, stop=True, skip_group_check=True)
                mm.then_inc(scoresT_ready.sem, 1)

            def values(i, j, u, hh):
                c = j % PAIRS
                if hh == 0:
                    pe.wait_ge(probs_ready.sem, probs_ready.at(i, TB * (j + 1)))
                    if c % 2 == 0:
                        pe.wait_ge(pv_read.sem, pv_read.at(i, c // 2))
                r = 32 * ((2 * c + hh) % 4)
                col = (2 * c + hh) * VW
                for kt in range(TB):
                    mm = pe.matmul(ps_m[r:r + 32, first_q[kt]:S], v_row[u][:, kt, col:col + 32],
                                   E[:, c % 2, hh, OFF[kt]:OFF[kt] + S - first_q[kt]], start=(kt == 0),
                                   stop=(kt == TB - 1), skip_group_check=True)
                if hh == 1:
                    mm.then_inc(pv_ready.sem, 1)

            def back(i, g):
                pe.wait_ge(pv_read.sem, pv_read.at(i, g + 1))
                for t in range(TB):
                    tr = pe.transpose(ps_tr[:, t * P:(t + 1) * P], oT[:, t * P:(t + 1) * P], core.identf[:, :])
                tr.then_inc(pvT_ready.sem, 1)

            def output_back(i, n):
                pe.wait_ge(pvT_read.sem, pvT_read.at(i, G * n))
                for t in range(TB):
                    tr = pe.transpose(ps_tr[:, t * P:(t + 1) * P], ao[:, t, :], core.identf[:, :])
                tr.then_inc(attnT_in_psum.sem, 1)

            def output_projection(i, n):
                pe.wait_ge(attnT_ready.sem, attnT_ready.at(i, n))
                for t in range(TB):
                    mm = pe.matmul(ps_tr[:, t * P:(t + 1) * P], aoT[:, t * P:(t + 1) * P], wo[:, :], start=True, stop=True)
                mm.then_inc(out_ready.sem, 1)

            def start():
                before = Batch(None, 0, -1)
                for t in range(TB):
                    projection(before, t)
                    pe.wait_ge(proj_read.sem, proj_read.at(0, t + 1))
                transposes(Batch(None, 0, 0), 0, 0)
                pe.wait_ge(qkT_ready.sem, qkT_ready.at(0, 1))
                for qt in range(TB):
                    scores(Batch(None, 0, 0), 0, qt)

            def batch(i, u, behind, ahead):
                for j in range(PAIRS):
                    more = j + 1 < PAIRS or ahead
                    if j == 0 and behind:
                        pe.wait_ge(pvT_read.sem, pvT_read.at(i, -1))
                    if j in (1, 2) and ahead:
                        pe.wait_ge(proj_read.sem, proj_read.at(i, TB + 1 + j))
                    if j == 2 and behind:
                        pe.wait_ge(pvT_read.sem, pvT_read.at(i, 0))
                    if j == 3 and ahead:
                        pe.wait_ge(proj_read.sem, proj_read.at(i, 2 * TB))
                    if j == 3 and behind and projected:
                        pe.wait_ge(attnT_ready.sem, attnT_ready.at(i, 0))
                    if j == 4 and behind and projected:
                        pe.wait_ge(out_read.sem, out_read.at(i, 0))
                    if j >= 4 and j % 2 == 0:
                        pe.wait_ge(pvT_read.sem, pvT_read.at(i, j // 2 - 1))
                    if more:
                        transposes(i, j + 1, u if j + 1 < PAIRS else 1 - u)
                    if j > 0 or behind:
                        values(i, j - 1, u if j > 0 else 1 - u, 0)
                    if more:
                        pe.wait_ge(qkT_ready.sem, qkT_ready.at(i, j + 2))
                    transposes2(i, j, u)
                    if j > 0 or behind:
                        values(i, j - 1, u if j > 0 else 1 - u, 1)
                    pe.wait_ge(q2T_ready.sem, q2T_ready.at(i, j + 1))
                    for x in range(TB):
                        if more:
                            scores(i, j + 1, x)
                        scoresT(i, j, x)
                        if x == 1:
                            if j == 0 and ahead:
                                projection(i, 0)
                            if j == 2 and ahead:
                                projection(i, 3)
                            if j % 2 == 1 and (j > 1 or behind):
                                back(i, (j - 3) // 2)
                        if x == 3:
                            if j == 0 and ahead:
                                pe.wait_ge(proj_read.sem, proj_read.at(i, TB + 1))
                                projection(i, 1)
                            if j == 1 and ahead:
                                if behind:
                                    pe.wait_ge(pvT_read.sem, pvT_read.at(i, 0))
                                projection(i, 2)
                            if j == 2 and behind and projected:
                                if ahead:
                                    pe.wait_ge(proj_read.sem, proj_read.at(i, 2 * TB))
                                output_back(i, 0)
                            if j == 3 and behind and projected:
                                pe.wait_ge(pvT_read.sem, pvT_read.at(i, 1))
                                output_projection(i, 0)

            def finish():
                last = Batch(None, 0, B - 1)
                for hh in range(2):
                    values(last, PAIRS - 1, (B - 1) % 2, hh)
                pe.wait_ge(pvT_read.sem, pvT_read.at(last, G - 1))
                back(last, G - 1)
                if projected:
                    output_back(last, 1)
                    output_projection(last, 1)

            all_batches(pe, start, batch, finish)

        @block.scalar
        def _(act):
            def copy_x(i):
                act.wait_ge(proj_in_psum.sem, proj_in_psum.at(i, TB))
                act.activation(xT[:, :], core.XNT[:, bass.ds(i.times(S, S), S)], ACT.Copy).then_inc(xT_ready.sem, 1)

            def copy_qk(i, j):
                act.wait_ge(qkT_in_psum.sem, qkT_in_psum.at(i, j + 1))
                act.wait_ge(scoresT_ready.sem, scoresT_ready.at(i, TB * (j - 1)))
                act.activation(qkT[:, j % 2, :, :], tr_b.rearrange("p (a s) -> p a s", a=2), ACT.Copy).then_inc(qkT_ready.sem, 1)

            def copy_group(i, g):
                act.wait_ge(pv_ready.sem, pv_ready.at(i, 2 * g + 2))
                act.wait_ge(pvT_ready.sem, pvT_ready.at(i, g))
                act.activation(oT[:, :], ps_m[:, :], ACT.Copy).then_inc(pv_read.sem, 1)

            def copy_output(i, n):
                act.wait_ge(attnT_in_psum.sem, attnT_in_psum.at(i, n))
                act.activation(aoT[:, :], ps_tr[:, :], ACT.Copy).then_inc(attnT_ready.sem, 1)

            def start():
                copy_x(Batch(None, 0, -1))
                act.wait_ge(qkT_in_psum.sem, qkT_in_psum.at(0, 1))
                act.activation(qkT[:, 0, :, :], tr_b.rearrange("p (a s) -> p a s", a=2), ACT.Copy).then_inc(qkT_ready.sem, 1)

            def batch(i, u, behind, ahead):
                for j in range(PAIRS):
                    if j == 0 and ahead:
                        copy_x(i)
                    if j == 3 and behind and projected:
                        copy_output(i, 0)
                    if j + 1 < PAIRS or ahead:
                        copy_qk(i, j + 1)
                    act.wait_ge(q2T_in_psum.sem, q2T_in_psum.at(i, j + 1))
                    act.activation(q2T[:, j % 2, :], tr_b[:, 0:S], ACT.Copy).then_inc(q2T_ready.sem, 1)
                    act.wait_ge(pv_ready.sem, pv_ready.at(i, j - 1))
                    for kt in range(TB):
                        n = TB * j + kt
                        act.wait_ge(scoresT_ready.sem, scoresT_ready.at(i, n + 1))
                        act.activation(E[:, j % 2, :, OFF[kt]:OFF[kt] + S - first_q[kt]], ps_t[n % 2][:, :, 0:S - first_q[kt]],
                                       ACT.Exp, scale=scale).then_inc(probs_ready.sem, 1)
                        if kt == 1 and j % 2 == 0 and (j > 0 or behind):
                            copy_group(i, j // 2 - 1)

            def finish():
                copy_group(Batch(None, 0, B - 1), G - 1)
                if projected:
                    copy_output(Batch(None, 0, B - 1), 1)

            all_batches(act, start, batch, finish)

        @block.gpsimd
        def _(pool):
            for u in range(2):
                pool.memset(ks[u], 0.0).then_inc(started, 1)
            pool.wait_ge(started, 2)
            for u in range(2):
                pool.memset(k4[u][:, :, M_ROW:M_ROW + 3], 1.0).then_inc(started, 1)
                pool.memset(v_row[u][:, :, :], 1.0).then_inc(started, 1)
            pool.wait_ge(started, 6)

            def split_k(i, u):
                ch = Chain(pool_step, pool, Batch(i.r, i.step, i.plus + 1), core.pool_passed)
                pool.wait_ge(rotated.sem, rotated.at(i, 2))
                pool.sem_inc(core.pool_passed, 1)
                src = (rot[:, :, H:2 * H, :] if rope else qkv[:, :, D:2 * D].rearrange("p t (h d) -> p t h d", d=HD))
                ksrc = k_tmp[:, :, :].rearrange("p (t h) d -> p t h d", t=TB)
                ch.link(pool.tensor_copy(ksrc, src))
                split3(ch, pool, [[k4[u][:, :, r:r + HD] for r in rows] for rows in K_ROWS],
                       k_tmp[:, :, :], k_rest[:, :, :], k_tmp[:, :, :])
                ch.close()
                pool.memset(k_rest[:, 0, 0:1], 0.0).then_inc(k_ready.sem, 1)

            def reciprocal_root(i, n):
                pool.wait_ge(stats_ready.sem, stats_ready.at(i, n))
                pool.tensor_tensor(rstd[:, :], var[:, :], core.minus_half[:, 0:TB], ALU.pow).then_inc(rstd_ready.sem, 1)

            def batch(i, u, behind, ahead):
                if behind and normed:
                    reciprocal_root(i, 0)
                if ahead:
                    split_k(i, 1 - u)

            def finish():
                if normed:
                    reciprocal_root(Batch(None, 0, B - 1), 1)

            all_batches(pool, lambda: split_k(Batch(None, 0, -1), 0), batch, finish)

        @block.vector
        def _(dve):
            for u in range(2):
                dve.memset(qs[u], 0.0).then_inc(q_cleared, 1)
            dve.wait_ge(q_cleared, 2)
            dve.wait_ge(started, 6)

            def read_projection(i, t, ch):
                dve.wait_ge(proj_in_psum.sem, proj_in_psum.at(i, TB + t + 1))
                if t == 0:
                    dve.wait_ge(k_ready.sem, k_ready.at(i, 1))
                src = ps_tr[:, 0:3 * D]
                if grouped:
                    for g in range(4):
                        for r in range(4):
                            dst = qkv[:, :, :].rearrange("p n (a h d) -> p a n h d", a=3, d=HD)
                            e = dve.tensor_copy(dst[32 * g:32 * g + 32, :, :, 4 * t + r, :],
                                                src[32 * r:32 * r + 32, :].rearrange("p (a n g d) -> p a n g d", a=3, n=4, g=4)[:, :, :, g, :])
                elif bias is not None:
                    e = dve.tensor_tensor(qkv[:, t, :], src, bias[:, :], ALU.add)
                else:
                    e = dve.tensor_copy(qkv[:, t, :], src)
                e.then_inc(proj_read.sem, 1)
                dve.wait_ge(proj_read.sem, proj_read.at(i, TB + t + 1))

            def rotate(i, u, ch):
                qk = qkv[:, :, 0:2 * D].rearrange("p t (h d) -> p t h d", d=HD)
                dve.memset(q4[u][:, :, M_ROW:M_ROW + 3], 0.0)
                if rope:
                    cos = core.w["rope"][:, :, 0:1, :].broadcast_to([P, TB, 2 * H, HD])
                    sin = core.w["rope"][:, :, 1:2, :].broadcast_to([P, TB, 2 * H, HD])
                    dve.tensor_tensor(rot[:, :, :, :], qk, cos, ALU.mult)
                    dve.tensor_tensor(swapped[:, :, :, 0::2], qk[:, :, :, 1::2], sin[:, :, :, 0::2], ALU.mult)
                    ch.link(dve.tensor_tensor(swapped[:, :, :, 1::2], qk[:, :, :, 0::2], sin[:, :, :, 1::2], ALU.mult))
                    dve.tensor_tensor(rot[:, :, :, :], rot[:, :, :, :], swapped[:, :, :, :], ALU.add).then_inc(rotated.sem, 1)
                else:
                    dve.memset(den[:, 0, :], 0.0).then_inc(rotated.sem, 1)
                dve.wait_ge(rotated.sem, rotated.at(i, 2))

            def split_q(i, u, ch):
                q0 = rot[:, :, 0:H, :] if rope else qkv[:, :, 0:D].rearrange("p t (h d) -> p t h d", d=HD)
                qsrc = q_tmp[:, :, :].rearrange("p (t h) d -> p t h d", t=TB)
                ch.link(dve.tensor_copy(qsrc, q0))
                split3(ch, dve, [[q4[u][:, :, r:r + HD] for r in rows] for rows in Q_ROWS],
                       q_tmp[:, :, :], q_rest[:, :, :], q_tmp[:, :, :])
                dve.tensor_copy(v1[u][:, :, :, 0:HD], qkv[:, :, 2 * D:3 * D].rearrange("p t (h d) -> p t h d", d=HD)).then_inc(qv_ready.sem, 1)

            def maxima(i, j, u, ch, between=None, after=None):
                for x in range(TB):
                    qt = TB - 1 - x
                    for hh in range(2):
                        n = 8 * j + 2 * x + hh
                        c = 2 * (j % PAIRS) + hh
                        dve.wait_ge(scores_ready.sem, scores_ready.at(i, n + 1))
                        dve.tensor_reduce(negm[:, qt, c:c + 1], ps_s[hh][:, 0:keys[qt]],
                                          AX.X, ALU.max, negate=True).then_inc(scores_read.sem, 1)
                    if x == 2 and between is not None:
                        between()
                if after is not None:
                    after()
                dve.wait_ge(scores_read.sem, scores_read.at(i, 8 * (j + 1)))
                c = 2 * (j % PAIRS)
                q5 = qs[u].rearrange("p t (h s) -> p t h s", s=SLOT)[:, :, c:c + 2, :]
                src = negm[:, :, c:c + 2]
                for n in range(3):
                    place = q5[:, :, :, M_ROW + n]
                    e = dve.tensor_copy(place, src)
                    if n == 2:
                        e.then_inc(max_ready.sem, 1)
                        break
                    ch.link(e)
                    dst = (m_rest, m_tmp)[n][:, :, :]
                    ch.link(dve.tensor_tensor(dst, src, place, ALU.subtract))
                    src = dst

            def weighted(i, g, ch):
                dve.wait_ge(pvT_ready.sem, pvT_ready.at(i, g + 1))
                pv = ps_tr[:, :].rearrange("p (t h c) -> p t h c", t=TB, c=32)
                ch.link(dve.tensor_scalar(den[:, :, :], pv[:, :, :, HD], eps, None, ALU.add))
                ch.link(dve.reciprocal(rec[:, :, :], den[:, :, :]))
                r = rec[:, :, :].rearrange("p t (h a) -> p t h a", a=1).broadcast_to([P, TB, 4, HD])
                c = g % G * 32
                dve.tensor_tensor(ao[:, :, c:c + 32].rearrange("p t (h d) -> p t h d", d=HD),
                                  pv[:, :, :, 0:HD], r, ALU.mult).then_inc(pvT_read.sem, 1)

            def read_output(i, n, ch):
                dve.wait_ge(out_ready.sem, out_ready.at(i, n + 1))
                po = ps_tr[:, :].rearrange("p (t d) -> p t d", t=TB)
                if bo is not None:
                    e = dve.tensor_tensor(y[:, :, :], po, bo[:, :].rearrange("p (a d) -> p a d", a=1).broadcast_to([P, TB, D]), ALU.add)
                else:
                    e = dve.tensor_copy(y[:, :, :], po)
                e.then_inc(out_read.sem, 1)
                dve.wait_ge(out_read.sem, out_read.at(i, n + 1))

            def output(i, n, ch):
                here = bass.ds(i.times(TB, n * TB), TB)
                if grouped:
                    dve.wait_ge(pvT_read.sem, pvT_read.at(i, G * (n + 1)))
                    for g in range(4):
                        for r in range(4):
                            src = ao[:, :, :].rearrange("p n (t r d) -> p t n r d", t=4, r=4)[32 * g:32 * g + 32, :, :, r, :]
                            dst = y[:, :, :].rearrange("p t (n g d) -> p t n g d", n=4, g=4)[32 * r:32 * r + 32, :, :, g, :]
                            e = dve.tensor_copy(dst, src)
                    ch.link(e)
                    xi = core.XN[:, here, :]
                    ch.link(dve.tensor_tensor(xi, xi, y[:, :, :], ALU.add))
                    return
                y2 = y[:, :, :]
                if normed:
                    ch.link(dve.tensor_tensor(y2, y2, core.XN[:, here, :], ALU.add))
                    for t in range(TB):
                        e = dve.bn_stats(stats[:, t, :], y[:, t, :])
                    ch.link(e)
                    dve.memset(den[:, 0, :], 0.0)
                    for t in range(TB):
                        e = dve.bn_aggr(mv[:, t, :], stats[:, t, :])
                    ch.link(e)
                    dve.tensor_scalar(var[:, :], mv[:, :, 1], LN_EPS, None, ALU.add).then_inc(stats_ready.sem, 1)
                    dve.wait_ge(rstd_ready.sem, rstd_ready.at(i, n + 1))
                    for t in range(TB):
                        e = dve.tensor_scalar(y[:, t, :], y[:, t, :], mv[:, t, 0:1], rstd[:, t:t + 1], ALU.subtract, ALU.mult)
                    ch.link(e)
                    for k, op in enumerate((ALU.mult, ALU.add)):
                        ch.link(dve.tensor_tensor(y2, y2, out_norm[:, k * D:(k + 1) * D].rearrange("p (a d) -> p a d", a=1).broadcast_to([P, TB, D]), op))
                xi = core.X[:, here, :]
                ch.link(dve.tensor_tensor(xi, xi, y2, ALU.add))

            def start():
                before = Batch(None, 0, -1)
                ch = Chain(dve_step, dve, 0)
                for t in range(TB):
                    read_projection(before, t, ch)
                rotate(before, 0, ch)
                split_q(before, 0, ch)
                maxima(Batch(None, 0, 0), 0, 0, ch)
                ch.close()

            def batch(i, u, behind, ahead):
                ch = Chain(dve_step, dve, Batch(i.r, i.step, i.plus + 1))
                for j in range(PAIRS):
                    def between():
                        if j == 0 and ahead:
                            read_projection(i, 0, ch)
                        if j == 2 and ahead:
                            read_projection(i, 3, ch)
                        if j % 2 == 1 and (j > 1 or behind):
                            weighted(i, (j - 3) // 2, ch)

                    def after():
                        if j == 0 and ahead:
                            read_projection(i, 1, ch)
                        if j == 1 and ahead:
                            read_projection(i, 2, ch)
                        if j == 3 and behind and projected:
                            read_output(i, -1, ch)

                    if j + 1 < PAIRS or ahead:
                        maxima(i, j + 1, u if j + 1 < PAIRS else 1 - u, ch, between, after)
                    else:
                        between()
                    if j == 2 and ahead:
                        rotate(i, 1 - u, ch)
                    if j == (2 if grouped else 3) and behind:
                        output(i, -1, ch)
                    if j == 4 and ahead:
                        split_q(i, 1 - u, ch)
                ch.close()

            def finish():
                last = Batch(None, 0, B - 1)
                ch = Chain(dve_step, dve, B + 1)
                weighted(last, G - 1, ch)
                if projected:
                    read_output(last, 0, ch)
                output(last, 0, ch)
                ch.close()

            all_batches(dve, start, batch, finish)

    core.end(B, sig)
    core.end(B + 2, [dve_step])
    core.end(B, [pool_step])


def batch_norm_stage(core, name):
    nc = core.nc
    with ExitStack() as ctx:
        def sb(n, shape, dt=FP32):
            return ctx.enter_context(nc.sbuf_tensor(f"{name}_{n}", shape, dt))

        stats = sb("stats", [P, TB, 6])
        mv = sb("mv", [P, 2])
        both = sb("both", [P, 2])
        sq = sb("sq", [P, 1])
        mean = sb("mean", [P, 2])
        msq = sb("msq", [P, 1])
        var = sb("var", [P, 1])
        rstd = sb("rstd", [P, 1])
        average = sb("average", [P, P])
        xs = sb("xs", [P, TB, D])
        xn = sb("xn", [P, TB, D])
        ps = ctx.enter_context(nc.psum_tensor(f"{name}_ps", [P, 2], FP32))
        sig = core.begin(dve_step=12, stats_ready=1, out_ready=1, sum_ready=1, rstd_ready=1)
        dve_step, stats_ready, out_ready, sum_ready, rstd_ready = sig
        made = ctx.enter_context(nc.semaphore(f"{name}_made"))
        block = ctx.enter_context(nc.Block())

        @block.vector
        def _(dve):
            dve.memset(average[:, :], 1.0 / P).then_inc(made, 1)
            with dve.Fori(0, B) as i:
                ch = Chain(dve_step, dve, i)
                ch.link(dve.tensor_copy(xn[:, :, :], core.XN[:, bass.ds(i * TB, TB), :]))
                for t in range(TB):
                    e = dve.bn_stats(stats[:, t, :], xn[:, t, :])
                ch.link(e)
                dve.memset(sq[:, :], 0.0)
                ch.link(dve.bn_aggr(mv[:, :], stats[:, :, :].rearrange("p t s -> p (t s)")))
                dve.tensor_copy(both[:, 0:1], mv[:, 0:1])
                ch.link(dve.tensor_tensor(sq[:, :], mv[:, 0:1], mv[:, 0:1], ALU.mult))
                dve.tensor_tensor(both[:, 1:2], sq[:, :], mv[:, 1:2], ALU.add).then_inc(stats_ready.sem, 1)
                dve.wait_ge(out_ready.sem, out_ready.at(i, 1))
                ch.link(dve.tensor_copy(mean[:, :], ps[:, :]))
                ch.link(dve.tensor_tensor(msq[:, :], mean[:, 0:1], mean[:, 0:1], ALU.mult))
                ch.link(dve.tensor_tensor(var[:, :], mean[:, 1:2], msq[:, :], ALU.subtract))
                dve.tensor_scalar(var[:, :], var[:, :], LN_EPS, None, ALU.add).then_inc(sum_ready.sem, 1)
                dve.wait_ge(rstd_ready.sem, rstd_ready.at(i, 1))
                ch.link(dve.tensor_scalar(xs[:, :, :], xn[:, :, :], mean[:, 0:1], rstd[:, 0:1], ALU.subtract, ALU.mult))
                xi = core.X[:, bass.ds(i * TB, TB), :]
                ch.link(dve.tensor_tensor(xi, xi, xs[:, :, :], ALU.add))
                ch.close()

        @block.gpsimd
        def _(pool):
            with pool.Fori(0, B) as i:
                pool.wait_ge(sum_ready.sem, sum_ready.at(i, 1))
                pool.tensor_tensor(rstd[:, :], var[:, :], core.minus_half[:, 0:1], ALU.pow).then_inc(rstd_ready.sem, 1)

        @block.tensor
        def _(pe):
            pe.wait_ge(made, 1)
            with pe.Fori(0, B) as i:
                pe.wait_ge(stats_ready.sem, stats_ready.at(i, 1))
                pe.matmul(ps[:, :], average[:, :], both[:, :], start=True, stop=True).then_inc(out_ready.sem, 1)

    core.end(B, sig)


def single_head_attention_stage(core, name, w):
    nc = core.nc
    scale = 1.0 / math.sqrt(D)
    with ExitStack() as ctx:
        def sb(n, shape, dt=FP32):
            return ctx.enter_context(nc.sbuf_tensor(f"{name}_{n}", shape, dt))

        def psum(n, shape, dt=FP32):
            return ctx.enter_context(nc.psum_tensor(f"{name}_{n}", shape, dt))

        xT = sb("xT", [P, S])
        qT = sb("qT", [P, S])
        kT = sb("kT", [P, S])
        v = sb("v", [P, TB, D])
        m = sb("m", [P, TB])
        negm = sb("negm", [P, TB])
        E = sb("E", [P, TB, S])
        total = sb("total", [P, TB])
        rec = sb("rec", [P, TB])
        ET = sb("ET", [P, TB, S])
        y = sb("y", [P, TB, D])
        ps_q, ps_k, ps_v, ps_o = [psum(n, [P, S]) for n in ("ps_q", "ps_k", "ps_v", "ps_o")]
        ps_s = [psum(f"ps_s{n}", [P, S]) for n in range(2)]
        ps_e = [psum(f"ps_e{n}", [P, S]) for n in range(2)]
        sig = core.begin(dve_step=32, xT_ready=1, proj_in_psum=1, proj_read=2, qv_ready=1, scores_ready=TB, max_ready=TB,
                         probs_ready=TB, pvT_ready=TB, pvT_read=TB, out_ready=1, out_read=1)
        (dve_step, xT_ready, proj_in_psum, qk_ready, v_ready, scores_ready, max_ready, probs_ready,
         probsT_in_psum, probsT_ready, out_ready, out_read) = sig
        block = ctx.enter_context(nc.Block())

        def probabilities_back(pe, i, qt):
            pe.wait_ge(probs_ready.sem, probs_ready.at(i, qt + 1))
            pe.wait_ge(probsT_ready.sem, probsT_ready.at(i, qt - 1))
            for kt in range(qt + 1):
                tr = pe.transpose(ps_e[qt % 2][:, kt * P:(kt + 1) * P], E[:, qt, kt * P:(kt + 1) * P], core.identf[:, :])
            tr.then_inc(probsT_in_psum.sem, 1)

        @block.tensor
        def _(pe):
            with pe.Fori(0, B) as i:
                pe.wait_ge(xT_ready.sem, xT_ready.at(i, 1))
                pe.matmul(ps_q[:, :], w[:, 0:D], xT[:, :], start=True, stop=True)
                pe.matmul(ps_k[:, :], w[:, D:2 * D], xT[:, :], start=True, stop=True)
                for t in range(TB):
                    mm = pe.matmul(ps_v[:, t * D:(t + 1) * D], xT[:, t * P:(t + 1) * P], w[:, 2 * D:3 * D], start=True, stop=True)
                mm.then_inc(proj_in_psum.sem, 1)
                pe.wait_ge(qk_ready.sem, qk_ready.at(i, 2))
                for qt in range(TB):
                    pe.wait_ge(probs_ready.sem, probs_ready.at(i, qt - 1))
                    n = P * (qt + 1)
                    pe.matmul(ps_s[qt % 2][:, 0:n], qT[:, qt * P:n], kT[:, 0:n], start=True, stop=False, skip_group_check=True)
                    pe.matmul(ps_s[qt % 2][:, qt * P:n], core.identb[:, :], core.mask_qk[:, :],
                              start=False, stop=True, skip_group_check=True).then_inc(scores_ready.sem, 1)
                    if qt > 0:
                        probabilities_back(pe, i, qt - 1)
                probabilities_back(pe, i, TB - 1)
                pe.wait_ge(v_ready.sem, v_ready.at(i, 1))
                pe.wait_ge(out_read.sem, out_read.at(i, 0))
                for qt in range(TB):
                    pe.wait_ge(probsT_ready.sem, probsT_ready.at(i, qt + 1))
                    for kt in range(qt + 1):
                        mm = pe.matmul(ps_o[:, qt * D:(qt + 1) * D], ET[:, qt, kt * P:(kt + 1) * P], v[:, kt, :],
                                       start=(kt == 0), stop=(kt == qt), skip_group_check=True)
                mm.then_inc(out_ready.sem, 1)

        @block.scalar
        def _(act):
            with act.Fori(0, B) as i:
                act.wait_ge(proj_in_psum.sem, proj_in_psum.at(i, 0))
                act.activation(xT[:, :], core.XNT[:, bass.ds(i * S, S)], ACT.Copy).then_inc(xT_ready.sem, 1)
                act.wait_ge(scores_ready.sem, scores_ready.at(i, 0))
                act.wait_ge(proj_in_psum.sem, proj_in_psum.at(i, 1))
                act.activation(qT[:, :], ps_q[:, :], ACT.Copy).then_inc(qk_ready.sem, 1)
                act.activation(kT[:, :], ps_k[:, :], ACT.Copy).then_inc(qk_ready.sem, 1)
                for qt in range(TB):
                    n = P * (qt + 1)
                    act.wait_ge(max_ready.sem, max_ready.at(i, qt + 1))
                    act.wait_ge(probsT_in_psum.sem, probsT_in_psum.at(i, 0))
                    act.activation(E[:, qt, 0:n], ps_s[qt % 2][:, 0:n], ACT.Exp, bias=negm[:, qt:qt + 1], scale=scale,
                                   accum_out=total[:, qt:qt + 1]).then_inc(probs_ready.sem, 1)

        @block.vector
        def _(dve):
            with dve.Fori(0, B) as i:
                ch = Chain(dve_step, dve, i)
                dve.wait_ge(proj_in_psum.sem, proj_in_psum.at(i, 1))
                dve.tensor_copy(v[:, :, :], ps_v[:, :].rearrange("p (t d) -> p t d", t=TB)).then_inc(v_ready.sem, 1)

                def back(qt):
                    dve.wait_ge(probsT_in_psum.sem, probsT_in_psum.at(i, qt + 1))
                    n = P * (qt + 1)
                    dve.tensor_copy(ET[:, qt, 0:n], ps_e[qt % 2][:, 0:n]).then_inc(probsT_ready.sem, 1)

                for qt in range(TB):
                    dve.wait_ge(scores_ready.sem, scores_ready.at(i, qt + 1))
                    ch.link(dve.tensor_reduce(m[:, qt:qt + 1], ps_s[qt % 2][:, 0:P * (qt + 1)], AX.X, ALU.max, negate=True))
                    dve.tensor_scalar(negm[:, qt:qt + 1], m[:, qt:qt + 1], scale, None, ALU.mult).then_inc(max_ready.sem, 1)
                    if qt > 0:
                        back(qt - 1)
                back(TB - 1)
                dve.wait_ge(probs_ready.sem, probs_ready.at(i, TB))
                ch.link(dve.reciprocal(rec[:, :], total[:, :]))
                dve.wait_ge(out_ready.sem, out_ready.at(i, 1))
                r = rec[:, :].rearrange("p (t a) -> p t a", a=1).broadcast_to([P, TB, D])
                dve.tensor_tensor(y[:, :, :], ps_o[:, :].rearrange("p (t d) -> p t d", t=TB), r, ALU.mult).then_inc(out_read.sem, 1)
                dve.wait_ge(out_read.sem, out_read.at(i, 1))
                xi = core.X[:, bass.ds(i * TB, TB), :]
                ch.link(dve.tensor_tensor(xi, xi, y[:, :, :], ALU.add))
                ch.close()

    core.end(B, sig)


def linear_attention_stage(core, name, w, norm_w, head_mask, block_mask):
    nc = core.nc
    with ExitStack() as ctx:
        def sb(n, shape, dt=FP32):
            return ctx.enter_context(nc.sbuf_tensor(f"{name}_{n}", shape, dt))

        def psum(n, shape, dt=FP32):
            return ctx.enter_context(nc.psum_tensor(f"{name}_{n}", shape, dt))

        NA = 3
        xT = sb("xT", [P, S])
        k = sb("k", [P, TB, D])
        qv = sb("qv", [P, TB, 2 * D])
        sq = sb("sq", [P, TB, 2 * D])
        ms = sb("ms", [P, TB, 2 * H])
        rstd = sb("rstd", [P, TB, 2 * H])
        qT = sb("qT", [P, S])
        qTm = sb("qTm", [P, 4, S])
        state = sb("state", [P, TB - 1, D])
        A = sb("A", [P, NA, TB, P])
        y = sb("y", [P, TB, D])
        ps_p = psum("ps_p", [P, TB, 2 * D])
        ps_q = psum("ps_q", [P, S])
        ps_w = psum("ps_w", [P, TB, D])
        ps_o = psum("ps_o", [P, TB, D])
        ps_s = [psum(f"ps_s{n}", [P, TB, P]) for n in range(NA)]
        sig = core.begin(dve_step=16, xT_ready=1, proj_in_psum=1, stats_ready=1, rstd_ready=1, qv_ready=1,
                         qkT_in_psum=1, qkT_ready=5, state_ready=1, state_used=1, scores_ready=H, scores_read=H,
                         pv_ready=H, out_read=1)
        (dve_step, xT_ready, proj_in_psum, stats_ready, rstd_ready, qv_ready, qT_in_psum, qT_ready, state_in_psum,
         state_ready, scores_ready, scores_read, pv_ready, out_read) = sig
        block = ctx.enter_context(nc.Block())

        @block.tensor
        def _(pe):
            with pe.Fori(0, B) as i:
                pe.wait_ge(xT_ready.sem, xT_ready.at(i, 1))
                for t in range(TB):
                    mm = pe.matmul(ps_p[:, t, :], xT[:, t * P:(t + 1) * P], w[:, :], start=True, stop=True)
                mm.then_inc(proj_in_psum.sem, 1)
                pe.wait_ge(qv_ready.sem, qv_ready.at(i, 1))
                for t in range(TB):
                    tr = pe.transpose(ps_q[:, t * P:(t + 1) * P], qv[:, t, 0:D], core.identf[:, :])
                tr.then_inc(qT_in_psum.sem, 1)
                for t in range(1, TB):
                    for b in range(t):
                        mm = pe.matmul(ps_w[:, t - 1, :], k[:, b, :], qv[:, b, D:2 * D], start=(b == 0), stop=(b == t - 1))
                mm.then_inc(state_in_psum.sem, 1)

                def scores(h):
                    r = slice(32 * (h // 4), 32 * (h // 4) + 32)
                    pe.wait_ge(scores_read.sem, scores_read.at(i, h - NA + 1))
                    for t in range(TB):
                        mm = pe.matmul(ps_s[h % NA][:, t, :], xT[r, t * P:(t + 1) * P], qTm[r, h % 4, t * P:(t + 1) * P],
                                       start=True, stop=True)
                    mm.then_inc(scores_ready.sem, 1)

                pe.wait_ge(qT_ready.sem, qT_ready.at(i, 5))
                for h in range(NA - 1):
                    scores(h)
                pe.wait_ge(state_ready.sem, state_ready.at(i, 1))
                pe.wait_ge(out_read.sem, out_read.at(i, 0))
                for t in range(1, TB):
                    pe.matmul(ps_o[:, t, :], qT[:, t * P:(t + 1) * P], state[:, t - 1, :], start=(t == 1), stop=False, skip_group_check=True)
                for h in range(H):
                    if h + NA - 1 < H:
                        scores(h + NA - 1)
                    pe.wait_ge(scores_read.sem, scores_read.at(i, h + 1))
                    for t in range(TB):
                        mm = pe.matmul(ps_o[:, t, h * HD:(h + 1) * HD], A[:, h % NA, t, :], qv[:, t, D + h * HD:D + (h + 1) * HD],
                                       start=False, stop=(h == H - 1), skip_group_check=True)
                    mm.then_inc(pv_ready.sem, 1)

        @block.scalar
        def _(act):
            with act.Fori(0, B) as i:
                act.wait_ge(pv_ready.sem, pv_ready.at(i, 0))
                act.activation(xT[:, :], core.XNT[:, bass.ds(i * S, S)], ACT.Copy).then_inc(xT_ready.sem, 1)
                act.wait_ge(qT_in_psum.sem, qT_in_psum.at(i, 1))
                for n in range(4):
                    act.activation(qTm[:, n, :], ps_q[:, :], ACT.Copy, scale=head_mask[:, n:n + 1]).then_inc(qT_ready.sem, 1)
                act.activation(qT[:, :], ps_q[:, :], ACT.Copy).then_inc(qT_ready.sem, 1)

        @block.gpsimd
        def _(pool):
            with pool.Fori(0, B) as i:
                pool.wait_ge(stats_ready.sem, stats_ready.at(i, 1))
                pool.tensor_tensor(rstd[:, :, :], ms[:, :, :],
                                   core.minus_half[:, 0:1].rearrange("p (a b) -> p a b", a=1).broadcast_to([P, TB, 2 * H]),
                                   ALU.pow).then_inc(rstd_ready.sem, 1)

        @block.vector
        def _(dve):
            with dve.Fori(0, B) as i:
                ch = Chain(dve_step, dve, i)
                dve.tensor_copy(k[:, :, :], core.XN[:, bass.ds(i * TB, TB), :])
                dve.wait_ge(proj_in_psum.sem, proj_in_psum.at(i, 1))
                ch.link(dve.tensor_copy(qv[:, :, :], ps_p[:, :, :]))
                ch.link(dve.tensor_tensor(sq[:, :, :], qv[:, :, :], qv[:, :, :], ALU.mult))
                ch.link(dve.tensor_reduce(ms[:, :, :], sq[:, :, :].rearrange("p t (h d) -> p t h d", d=HD), AX.X, ALU.add))
                dve.tensor_scalar(ms[:, :, :], ms[:, :, :], 1.0 / HD, 1e-8, ALU.mult, ALU.add).then_inc(stats_ready.sem, 1)
                dve.wait_ge(rstd_ready.sem, rstd_ready.at(i, 1))
                qv4 = qv[:, :, :].rearrange("p t (h d) -> p t h d", d=HD)
                r4 = rstd[:, :, :].rearrange("p t (h a) -> p t h a", a=1).broadcast_to([P, TB, 2 * H, HD])
                ch.link(dve.tensor_tensor(qv4, qv4, r4, ALU.mult))
                nw = norm_w[:, :].rearrange("p (a d) -> p a d", a=1).broadcast_to([P, TB, 2 * D])
                dve.tensor_tensor(qv[:, :, :], qv[:, :, :], nw, ALU.mult).then_inc(qv_ready.sem, 1)
                dve.wait_ge(state_in_psum.sem, state_in_psum.at(i, 1))
                dve.tensor_tensor(state[:, :, :], ps_w[:, 0:TB - 1, :],
                                  block_mask.rearrange("p (a d) -> p a d", a=1).broadcast_to([P, TB - 1, D]),
                                  ALU.mult).then_inc(state_ready.sem, 1)
                keep = core.keep_kq[:, :].rearrange("p (a d) -> p a d", a=1).broadcast_to([P, TB, P])
                for h in range(H):
                    dve.wait_ge(scores_ready.sem, scores_ready.at(i, h + 1))
                    dve.wait_ge(pv_ready.sem, pv_ready.at(i, h - NA + 1))
                    dve.tensor_tensor(A[:, h % NA, :, :], ps_s[h % NA][:, :, :], keep, ALU.mult).then_inc(scores_read.sem, 1)
                dve.wait_ge(pv_ready.sem, pv_ready.at(i, H))
                dve.tensor_copy(y[:, :, :], ps_o[:, :, :]).then_inc(out_read.sem, 1)
                dve.wait_ge(out_read.sem, out_read.at(i, 1))
                xi = core.X[:, bass.ds(i * TB, TB), :]
                ch.link(dve.tensor_tensor(xi, xi, y[:, :, :], ALU.add))
                ch.close()

    core.end(B, sig)


def batch_attention_stage(core, name, w, bias, wo, bo):
    nc = core.nc
    scale = HD ** -0.5
    tri = [b * (b + 1) // 2 for b in range(B + 1)]
    with ExitStack() as ctx:
        def sb(n, shape, dt=FP32):
            return ctx.enter_context(nc.sbuf_tensor(f"{name}_{n}", shape, dt))

        def psum(n, shape, dt=FP32):
            return ctx.enter_context(nc.psum_tensor(f"{name}_{n}", shape, dt))

        xT = sb("xT", [P, B, P])
        qkv = sb("qkv", [P, B, 3 * D])
        rot = sb("rot", [P, B, 2 * H, HD])
        swapped = sb("swapped", [P, B, 2 * H, HD])
        prod = sb("prod", [P, tri[B], H, HD])
        sc = sb("sc", [P, B, H, B])
        e = sb("e", [P, B, H, B])
        top = sb("top", [P, B, H])
        total = sb("total", [P, B, H])
        att = sb("att", [P, B, D])
        attT = sb("attT", [P, B, P])
        y = sb("y", [P, B, D])
        ps_p = [psum(f"ps_p{n}", [P, 3 * D]) for n in range(4)]
        ps_t = [psum(f"ps_t{n}", [P, 4, P]) for n in range(2)]
        ps_o = [psum(f"ps_o{n}", [P, 4, D]) for n in range(2)]
        sig = core.begin(dve_step=32, xT_ready=1, proj_in_psum=B, proj_read=B, gate_ready=1, exp_ready=1,
                         attn_ready=1, attnT_in_psum=2, attnT_ready=2, out_ready=2, out_read=2)
        (dve_step, xT_ready, proj_in_psum, proj_read, scores_ready, probs_ready, attn_ready, attnT_in_psum,
         attnT_ready, out_ready, out_read) = sig
        block = ctx.enter_context(nc.Block())

        @block.tensor
        def _(pe):
            with pe.Fori(0, TB) as i:
                pe.wait_ge(xT_ready.sem, xT_ready.at(i, 1))
                for b in range(B):
                    pe.wait_ge(proj_read.sem, proj_read.at(i, b - 3))
                    pe.matmul(ps_p[b % 4][:, :], xT[:, b, :], w[:, :], start=True, stop=True).then_inc(proj_in_psum.sem, 1)
                pe.wait_ge(attn_ready.sem, attn_ready.at(i, 1))
                for n in range(2):
                    for b in range(4):
                        tr = pe.transpose(ps_t[n][:, b, :], att[:, 4 * n + b, :], core.identf[:, :])
                    tr.then_inc(attnT_in_psum.sem, 1)
                for n in range(2):
                    pe.wait_ge(attnT_ready.sem, attnT_ready.at(i, n + 1))
                    pe.wait_ge(out_read.sem, out_read.at(i, n - 1))
                    for b in range(4):
                        mm = pe.matmul(ps_o[n][:, b, :], attT[:, 4 * n + b, :], wo[:, :], start=True, stop=True)
                    mm.then_inc(out_ready.sem, 1)

        @block.scalar
        def _(act):
            with act.Fori(0, TB) as i:
                act.wait_ge(proj_in_psum.sem, proj_in_psum.at(i, 0))
                act.activation(xT[:, :, :], core.XNT[:, :].rearrange("p (b t n) -> p b t n", b=B, t=TB)[:, :, bass.ds(i, 1), :]
                               .rearrange("p b a n -> p b (a n)"), ACT.Copy).then_inc(xT_ready.sem, 1)
                act.wait_ge(scores_ready.sem, scores_ready.at(i, 1))
                act.activation(e[:, :, :, :], sc[:, :, :, :], ACT.Exp, scale=scale).then_inc(probs_ready.sem, 1)
                for n in range(2):
                    act.wait_ge(attnT_in_psum.sem, attnT_in_psum.at(i, n + 1))
                    act.wait_ge(out_ready.sem, out_ready.at(i, 0))
                    act.activation(attT[:, 4 * n:4 * n + 4, :], ps_t[n][:, :, :], ACT.Copy).then_inc(attnT_ready.sem, 1)

        @block.vector
        def _(dve):
            with dve.Fori(0, TB) as i:
                ch = Chain(dve_step, dve, i)
                dve.memset(sc[:, :, :, :], NEG)
                for b in range(B):
                    dve.wait_ge(proj_in_psum.sem, proj_in_psum.at(i, b + 1))
                    dve.tensor_tensor(qkv[:, b, :], ps_p[b % 4][:, :], bias[:, :], ALU.add).then_inc(proj_read.sem, 1)
                dve.wait_ge(proj_read.sem, proj_read.at(i, B))
                qk = qkv[:, :, 0:2 * D].rearrange("p b (h d) -> p b h d", d=HD)
                cos = core.w["rope_batch"][:, :, 0:1, :].broadcast_to([P, B, 2 * H, HD])
                sin = core.w["rope_batch"][:, :, 1:2, :].broadcast_to([P, B, 2 * H, HD])
                dve.tensor_tensor(rot[:, :, :, :], qk, cos, ALU.mult)
                dve.tensor_tensor(swapped[:, :, :, 0::2], qk[:, :, :, 1::2], sin[:, :, :, 0::2], ALU.mult)
                ch.link(dve.tensor_tensor(swapped[:, :, :, 1::2], qk[:, :, :, 0::2], sin[:, :, :, 1::2], ALU.mult))
                ch.link(dve.tensor_tensor(rot[:, :, :, :], rot[:, :, :, :], swapped[:, :, :, :], ALU.add))
                for b in range(B):
                    q = rot[:, b:b + 1, 0:H, :].broadcast_to([P, b + 1, H, HD])
                    m = dve.tensor_tensor(prod[:, tri[b]:tri[b + 1], :, :], q, rot[:, 0:b + 1, H:2 * H, :], ALU.mult)
                ch.link(m)
                for b in range(B):
                    m = dve.tensor_reduce(sc[:, b, :, :].rearrange("p h c -> p c h")[:, 0:b + 1, :],
                                          prod[:, tri[b]:tri[b + 1], :, :], AX.X, ALU.add)
                ch.link(m)
                ch.link(dve.tensor_reduce(top[:, :, :], sc[:, :, :, :], AX.X, ALU.max))
                dve.tensor_tensor(sc[:, :, :, :], sc[:, :, :, :],
                                  top[:, :, :].rearrange("p b (h a) -> p b h a", a=1).broadcast_to([P, B, H, B]),
                                  ALU.subtract).then_inc(scores_ready.sem, 1)
                dve.wait_ge(probs_ready.sem, probs_ready.at(i, 1))
                dve.tensor_reduce(total[:, :, :], e[:, :, :, :], AX.X, ALU.add)
                v4 = qkv[:, :, 2 * D:3 * D].rearrange("p b (h d) -> p b h d", d=HD)
                for b in range(B):
                    p4 = e[:, b, :, 0:b + 1].rearrange("p h (c a) -> p c h a", a=1).broadcast_to([P, b + 1, H, HD])
                    m = dve.tensor_tensor(prod[:, tri[b]:tri[b + 1], :, :], p4, v4[:, 0:b + 1, :, :], ALU.mult)
                ch.link(m)
                for b in range(B):
                    m = dve.tensor_reduce(att[:, b, :], prod[:, tri[b]:tri[b + 1], :, :].rearrange("p c h d -> p (h d) c"), AX.X, ALU.add)
                dve.reciprocal(total[:, :, :], total[:, :, :])
                ch.link(dve.memset(top[:, 0, :], 0.0))
                a4 = att[:, :, :].rearrange("p b (h d) -> p b h d", d=HD)
                dve.tensor_tensor(a4, a4, total[:, :, :].rearrange("p b (h a) -> p b h a", a=1).broadcast_to([P, B, H, HD]),
                                  ALU.mult).then_inc(attn_ready.sem, 1)
                b4 = bo[:, :].rearrange("p (a d) -> p a d", a=1).broadcast_to([P, 4, D])
                for n in range(2):
                    dve.wait_ge(out_ready.sem, out_ready.at(i, n + 1))
                    dve.tensor_tensor(y[:, 4 * n:4 * n + 4, :], ps_o[n][:, :, :], b4, ALU.add).then_inc(out_read.sem, 1)
                dve.wait_ge(out_read.sem, out_read.at(i, 2))
                xi = core.X[:, :, :].rearrange("p (b t) d -> p b t d", b=B)[:, :, bass.ds(i, 1), :].rearrange("p b a d -> p b (a d)")
                ch.link(dve.tensor_tensor(xi, xi, y[:, :, :], ALU.add))
                ch.close()

    core.end(TB, sig)


def mixer_stage(core, name, w, meanT):
    nc = core.nc
    DH, SLOTS, NR = 32, 64, 3
    RMS_EPS = 1.1920929e-07
    scale, land_scale = 1.0 / math.sqrt(DH), 1.0 / math.sqrt(D)
    with ExitStack() as ctx:
        def sb(n, shape, dt=FP32):
            return ctx.enter_context(nc.sbuf_tensor(f"{name}_{n}", shape, dt))

        def psum(n, shape, dt=FP32):
            return ctx.enter_context(nc.psum_tensor(f"{name}_{n}", shape, dt))

        xr = sb("xr", [P, TB, D])
        sq = sb("sq", [P, TB, D])
        ms = sb("ms", [P, TB])
        rstd = sb("rstd", [P, 2, TB])
        xn = sb("xn", [P, TB, D])
        xnT = sb("xnT", [P, S])
        xsum = sb("xsum", [P, 1])
        fresh = sb("fresh", [P, S])
        lam = sb("lam", [P, S])
        one_less = sb("one_less", [P, 1])
        minus_slam = sb("minus_slam", [P, 1])
        ssm = sb("ssm", [P, S])
        sum_rep = sb("sum_rep", [P, P])
        last_rep = sb("last_rep", [P, P])
        hidden = sb("hidden", [SLOTS, P])
        route = sb("route", [P, NR])
        route_e = sb("route_e", [P, NR])
        route_s = sb("route_s", [P, 4])
        land_s = sb("land_s", [P, 4])
        land_e = sb("land_e", [P, SLOTS])
        land_p = sb("land_p", [P, SLOTS])
        qT = sb("qT", [2 * DH, S])
        kT = sb("kT", [2 * DH, S])
        v = sb("v", [P, TB, DH])
        m = sb("m", [P, 2 * TB])
        negm = sb("negm", [P, 2 * TB])
        total = sb("total", [P, 2 * TB])
        rec = sb("rec", [P, 2 * TB])
        E = sb("E", [P, 4, S])
        first = sb("first", [P, 2, S])
        wt = sb("wt", [P, 2, S])
        wtT = sb("wtT", [P, TB, S])
        ctxT = sb("ctxT", [DH, S])
        mixT = sb("mixT", [P, S])
        o = sb("o", [P, TB, D])
        average = sb("average", [P, 1])
        ps_x = psum("ps_x", [P, S])
        ps_qk = psum("ps_qk", [P, S])
        ps_r = psum("ps_r", [P, S])
        ps_m = psum("ps_m", [P, S])
        ps_s = [psum(f"ps_s{n}", [P, S]) for n in range(2)]
        ps_e = [psum(f"ps_e{n}", [P, TB, P]) for n in range(2)]
        V0, R0, L0 = 0, TB * DH, TB * DH + P
        sig = core.begin(dve_step=48, stats_ready=2, rstd_ready=2, norm_ready=1, normT_in_psum=1, normT_ready=1,
                         decayed=1, repeated=1, proj_in_psum=1, proj_read=2, qv_ready=1, silu_ready=1,
                         route_in_psum=1, route_max=1, route_exp=1, route_ready=1, land_max=1, land_exp=1,
                         scores_ready=8, max_ready=8, probs_ready=8, attn_ready=TB, attnT_in_psum=TB, attnT_ready=TB,
                         pv_ready=1, pv_read=1, out_ready=1, mixed_ready=1, down_ready=1, output_ready=1, mean_in_psum=1)
        (dve_step, stats_ready, rstd_ready, norm_ready, normT_in_psum, normT_ready, decayed, repeated, proj_in_psum,
         qk_ready, v_ready, silu_ready, route_in_psum, route_max, route_exp, route_ready, land_max,
         land_exp, scores_ready, max_ready, probs_ready, attn_ready, attnT_in_psum, attnT_ready, context_in_psum,
         context_ready, slr_in_psum, mixed_ready, output_in_psum, output_ready, mean_in_psum) = sig
        started = ctx.enter_context(nc.semaphore(f"{name}_started"))
        block = ctx.enter_context(nc.Block())

        @block.tensor
        def _(pe):
            with pe.Fori(0, B) as i:
                pe.wait_ge(norm_ready.sem, norm_ready.at(i, 1))
                for t in range(TB):
                    tr = pe.transpose(ps_x[:, t * P:(t + 1) * P], xn[:, t, :], core.identf[:, :])
                tr.then_inc(normT_in_psum.sem, 1)
                pe.wait_ge(normT_ready.sem, normT_ready.at(i, 1))
                pe.matmul(ps_qk[:, :], w["l3b_qk"][:, 0:4 * DH], xnT[:, :], start=True, stop=True)
                for t in range(TB):
                    mm = pe.matmul(ps_r[:, V0 + t * DH:V0 + (t + 1) * DH], xnT[:, t * P:(t + 1) * P], w["l3b_qk"][:, 4 * DH:5 * DH],
                                   start=True, stop=True)
                pe.wait_ge(repeated.sem, repeated.at(i, 1))
                pe.matmul(ps_r[0:SLOTS, R0:R0 + P], w["l3b_r1"][:, :], sum_rep[:, :], start=True, stop=True)
                pe.matmul(ps_r[:, L0:L0 + SLOTS], last_rep[:, :], w["l3b_landT"][:, :], start=True, stop=True).then_inc(proj_in_psum.sem, 1)
                pe.wait_ge(silu_ready.sem, silu_ready.at(i, 1))
                pe.matmul(ps_m[:, 0:NR], hidden[:, :], w["l3b_r2"][0:SLOTS, :], start=True, stop=True).then_inc(route_in_psum.sem, 1)
                pe.wait_ge(qk_ready.sem, qk_ready.at(i, 2))
                pe.wait_ge(v_ready.sem, v_ready.at(i, 1))

                def back(qt):
                    pe.wait_ge(attn_ready.sem, attn_ready.at(i, qt + 1))
                    pe.wait_ge(attnT_ready.sem, attnT_ready.at(i, qt - 1))
                    for kt in range(TB):
                        tr = pe.transpose(ps_e[qt % 2][:, kt, :], wt[:, qt % 2, kt * P:(kt + 1) * P], core.identf[:, :])
                    tr.then_inc(attnT_in_psum.sem, 1)

                for qt in range(TB):
                    for a in range(2):
                        n = 2 * qt + a
                        pe.wait_ge(probs_ready.sem, probs_ready.at(i, n - 1))
                        pe.matmul(ps_s[a][:, :], qT[DH * a:DH * a + DH, qt * P:(qt + 1) * P], kT[DH * a:DH * a + DH, :],
                                  start=True, stop=True).then_inc(scores_ready.sem, 1)
                    if qt > 0:
                        back(qt - 1)
                back(TB - 1)
                pe.wait_ge(attnT_ready.sem, attnT_ready.at(i, TB))
                for kt in range(TB):
                    mm = pe.matmul(ps_qk[0:DH, :], v[:, kt, :], wtT[:, kt, :], start=(kt == 0), stop=(kt == TB - 1))
                mm.then_inc(context_in_psum.sem, 1)
                pe.wait_ge(context_ready.sem, context_ready.at(i, 1))
                pe.matmul(ps_x[:, :], w["l3b_wo"][0:DH, :], ctxT[:, :], start=True, stop=True).then_inc(slr_in_psum.sem, 1)
                pe.wait_ge(mixed_ready.sem, mixed_ready.at(i, 1))
                for t in range(TB):
                    pe.matmul(ps_e[0][:, t, :], mixT[:, t * P:(t + 1) * P], w["l3b_mix"][:, 0, :], start=True, stop=False)
                    mm = pe.matmul(ps_e[0][:, t, :], xnT[:, t * P:(t + 1) * P], w["l3b_mix"][:, 1, :], start=False, stop=True)
                mm.then_inc(output_in_psum.sem, 1)
                pe.wait_ge(output_ready.sem, output_ready.at(i, 1))
                for t in range(TB):
                    mm = pe.matmul(ps_m[:, 8:9], o[:, t, :], average[:, :], start=(t == 0), stop=(t == TB - 1))
                mm.then_inc(mean_in_psum.sem, 1)

        @block.scalar
        def _(act):
            act.wait_ge(started, 1)
            with act.Fori(0, B) as i:
                act.wait_ge(normT_in_psum.sem, normT_in_psum.at(i, 1))
                act.activation(xnT[:, :], ps_x[:, :], ACT.Copy, accum_out=xsum[:, :]).then_inc(normT_ready.sem, 1)
                act.activation(fresh[:, :], ps_x[:, :], ACT.Copy, scale=one_less[:, :]).then_inc(decayed.sem, 1)
                act.wait_ge(proj_in_psum.sem, proj_in_psum.at(i, 1))
                act.activation(qT[:, :], ps_qk[0:2 * DH, :], ACT.Copy).then_inc(qk_ready.sem, 1)
                act.activation(kT[:, :], ps_qk[2 * DH:4 * DH, :], ACT.Copy).then_inc(qk_ready.sem, 1)
                act.wait_ge(v_ready.sem, v_ready.at(i, 1))
                act.activation(hidden[:, :], ps_r[0:SLOTS, R0:R0 + P], ACT.Silu, scale=1.0 / S).then_inc(silu_ready.sem, 1)
                act.wait_ge(land_max.sem, land_max.at(i, 1))
                act.activation(land_e[:, :], land_p[:, :], ACT.Exp, bias=land_s[:, 0:1], scale=land_scale,
                               accum_out=land_s[:, 1:2]).then_inc(land_exp.sem, 1)
                act.wait_ge(route_max.sem, route_max.at(i, 1))
                act.activation(route_e[:, :], route[:, :], ACT.Exp, bias=route_s[:, 0:1],
                               accum_out=route_s[:, 1:2]).then_inc(route_exp.sem, 1)

                def copy_back(qt):
                    act.wait_ge(attnT_in_psum.sem, attnT_in_psum.at(i, qt + 1))
                    act.activation(wtT[:, :, qt * P:(qt + 1) * P], ps_e[qt % 2][:, :, :], ACT.Copy).then_inc(attnT_ready.sem, 1)

                for qt in range(TB):
                    for a in range(2):
                        n = 2 * qt + a
                        act.wait_ge(max_ready.sem, max_ready.at(i, n + 1))
                        act.wait_ge(attn_ready.sem, attn_ready.at(i, qt - 1))
                        act.activation(E[:, n % 4, :], ps_s[a][:, :], ACT.Exp, bias=negm[:, n:n + 1], scale=scale,
                                       accum_out=total[:, n:n + 1]).then_inc(probs_ready.sem, 1)
                    if qt > 0:
                        copy_back(qt - 1)
                copy_back(TB - 1)
                act.wait_ge(context_in_psum.sem, context_in_psum.at(i, 1))
                act.wait_ge(route_ready.sem, route_ready.at(i, 1))
                act.activation(ctxT[:, :], ps_qk[0:DH, :], ACT.Copy, scale=route_s[0:DH, 2:3]).then_inc(context_ready.sem, 1)

        @block.gpsimd
        def _(pool):
            with pool.Fori(0, B) as i:
                for n in range(2):
                    pool.wait_ge(stats_ready.sem, stats_ready.at(i, n + 1))
                    pool.tensor_tensor(rstd[:, n, :], ms[:, :], core.minus_half[:, 0:TB], ALU.pow).then_inc(rstd_ready.sem, 1)

        @block.vector
        def _(dve):
            dve.tensor_copy(lam[:, :], w["l3b_lam"][:, :].broadcast_to([P, S]))
            dve.tensor_scalar(one_less[:, :], w["l3b_lam"][:, :], -1.0, 1.0, ALU.mult, ALU.add)
            dve.tensor_scalar(minus_slam[:, :], w["l3b_slam"][:, :], -1.0, None, ALU.mult)
            dve.memset(average[:, :], 1.0 / S).then_inc(started, 1)
            dve.wait_ge(started, 1)

            def rms(ch, i, n, x, weight):
                ch.link(dve.tensor_tensor(sq[:, :, :], x, x, ALU.mult))
                ch.link(dve.tensor_reduce(ms[:, :], sq[:, :, :], AX.X, ALU.add))
                dve.tensor_scalar(ms[:, :], ms[:, :], 1.0 / D, RMS_EPS, ALU.mult, ALU.add).then_inc(stats_ready.sem, 1)
                dve.wait_ge(rstd_ready.sem, rstd_ready.at(i, n + 1))
                r = rstd[:, n, :].rearrange("p (t a) -> p t a", a=1).broadcast_to([P, TB, D])
                ch.link(dve.tensor_tensor(x, x, r, ALU.mult))
                return dve.tensor_tensor(x, x, weight.rearrange("p (a d) -> p a d", a=1).broadcast_to([P, TB, D]), ALU.mult)

            with dve.Fori(0, B) as i:
                ch = Chain(dve_step, dve, i)
                dve.tensor_copy(xr[:, :, :], core.XN[:, bass.ds(i * TB, TB), :])
                ch.link(dve.tensor_copy(xn[:, :, :], core.XN[:, bass.ds(i * TB, TB), :]))
                rms(ch, i, 0, xn[:, :, :], w["l3b_norm_w"][:, 0:D]).then_inc(norm_ready.sem, 1)
                dve.wait_ge(normT_ready.sem, normT_ready.at(i, 1))
                dve.tensor_copy(sum_rep[:, :], xsum[:, :].broadcast_to([P, P]))
                dve.tensor_copy(last_rep[:, :], xnT[:, S - 1:S].broadcast_to([P, P])).then_inc(repeated.sem, 1)
                dve.wait_ge(decayed.sem, decayed.at(i, 1))
                ch.link(dve.tensor_tensor_scan(ssm[:, :], lam[:, :], fresh[:, :], 0.0, ALU.mult, ALU.add))
                dve.wait_ge(proj_in_psum.sem, proj_in_psum.at(i, 1))
                ch.link(dve.tensor_copy(land_p[:, :], ps_r[:, L0:L0 + SLOTS]))
                dve.tensor_copy(v[:, :, :], ps_r[:, V0:V0 + TB * DH].rearrange("p (t d) -> p t d", t=TB)).then_inc(v_ready.sem, 1)
                ch.link(dve.tensor_reduce(land_s[:, 2:3], land_p[:, :], AX.X, ALU.max, negate=True))
                dve.tensor_scalar(land_s[:, 0:1], land_s[:, 2:3], land_scale, None, ALU.mult).then_inc(land_max.sem, 1)
                dve.wait_ge(route_in_psum.sem, route_in_psum.at(i, 1))
                ch.link(dve.tensor_tensor(route[:, :], ps_m[:, 0:NR], w["l3b_rb"][:, :], ALU.add))
                dve.tensor_reduce(route_s[:, 0:1], route[:, :], AX.X, ALU.max, negate=True).then_inc(route_max.sem, 1)
                dve.wait_ge(land_exp.sem, land_exp.at(i, 1))
                ch.link(dve.tensor_tensor(land_p[:, :], land_e[:, :], w["l3b_landT"][:, :], ALU.mult))
                dve.tensor_reduce(land_s[:, 2:3], land_p[:, :], AX.X, ALU.add)
                ch.link(dve.reciprocal(land_s[:, 3:4], land_s[:, 1:2]))
                ch.link(dve.tensor_tensor(land_s[:, 2:3], land_s[:, 2:3], land_s[:, 3:4], ALU.mult))
                dve.wait_ge(route_exp.sem, route_exp.at(i, 1))
                dve.tensor_tensor(route_s[:, 2:3], route_e[:, 1:2], route_e[:, 2:3], ALU.add)
                ch.link(dve.reciprocal(route_s[:, 3:4], route_s[:, 1:2]))
                ch.link(dve.tensor_tensor(route_s[:, 2:3], route_s[:, 2:3], route_s[:, 3:4], ALU.mult))
                dve.tensor_tensor(route_s[:, 3:4], route_e[:, 2:3], route_s[:, 3:4], ALU.mult).then_inc(route_ready.sem, 1)
                dve.wait_ge(route_ready.sem, route_ready.at(i, 1))
                ch.link(dve.tensor_tensor(land_s[:, 2:3], land_s[:, 2:3], route_s[:, 3:4], ALU.mult))

                def combined(qt):
                    dve.wait_ge(probs_ready.sem, probs_ready.at(i, 2 * qt + 2))
                    ch.link(dve.reciprocal(rec[:, 2 * qt:2 * qt + 2], total[:, 2 * qt:2 * qt + 2]))
                    dve.tensor_scalar(first[:, qt % 2, :], E[:, 2 * qt % 4, :], rec[:, 2 * qt:2 * qt + 1], None, ALU.mult)
                    ch.link(dve.tensor_tensor(rec[:, 2 * qt + 1:2 * qt + 2], rec[:, 2 * qt + 1:2 * qt + 2], minus_slam[:, :], ALU.mult))
                    dve.wait_ge(attnT_in_psum.sem, attnT_in_psum.at(i, qt - 1))
                    dve.scalar_tensor_tensor(wt[:, qt % 2, :], E[:, (2 * qt + 1) % 4, :], rec[:, 2 * qt + 1:2 * qt + 2],
                                             first[:, qt % 2, :], ALU.mult, ALU.add).then_inc(attn_ready.sem, 1)

                for qt in range(TB):
                    for a in range(2):
                        n = 2 * qt + a
                        dve.wait_ge(scores_ready.sem, scores_ready.at(i, n + 1))
                        ch.link(dve.tensor_reduce(m[:, n:n + 1], ps_s[a][:, :], AX.X, ALU.max, negate=True))
                        dve.tensor_scalar(negm[:, n:n + 1], m[:, n:n + 1], scale, None, ALU.mult).then_inc(max_ready.sem, 1)
                    if qt > 0:
                        combined(qt - 1)
                combined(TB - 1)
                dve.wait_ge(slr_in_psum.sem, slr_in_psum.at(i, 1))
                ch.link(dve.tensor_tensor(mixT[:, :], ssm[:, :], ps_x[:, :], ALU.add))
                dve.tensor_tensor(mixT[:, S - 1:S], mixT[:, S - 1:S], land_s[:, 2:3], ALU.add).then_inc(mixed_ready.sem, 1)
                dve.wait_ge(output_in_psum.sem, output_in_psum.at(i, 1))
                dve.wait_ge(mean_in_psum.sem, mean_in_psum.at(i, 0))
                ch.link(dve.tensor_copy(o[:, :, :], ps_e[0][:, :, :]))
                ch.link(rms(ch, i, 1, o[:, :, :], w["l3b_norm_w"][:, D:2 * D]))
                dve.tensor_tensor(o[:, :, :], o[:, :, :], xr[:, :, :], ALU.add).then_inc(output_ready.sem, 1)
                dve.wait_ge(output_ready.sem, output_ready.at(i, 1))
                xi = core.X[:, bass.ds(i * TB, TB), :]
                ch.link(dve.tensor_tensor(xi, xi, o[:, :, :], ALU.add))
                dve.wait_ge(mean_in_psum.sem, mean_in_psum.at(i, 1))
                ch.link(dve.tensor_copy(meanT[:, bass.ds(i, 1)], ps_m[:, 8:9]))
                ch.close()

    core.end(B, sig)


def bus_stage(core, name, w, meanT):
    nc = core.nc
    with ExitStack() as ctx:
        def sb(n, shape, dt=FP32):
            return ctx.enter_context(nc.sbuf_tensor(f"{name}_{n}", shape, dt))

        summary = sb("summary", [P, B])
        published = sb("published", [P, B, P])
        y = sb("y", [P, B, D])
        ps_c = ctx.enter_context(nc.psum_tensor(f"{name}_ps_c", [P, B], FP32))
        ps_p = ctx.enter_context(nc.psum_tensor(f"{name}_ps_p", [P, B], FP32))
        ps_y = ctx.enter_context(nc.psum_tensor(f"{name}_ps_y", [P, B, D], FP32))
        in_psum = ctx.enter_context(nc.semaphore(f"{name}_in_psum"))
        copied = ctx.enter_context(nc.semaphore(f"{name}_copied"))
        block = ctx.enter_context(nc.Block())

        @block.tensor
        def _(pe):
            pe.matmul(ps_c[:, :], w["l3b_bus"][:, 0:D], meanT[:, :], start=True, stop=True).then_inc(in_psum, 1)
            pe.wait_ge(copied, 1)
            pe.matmul(ps_p[:, :], w["l3b_bus"][:, D:2 * D], summary[:, :], start=True, stop=True).then_inc(in_psum, 1)
            pe.wait_ge(copied, 2)
            for b in range(B):
                mm = pe.matmul(ps_y[:, b, :], published[:, b, :], w["l3b_bus"][:, 2 * D:3 * D], start=True, stop=True)
            mm.then_inc(in_psum, 1)

        @block.vector
        def _(dve):
            dve.wait_ge(in_psum, 1)
            dve.tensor_copy(summary[:, :], ps_c[:, :]).then_inc(copied, 1)
            dve.wait_ge(in_psum, 2)
            dve.tensor_copy(published[:, :, :], ps_p[:, :].rearrange("p (b a) -> p b a", a=1).broadcast_to([P, B, P])).then_inc(copied, 1)
            dve.wait_ge(in_psum, 3)
            dve.tensor_scalar(y[:, :, :], ps_y[:, :, :], 0.1, None, ALU.mult).then_inc(copied, 1)
            dve.wait_ge(copied, 3)
            x = core.X[:, :, :].rearrange("p (b t) d -> p b t d", b=B)
            dve.tensor_tensor(x, x, y[:, :, :].rearrange("p b (a d) -> p b a d", a=1).broadcast_to([P, B, TB, D]),
                              ALU.add).then_inc(copied, 1)


def gates_stage(core, name, w, bias, top2, b2=None):
    nc = core.nc
    NE = 8
    with ExitStack() as ctx:
        def sb(n, shape, dt=FP32):
            return ctx.enter_context(nc.sbuf_tensor(f"{name}_{n}", shape, dt))

        xT = sb("xT", [P, S])
        logits = sb("logits", [P, TB, NE])
        top = sb("top", [P, TB, 8])
        top_u = sb("top_u", [P, TB, 8], U32)
        top_i = sb("top_i", [P, TB, 8])
        negm = sb("negm", [P, TB])
        shifted = sb("shifted", [P, TB, NE])
        e = sb("e", [P, TB, NE])
        total = sb("total", [P, TB])
        first = sb("first", [P, TB, NE])
        second = sb("second", [P, TB, NE])
        g_s = sb("g_s", [P, TB, NE])
        gT = sb("gT", [NE, S])
        ps_g = ctx.enter_context(nc.psum_tensor(f"{name}_ps_g", [P, TB, NE], FP32))
        ps_gT = ctx.enter_context(nc.psum_tensor(f"{name}_ps_gT", [NE, S], FP32))
        ps_b = ctx.enter_context(nc.psum_tensor(f"{name}_ps_b", [P, TB, D], FP32))
        biased = int(b2 is not None)
        sig = core.begin(dve_step=32, xT_ready=1, proj_in_psum=1, proj_read=1, gate_ready=1, exp_ready=int(top2),
                         attnT_in_psum=biased, attnT_ready=biased, out_ready=biased)
        dve_step, xT_ready, proj_in_psum, proj_read, gate_ready, exp_ready, gT_in_psum, gT_ready, out_ready = sig
        block = ctx.enter_context(nc.Block())

        @block.scalar
        def _(act):
            with act.Fori(0, B) as i:
                act.wait_ge(proj_in_psum.sem, proj_in_psum.at(i, 0))
                act.activation(xT[:, :], core.XNT[:, bass.ds(i * S, S)], ACT.Copy).then_inc(xT_ready.sem, 1)
                if top2:
                    act.wait_ge(gate_ready.sem, gate_ready.at(i, 1))
                    act.activation(e[:, :, :], shifted[:, :, :], ACT.Exp).then_inc(exp_ready.sem, 1)
                if b2 is not None:
                    act.wait_ge(gT_in_psum.sem, gT_in_psum.at(i, 1))
                    act.activation(gT[:, :], ps_gT[:, :], ACT.Copy).then_inc(gT_ready.sem, 1)

        @block.tensor
        def _(pe):
            with pe.Fori(0, B) as i:
                pe.wait_ge(xT_ready.sem, xT_ready.at(i, 1))
                pe.wait_ge(proj_read.sem, proj_read.at(i, 0))
                for t in range(TB):
                    mm = pe.matmul(ps_g[:, t, :], xT[:, t * P:(t + 1) * P], w[:, :], start=True, stop=True)
                mm.then_inc(proj_in_psum.sem, 1)
                if b2 is not None:
                    pe.wait_ge(gate_ready.sem, gate_ready.at(i, 1))
                    for t in range(TB):
                        tr = pe.transpose(ps_gT[:, t * P:(t + 1) * P], g_s[:, t, :], core.identf[:, :])
                    tr.then_inc(gT_in_psum.sem, 1)
                    pe.wait_ge(gT_ready.sem, gT_ready.at(i, 1))
                    for t in range(TB):
                        mm = pe.matmul(ps_b[:, t, :], gT[:, t * P:(t + 1) * P], b2[0:NE, :], start=True, stop=True)
                    mm.then_inc(out_ready.sem, 1)

        @block.vector
        def _(dve):
            with dve.Fori(0, B) as i:
                ch = Chain(dve_step, dve, i)
                dve.wait_ge(proj_in_psum.sem, proj_in_psum.at(i, 1))
                dve.tensor_tensor(logits[:, :, :], ps_g[:, :, :],
                                  bias[:, :].rearrange("p (a e) -> p a e", a=1).broadcast_to([P, TB, NE]),
                                  ALU.add).then_inc(proj_read.sem, 1)
                dve.wait_ge(proj_read.sem, proj_read.at(i, 1))
                ranked = logits
                if top2:
                    ch.link(dve.tensor_reduce(negm[:, :], logits[:, :, :], AX.X, ALU.max, negate=True))
                    dve.tensor_tensor(shifted[:, :, :], logits[:, :, :],
                                      negm[:, :].rearrange("p (t a) -> p t a", a=1).broadcast_to([P, TB, NE]),
                                      ALU.add).then_inc(gate_ready.sem, 1)
                    dve.wait_ge(exp_ready.sem, exp_ready.at(i, 1))
                    ch.link(dve.tensor_reduce(total[:, :], e[:, :, :], AX.X, ALU.add))
                    ch.link(dve.reciprocal(total[:, :], total[:, :]))
                    ch.link(dve.tensor_tensor(shifted[:, :, :], e[:, :, :],
                                              total[:, :].rearrange("p (t a) -> p t a", a=1).broadcast_to([P, TB, NE]),
                                              ALU.mult))
                    ranked = shifted
                dve.memset(negm[:, 0:1], 0.0)
                for t in range(TB):
                    m = dve.max(top[:, t, :], ranked[:, t, :])
                ch.link(m)
                dve.memset(negm[:, 0:1], 0.0)
                for t in range(TB):
                    m = dve.max_index(top_u[:, t, :], top[:, t, :], ranked[:, t, :])
                ch.link(m)
                ch.link(dve.tensor_copy(top_i[:, :, :], top_u[:, :, :]))
                if top2:
                    ch.link(dve.tensor_tensor(total[:, :], top[:, :, 0], top[:, :, 1], ALU.add))
                    ch.link(dve.tensor_scalar(total[:, :], total[:, :], 1e-6, None, ALU.add))
                    ch.link(dve.reciprocal(total[:, :], total[:, :]))
                    ch.link(dve.tensor_tensor(top[:, :, 0:2], top[:, :, 0:2],
                                              total[:, :].rearrange("p (t a) -> p t a", a=1).broadcast_to([P, TB, 2]),
                                              ALU.mult))
                    for t in range(TB):
                        dve.tensor_scalar(first[:, t, :], core.iota8[:, :], top_i[:, t, 0:1], top[:, t, 0:1], ALU.is_equal, ALU.mult)
                        m = dve.tensor_scalar(second[:, t, :], core.iota8[:, :], top_i[:, t, 1:2], top[:, t, 1:2], ALU.is_equal, ALU.mult)
                    ch.link(m)
                    ch.link(dve.tensor_tensor(core.G[:, bass.ds(i * TB, TB), :], first[:, :, :], second[:, :, :], ALU.add))
                else:
                    for t in range(TB):
                        m = dve.tensor_scalar(g_s[:, t, :], core.iota8[:, :], top_i[:, t, 0:1], None, ALU.is_equal)
                    m.then_inc(gate_ready.sem, 1)
                    dve.wait_ge(gate_ready.sem, gate_ready.at(i, 1))
                    ch.link(dve.tensor_copy(core.G[:, bass.ds(i * TB, TB), :], g_s[:, :, :]))
                    dve.wait_ge(out_ready.sem, out_ready.at(i, 1))
                    xi = core.X[:, bass.ds(i * TB, TB), :]
                    ch.link(dve.tensor_tensor(xi, xi, ps_b[:, :, :], ALU.add))
                ch.close()

    core.end(B, sig)


def experts_stage(core, name, up, down, b1=None, out_norm=False):
    nc = core.nc
    NE, NC = 8, 4
    with ExitStack() as ctx:
        def sb(n, shape, dt=FP32):
            return ctx.enter_context(nc.sbuf_tensor(f"{name}_{n}", shape, dt))

        hT = sb("hT", [P, 2, NC, S])
        acc = sb("acc", [P, TB, D])
        g = sb("g", [P, TB, NE])
        stats = sb("stats", [P, TB, 6])
        mv = sb("mv", [P, TB, 2])
        var = sb("var", [P, TB])
        rstd = sb("rstd", [P, TB])
        ps_up = [ctx.enter_context(nc.psum_tensor(f"{name}_up{n}", [P, S], FP32)) for n in range(4)]
        ps_down = [ctx.enter_context(nc.psum_tensor(f"{name}_down{n}", [P, TB, D], FP32)) for n in range(2)]
        sig = core.begin(dve_step=64, up_ready=NE * NC, act_ready=NE * NC, down_ready=NE, down_read=NE,
                         stats_ready=int(out_norm), rstd_ready=int(out_norm))
        dve_step, up_ready, act_ready, down_ready, down_read, stats_ready, rstd_ready = sig
        block = ctx.enter_context(nc.Block())

        @block.tensor
        def _(pe):
            pe.wait_ge(core.loads2, core.loads2_count)
            with pe.Fori(0, B) as i:
                def up_product(e, c):
                    n = NC * e + c
                    pe.wait_ge(act_ready.sem, act_ready.at(i, n - 3))
                    pe.matmul(ps_up[n % 4][:, :], up[:, e, c * P:(c + 1) * P], core.XNT[:, bass.ds(i * S, S)],
                              start=True, stop=True).then_inc(up_ready.sem, 1)

                def down_product(e):
                    pe.wait_ge(act_ready.sem, act_ready.at(i, NC * (e + 1)))
                    pe.wait_ge(down_read.sem, down_read.at(i, e - 1))
                    for t in range(TB):
                        for c in range(NC):
                            mm = pe.matmul(ps_down[e % 2][:, t, :], hT[:, e % 2, c, t * P:(t + 1) * P], down[:, e, c, :],
                                           start=(c == 0), stop=(c == NC - 1))
                    mm.then_inc(down_ready.sem, 1)

                for c in range(NC):
                    up_product(0, c)
                for e in range(NE):
                    if e + 1 < NE:
                        for c in range(NC):
                            up_product(e + 1, c)
                    down_product(e)

        @block.scalar
        def _(act):
            with act.Fori(0, B) as i:
                for e in range(NE):
                    act.wait_ge(down_ready.sem, down_ready.at(i, e - 1))
                    for c in range(NC):
                        n = NC * e + c
                        act.wait_ge(up_ready.sem, up_ready.at(i, n + 1))
                        if b1 is not None:
                            a = act.activation(hT[:, e % 2, c, :], ps_up[n % 4][:, :], ACT.Gelu, bias=b1[:, e, c:c + 1])
                        else:
                            a = act.activation(hT[:, e % 2, c, :], ps_up[n % 4][:, :], ACT.Gelu)
                        a.then_inc(act_ready.sem, 1)

        @block.gpsimd
        def _(pool):
            if out_norm:
                with pool.Fori(0, B) as i:
                    pool.wait_ge(stats_ready.sem, stats_ready.at(i, 1))
                    pool.tensor_tensor(rstd[:, :], var[:, :], core.minus_half[:, 0:TB], ALU.pow).then_inc(rstd_ready.sem, 1)

        @block.vector
        def _(dve):
            with dve.Fori(0, B) as i:
                ch = Chain(dve_step, dve, i)
                ch.link(dve.tensor_copy(g[:, :, :], core.G[:, bass.ds(i * TB, TB), :]))
                for e in range(NE):
                    dve.wait_ge(down_ready.sem, down_ready.at(i, e + 1))
                    for t in range(TB):
                        if e == 0:
                            a = dve.tensor_scalar(acc[:, t, :], ps_down[e % 2][:, t, :], g[:, t, e:e + 1], None, ALU.mult)
                        else:
                            a = dve.scalar_tensor_tensor(acc[:, t, :], ps_down[e % 2][:, t, :], g[:, t, e:e + 1],
                                                         acc[:, t, :], ALU.mult, ALU.add)
                    a.then_inc(down_read.sem, 1)
                    dve.wait_ge(down_read.sem, down_read.at(i, e + 1))
                if out_norm:
                    for t in range(TB):
                        a = dve.bn_stats(stats[:, t, :], acc[:, t, :])
                    ch.link(a)
                    dve.memset(var[:, :], 0.0)
                    for t in range(TB):
                        a = dve.bn_aggr(mv[:, t, :], stats[:, t, :])
                    ch.link(a)
                    dve.tensor_scalar(var[:, :], mv[:, :, 1], LN_EPS, None, ALU.add).then_inc(stats_ready.sem, 1)
                    dve.wait_ge(rstd_ready.sem, rstd_ready.at(i, 1))
                    for t in range(TB):
                        a = dve.tensor_scalar(acc[:, t, :], acc[:, t, :], mv[:, t, 0:1], rstd[:, t:t + 1], ALU.subtract, ALU.mult)
                    ch.link(a)
                    ch.link(dve.tensor_tensor(acc[:, :, :], acc[:, :, :], core.XN[:, bass.ds(i * TB, TB), :], ALU.add))
                xi = core.X[:, bass.ds(i * TB, TB), :]
                ch.link(dve.tensor_tensor(xi, xi, acc[:, :, :], ALU.add))
                ch.close()

    core.end(B, sig)


def expert_weights_stage(core, layer):
    with core.nc.Block() as block:
        @block.sync
        def _(sp):
            for name, room in ((f"{layer}_up", core.room_up), (f"{layer}_down", core.room_down)):
                core.w[name] = room
                src = core.dram[name]
                sp.dma_start(room[tuple(slice(0, x) for x in src.shape)], src).then_inc(core.loads2, 16)
                core.loads2_count += 16


def layer0_experts(core, name):
    expert_weights_stage(core, "l0f")
    norm_stage(core, name + "_norm")
    w = core.w
    gates_stage(core, name + "_gates", w["l0f_gate"], w["l0f_bias"], True)
    experts_stage(core, name, w["l0f_up"], w["l0f_down"], out_norm=True)


def layer1_experts(core, name, first):
    if first:
        expert_weights_stage(core, "l1f")
    norm_stage(core, name + "_norm")
    w = core.w
    gates_stage(core, name + "_gates", w["l1f_gate"], w["l1f_bias"], False, b2=w["l1f_b2"])
    experts_stage(core, name, w["l1f_up"], w["l1f_down"], b1=w["l1f_b1"])


BLOCK = 16
HID = 352
CHUNKS = ((0, 128), (128, 256), (256, 352))


def quantize(ch, dve, out, x, v, power, scale, inv):
    rows, blocks = scale.shape

    def wide(s):
        return s.rearrange("p (n a) -> p n a", a=1).broadcast_to([rows, blocks, BLOCK])

    ch.link(dve.tensor_reduce(scale, x, AX.X, ALU.max, apply_absolute_value=True))
    ch.link(dve.tensor_scalar(scale, scale, 1.0 / 6.0, 1e-12, ALU.mult, ALU.max))
    ch.link(dve.reciprocal(inv, scale))
    ch.link(dve.tensor_scalar(inv, inv, 1.0 - 2.0 ** -23, None, ALU.mult))
    ch.link(dve.tensor_tensor(v, x, wide(inv), ALU.mult))
    ch.link(dve.tensor_scalar(power.bitcast(U32), v.bitcast(U32), 0x7F800000, None, ALU.bitwise_and))
    ch.link(dve.tensor_scalar(power, power, 1.0, 0.75 * 2.0 ** 23, ALU.max, ALU.mult))
    ch.link(dve.tensor_tensor(v, v, power, ALU.add))
    ch.link(dve.tensor_tensor(v, v, power, ALU.subtract))
    return dve.tensor_tensor(out, v, wide(scale), ALU.mult)


def quantized_weights_stage(core, name, w_in, w_out):
    nc = core.nc
    R = 88
    w_inT, w_outT = core.w_inT, core.w_outT
    with ExitStack() as ctx:
        def sb(n, shape, dt=FP32):
            return ctx.enter_context(nc.sbuf_tensor(f"{name}_{n}", shape, dt))

        a = sb("a", [P, 64, BLOCK])
        b = sb("b", [P, 22, BLOCK])
        v = sb("v", [P, 64, BLOCK])
        power = sb("power", [P, 64, BLOCK])
        scale = sb("scale", [P, 64])
        inv = sb("inv", [P, 64])
        ps_in = [ctx.enter_context(nc.psum_tensor(f"{name}_in{n}", [P, HID], FP32)) for n in range(2)]
        ps_out = [ctx.enter_context(nc.psum_tensor(f"{name}_out{n}", [P, D], FP32)) for n in range(3)]
        sig = core.begin(dve_step=32, quant_ready=2, quantT_in_psum=1)
        dve_step, quant_ready, quantT_in_psum = sig
        block = ctx.enter_context(nc.Block())

        @block.vector
        def _(dve):
            ch = Chain(dve_step, dve, 0)
            quantize(ch, dve, a[0:R, :, :], w_in[0:R, :, :].rearrange("p t (n c) -> p (t n) c", c=BLOCK),
                     v[0:R, :, :], power[0:R, :, :], scale[0:R, :], inv[0:R, :]).then_inc(quant_ready.sem, 1)
            dve.wait_ge(quant_ready.sem, quant_ready.at(0, 1))
            quantize(ch, dve, b[:, :, :], w_out[:, :].rearrange("p (n c) -> p n c", c=BLOCK),
                     v[:, 0:22, :], power[:, 0:22, :], scale[:, 0:22], inv[:, 0:22]).then_inc(quant_ready.sem, 1)
            dve.wait_ge(quantT_in_psum.sem, quantT_in_psum.at(0, 1))
            for n in range(2):
                dve.tensor_copy(w_inT[:, n * HID:(n + 1) * HID], ps_in[n][:, :])
            for c, (lo, hi) in enumerate(CHUNKS):
                dve.tensor_copy(w_outT[0:hi - lo, c, :], ps_out[c][0:hi - lo, :])
            ch.close()

        @block.tensor
        def _(pe):
            pe.wait_ge(quant_ready.sem, quant_ready.at(0, 2))
            aw = a[:, :, :].rearrange("p (t n) c -> p t (n c)", t=8)
            for t in range(8):
                pe.transpose(ps_in[t // 4][:, (t % 4) * R:(t % 4 + 1) * R], aw[0:R, t, :], core.identf[0:R, 0:R])
            bw = b[:, :, :].rearrange("p n c -> p (n c)")
            for c, (lo, hi) in enumerate(CHUNKS):
                tr = pe.transpose(ps_out[c][0:hi - lo, :], bw[:, lo:hi], core.identf[:, :])
            tr.then_inc(quantT_in_psum.sem, 1)

    core.end(1, sig)


def quantized_ffn_stage(core, name):
    nc = core.nc
    w_inT, w_outT = core.w_inT, core.w_outT
    NX, NHB = TB * D // BLOCK, TB * HID // BLOCK
    with ExitStack() as ctx:
        def sb(n, shape, dt=FP32):
            return ctx.enter_context(nc.sbuf_tensor(f"{name}_{n}", shape, dt))

        xs = sb("xs", [P, TB, D])
        xq = sb("xq", [P, TB, D])
        xT = sb("xT", [P, S])
        v = sb("v", [P, NHB, BLOCK])
        power = sb("power", [P, NHB, BLOCK])
        scale = sb("scale", [P, NHB])
        inv = sb("inv", [P, NHB])
        sg = sb("sg", [P, TB, HID])
        h = sb("h", [P, TB, HID])
        hq = sb("hq", [P, TB, HID])
        hT = sb("hT", [P, 3, S])
        ps_x = ctx.enter_context(nc.psum_tensor(f"{name}_ps_x", [P, S], FP32))
        ps_g = [ctx.enter_context(nc.psum_tensor(f"{name}_g{n}", [P, 2, S], FP32)) for n in range(2)]
        ps_h = [ctx.enter_context(nc.psum_tensor(f"{name}_h{n}", [P, S], FP32)) for n in range(2)]
        ps_o = ctx.enter_context(nc.psum_tensor(f"{name}_o", [P, TB, D], FP32))
        sig = core.begin(dve_step=32, xq_ready=1, xqT_in_psum=1, xT_ready=1, up_ready=TB, act_ready=TB, mul_done=TB,
                         quant_ready=1, quantT_in_psum=3, quantT_ready=3, out_ready=1, out_read=1)
        (dve_step, xq_ready, xqT_in_psum, xT_ready, up_ready, act_ready, mul_done, quant_ready, quantT_in_psum,
         quantT_ready, out_ready, out_read) = sig
        block = ctx.enter_context(nc.Block())

        @block.vector
        def _(dve):
            def quantize_x(i, n, ch):
                ch.link(dve.tensor_copy(xs[:, :, :], core.XN[:, bass.ds((i + n) * TB, TB), :]))
                q = quantize(ch, dve, xq[:, :, :].rearrange("p t (n c) -> p (t n) c", c=BLOCK),
                             xs[:, :, :].rearrange("p t (n c) -> p (t n) c", c=BLOCK),
                             v[:, 0:NX, :], power[:, 0:NX, :], scale[:, 0:NX], inv[:, 0:NX])
                q.then_inc(xq_ready.sem, 1)
                dve.wait_ge(xq_ready.sem, xq_ready.at(i, n + 1))

            ch = Chain(dve_step, dve, 0)
            quantize_x(0, 0, ch)
            ch.close()

            def batch(i, ahead):
                ch = Chain(dve_step, dve, i + 1)
                for t in range(TB):
                    dve.wait_ge(act_ready.sem, act_ready.at(i, t + 1))
                    m = dve.tensor_tensor(h[:, t, :], sg[:, t, :], ps_g[t % 2][:, 1, 0:HID], ALU.mult).then_inc(mul_done.sem, 1)
                dve.wait_ge(mul_done.sem, mul_done.at(i, TB))
                quantize(ch, dve, hq[:, :, :].rearrange("p t (n c) -> p (t n) c", c=BLOCK),
                         h[:, :, :].rearrange("p t (n c) -> p (t n) c", c=BLOCK),
                         v[:, :, :], power[:, :, :], scale[:, :], inv[:, :]).then_inc(quant_ready.sem, 1)
                dve.wait_ge(quant_ready.sem, quant_ready.at(i, 1))
                if ahead:
                    quantize_x(i, 1, ch)
                dve.wait_ge(out_ready.sem, out_ready.at(i, 1))
                xi = core.X[:, bass.ds(i * TB, TB), :]
                dve.tensor_tensor(xi, xi, ps_o[:, :, :], ALU.add).then_inc(out_read.sem, 1)
                ch.close()

            with dve.Fori(0, B - 1) as i:
                batch(i, True)
            batch(B - 1, False)

        @block.tensor
        def _(pe):
            def input_products(i, n):
                pe.wait_ge(xq_ready.sem, xq_ready.at(i, n + 1))
                for t in range(TB):
                    tr = pe.transpose(ps_x[:, t * P:(t + 1) * P], xq[:, t, :], core.identf[:, :])
                tr.then_inc(xqT_in_psum.sem, 1)
                pe.wait_ge(xT_ready.sem, xT_ready.at(i, n + 1))
                for t in range(TB):
                    pe.wait_ge(mul_done.sem, mul_done.at(i, n * TB + t - 1))
                    for k in range(2):
                        mm = pe.matmul(ps_g[t % 2][:, k, 0:HID], xT[:, t * P:(t + 1) * P], w_inT[:, k * HID:(k + 1) * HID],
                                       start=True, stop=True)
                    mm.then_inc(up_ready.sem, 1)

            def batch(i, ahead):
                pe.wait_ge(quant_ready.sem, quant_ready.at(i, 1))
                for c, (lo, hi) in enumerate(CHUNKS):
                    pe.wait_ge(quantT_ready.sem, quantT_ready.at(i, c - 1))
                    for t in range(TB):
                        tr = pe.transpose(ps_h[c % 2][0:hi - lo, t * P:(t + 1) * P], hq[:, t, lo:hi], core.identf[:, :])
                    tr.then_inc(quantT_in_psum.sem, 1)
                pe.wait_ge(quantT_ready.sem, quantT_ready.at(i, 3))
                pe.wait_ge(out_read.sem, out_read.at(i, 0))
                for t in range(TB):
                    for c, (lo, hi) in enumerate(CHUNKS):
                        mm = pe.matmul(ps_o[:, t, :], hT[0:hi - lo, c, t * P:(t + 1) * P], w_outT[0:hi - lo, c, :],
                                       start=(c == 0), stop=(c == 2))
                mm.then_inc(out_ready.sem, 1)
                if ahead:
                    input_products(i, 1)

            input_products(0, 0)
            with pe.Fori(0, B - 1) as i:
                batch(i, True)
            batch(B - 1, False)

        @block.scalar
        def _(act):
            def input_activations(i, n):
                act.wait_ge(xqT_in_psum.sem, xqT_in_psum.at(i, n + 1))
                act.wait_ge(up_ready.sem, up_ready.at(i, n * TB))
                act.activation(xT[:, :], ps_x[:, :], ACT.Copy).then_inc(xT_ready.sem, 1)
                for t in range(TB):
                    act.wait_ge(up_ready.sem, up_ready.at(i, n * TB + t + 1))
                    act.wait_ge(mul_done.sem, mul_done.at(i, n * TB))
                    act.activation(sg[:, t, :], ps_g[t % 2][:, 0, 0:HID], ACT.Silu).then_inc(act_ready.sem, 1)

            def batch(i, ahead):
                for c, (lo, hi) in enumerate(CHUNKS):
                    act.wait_ge(quantT_in_psum.sem, quantT_in_psum.at(i, c + 1))
                    act.wait_ge(out_ready.sem, out_ready.at(i, 0))
                    act.activation(hT[0:hi - lo, c, :], ps_h[c % 2][0:hi - lo, :], ACT.Copy).then_inc(quantT_ready.sem, 1)
                if ahead:
                    input_activations(i, 1)

            input_activations(0, 0)
            with act.Fori(0, B - 1) as i:
                batch(i, True)
            batch(B - 1, False)

    core.end(B + 1, [dve_step])
    core.end(B, [xq_ready, xqT_in_psum, xT_ready, up_ready, act_ready, mul_done, quant_ready, quantT_in_psum, quantT_ready, out_ready, out_read])


def layer2_ffn(core, name, first):
    norm_stage(core, name + "_norm")
    if first:
        quantized_weights_stage(core, name + "_w", core.w["l2f_in"], core.w["l2f_out"])
    quantized_ffn_stage(core, name)


def layer3_ffn(core, name, first):
    norm_stage(core, name + "_norm")
    if first:
        quantized_weights_stage(core, name + "_w", core.w["l3f_in"], core.w["l3f_out"])
    quantized_ffn_stage(core, name)


def attention_program(nc, dram, out, stages):
    with ExitStack() as ctx:
        core = Core(nc, ctx)
        for name in SIGNALS:
            core.signals[name] = Signal(ctx.enter_context(nc.semaphore(name)))
        load_stage(core, dram)
        for stage in stages:
            stage(core)
        store_stage(core, out)




def layer0_attention_a(core):
    norm_stage(core, "l0a_norm")
    w = core.w
    linear_attention_stage(core, "l0a", w["l0a_w"], w["l0a_norm_w"], w["l0a_masks"][:, 0:4], w["l0a_masks"][:, 4:4 + D])


def layer0_attention_b(core):
    norm_stage(core, "l0b_norm")
    heads_attention_stage(core, "l0b", core.w["l0b_w"], rope=False, grouped=True)
    batch_norm_stage(core, "l0b_out")


def layer1_attention_a(core):
    norm_stage(core, "l1a_norm")
    w = core.w
    batch_attention_stage(core, "l1a", w["l1a_w"], w["l1a_bias"], w["l1a_wo"], w["l1a_bo"])


def layer1_attention_b(core):
    norm_stage(core, "l1b_norm")
    single_head_attention_stage(core, "l1b", core.w["l1b_w"])


def layer2_attention_a(core):
    norm_stage(core, "l2a_norm")
    w = core.w
    heads_attention_stage(core, "l2a", w["l2a_w"], w["l2a_wo"], bo=w["l2a_bo"], bias=w["l2a_bias"], eps=1e-8)


def layer2_attention_b(core):
    norm_stage(core, "l2b_norm")
    w = core.w
    heads_attention_stage(core, "l2b", w["l2b_w"], w["l2b_wo"], bo=w["l2b_bo"], rope=False, out_norm=w["l2b_gb"])


def layer3_attention_a(core):
    norm_stage(core, "l3a_norm")
    w = core.w
    heads_attention_stage(core, "l3a", w["l3a_w"], w["l3a_wo"], bo=w["l3a_bo"], bias=w["l3a_bias"])


def layer3_attention_b(core):
    norm_stage(core, "l3b_norm")
    with core.nc.sbuf_tensor("l3b_meanT", [P, B], FP32) as meanT:
        mixer_stage(core, "l3b_mixer", core.w, meanT)
        bus_stage(core, "l3b_bus", core.w, meanT)


def whole(stage, *args):
    return lambda core: stage(core, *args)


STAGES = [
    layer0_attention_a,
    whole(layer0_experts, "l0fa"),
    layer0_attention_b,
    whole(layer0_experts, "l0fb"),
    layer1_attention_a,
    whole(layer1_experts, "l1fa", True),
    layer1_attention_b,
    whole(layer1_experts, "l1fb", False),
    layer2_attention_a,
    whole(layer2_ffn, "l2fa", True),
    layer2_attention_b,
    whole(layer2_ffn, "l2fb", False),
    layer3_attention_a,
    whole(layer3_ffn, "l3fa", True),
    layer3_attention_b,
    whole(layer3_ffn, "l3fb", False),
]


def rope_table():
    pos = np.arange(S, dtype=np.float32)
    inv = (1.0 / np.float32(10000.0) ** (np.arange(0, HD, 2, dtype=np.float32) / np.float32(HD))).astype(np.float32)
    ang = (pos[:, None] * inv[None, :]).astype(np.float32)
    cos, sin = np.cos(ang), np.sin(ang)
    table = np.stack([np.repeat(cos, 2, axis=1), np.stack([-sin, sin], -1).reshape(S, HD)], 1)
    return table.astype(np.float32)


def lay_out(a):
    c = np.ascontiguousarray
    w = {}

    def put(name, x):
        w[name] = c(x)

    def row(x):
        return np.broadcast_to(c(x).reshape(1, -1), (P, x.size))

    put("X", a["L0_attn_a_X"])
    table = rope_table().reshape(TB, P, 2, HD).transpose(1, 0, 2, 3)
    put("rope", table)
    put("rope_batch", np.broadcast_to(rope_table()[None, :B], (P, B, 2, HD)))
    put("l0a_w", np.concatenate([a["L0_attn_a_Wq"].T, a["L0_attn_a_Wv"].T], 1))
    put("l0a_norm_w", row(np.stack([a["L0_attn_a_q_norm_w"], a["L0_attn_a_v_norm_w"]])))
    ch = np.arange(D)
    put("l0a_masks", np.concatenate([(ch[:, None] // HD) % 4 == np.arange(4)[None, :],
                                     ch[:, None] // HD == ch[None, :] // HD], 1).astype(np.float32))
    put("l0b_w", np.concatenate([a[f"L0_attn_b_W{n}"].T for n in "qkv"], 1))
    put("l0f_gate", a["L0_ffn_gate_w"].T)
    put("l0f_bias", row(a["L0_ffn_expert_bias"]))
    put("l0f_up", a["L0_ffn_w_up"].transpose(2, 0, 1))
    put("l0f_down", a["L0_ffn_w_down"].reshape(8, D, 4, P).transpose(3, 0, 2, 1))
    put("l1a_w", a["L1_attn_a_Wqkv"])
    put("l1a_bias", row(a["L1_attn_a_bqkv"]))
    put("l1a_wo", a["L1_attn_a_Wout"])
    put("l1a_bo", row(a["L1_attn_a_bout"]))
    put("l1b_w", np.concatenate([a[f"L1_attn_b_W{n}"] for n in "qkv"], 1))
    put("l1f_gate", a["L1_ffn_Wg"])
    put("l1f_bias", row(a["L1_ffn_bg"]))
    put("l1f_up", a["L1_ffn_W1"].transpose(1, 0, 2))
    put("l1f_b1", a["L1_ffn_b1"].reshape(8, 4, P).transpose(2, 0, 1))
    put("l1f_down", a["L1_ffn_W2"].reshape(8, 4, P, D).transpose(2, 0, 1, 3))
    put("l1f_b2", a["L1_ffn_b2"])
    put("l2a_w", np.concatenate([a[f"L2_attn_a_W{n}"].T for n in "qkv"], 1))
    put("l2a_bias", row(np.concatenate([a[f"L2_attn_a_b{n}"] for n in "qkv"])))
    put("l2a_wo", a["L2_attn_a_Wo"].T)
    put("l2a_bo", row(a["L2_attn_a_bo"]))
    put("l2b_w", a["L2_attn_b_w_qkv"])
    put("l2b_wo", a["L2_attn_b_w_proj"])
    put("l2b_bo", row(a["L2_attn_b_b_proj"]))
    put("l2b_gb", row(np.stack([a["L2_attn_b_ln_gamma"], a["L2_attn_b_ln_beta"]])))
    for n in "23":
        put(f"l{n}f_in", np.concatenate([a[f"L{n}_ffn_w_gate"], a[f"L{n}_ffn_w_up"]], 0)
            .reshape(8, 88, D).transpose(1, 0, 2))
        put(f"l{n}f_out", a[f"L{n}_ffn_w_down"])
    put("l3a_w", a["L3_attn_a_qkv_w"].T)
    put("l3a_bias", row(a["L3_attn_a_qkv_b"]))
    put("l3a_wo", a["L3_attn_a_proj_w"].T)
    put("l3a_bo", row(a["L3_attn_a_proj_b"]))
    put("l3b_norm_w", row(np.stack([a["L3_attn_b_w_norm_in"], a["L3_attn_b_w_norm_out"]])))
    put("l3b_r1", a["L3_attn_b_router_w1"])
    put("l3b_r2", a["L3_attn_b_router_w2"])
    put("l3b_rb", row(a["L3_attn_b_router_b2"]))
    put("l3b_lam", np.repeat(a["L3_attn_b_lambdas"], D // 8).reshape(D, 1))
    put("l3b_qk", np.concatenate([a[f"L3_attn_b_slr_w{n}"] for n in ("q1", "q2", "k1", "k2", "v")], 1))
    put("l3b_wo", a["L3_attn_b_slr_wo"])
    put("l3b_slam", row(a["L3_attn_b_slr_lam"].reshape(1)))
    put("l3b_landT", a["L3_attn_b_landmarks"].T)
    put("l3b_mix", a["L3_attn_b_mix_w"].reshape(2, D, D).transpose(1, 0, 2))
    put("l3b_bus", np.concatenate([a[f"L3_attn_b_bus_{n}"] for n in ("compress", "publish", "expand")], 1))
    return w


def kernel(**inputs):
    import concourse.bacc as bacc
    from concourse.bass_utils import run_bass_kernel_spmd

    nc = bacc.Bacc("TRN2", target_bir_lowering=False, num_devices=1)
    arrays, dram = {}, {}
    for name, x in lay_out({k: np.asarray(v) for k, v in inputs.items()}).items():
        arrays[f"in_{name}"] = x
        dram[name] = nc.dram_tensor(f"in_{name}", x.shape, FP32, kind="ExternalInput").ap()
    out = nc.dram_tensor("out_0", (B, S, D), FP32, kind="ExternalOutput").ap()
    attention_program(nc, dram, out, STAGES)
    got = run_bass_kernel_spmd(nc, [arrays], core_ids=[0])
    return got.results[0]["out_0"]
```
